# Optimizing a Trainium2 kernel written in Bass

```python
import numpy as np
import jax
import jax.numpy as jnp

def _softmax(x, axis=-1):
    return jax.nn.softmax(x, axis=axis)

def _gelu(x):
    return jax.nn.gelu(x, approximate=True)

def _silu(x):
    return jax.nn.silu(x)

def _sigmoid(x):
    return jax.nn.sigmoid(x)

def _layernorm(x, axis=-1, eps=1e-05):
    m = jnp.mean(x, axis=axis, keepdims=True)
    v = jnp.var(x, axis=axis, keepdims=True)
    return (x - m) / jnp.sqrt(v + eps)

def _scatter_add(tgt, idx, src, axis=0):
    return tgt.at[idx].add(src)

def _segment_sum(src, seg, n):
    return jax.ops.segment_sum(src, seg, n)
kernel_name = 'mk_flamingo_gated_d2_seqx_r4_c03db0'

def setup_inputs(seed: int=0):
    np.random.seed(seed)
    _w = jnp.asarray

    def _rec_inputs():
        import jax
        import jax.numpy as jnp
        _rk = jax.random.key(seed)
        x = 4.136e-05 + 0.9999 * jax.random.normal(jax.random.fold_in(_rk, 1), (4, 512, 512), jnp.float32)
        _lenS = 512 - jax.random.randint(jax.random.fold_in(_rk, 7), (4,), 0, max(1, 512 // 4) + 1, jnp.int32)
        _lenS2 = 512 - jax.random.randint(jax.random.fold_in(_rk, 8), (4,), 0, max(1, 512 // 4) + 1, jnp.int32)
        _ctx_1024P = jax.random.normal(jax.random.fold_in(_rk, 11), (4, 16, 256), jnp.float32)
        _ctx_1024c = jax.random.dirichlet(jax.random.fold_in(_rk, 511), 0.3 * jnp.ones((16,), jnp.float32), (4, 512))
        _ctx_1024t = jnp.einsum('bsk,bkd->bsd', _ctx_1024c, _ctx_1024P)
        _ctx_1024t = _ctx_1024t * jax.lax.rsqrt(jnp.mean(jnp.square(_ctx_1024t)) + 1e-12) * 0.953939
        ctx_1024 = -0.000292821 + 1.00034 * (_ctx_1024t + 0.3 * jax.random.normal(jax.random.fold_in(_rk, 611), (4, 512, 256), jnp.float32))
        _g = jax.random.normal(jax.random.fold_in(_rk, 9001), (2, 2), jnp.float32)
        _g = jnp.sign(_g) * jnp.maximum(jnp.abs(_g), 1.0) + (_g == 0) * 1.0
        g_xattn = _g[0]
        g_ffn = _g[1]
        return (x, ctx_1024, g_xattn, g_ffn)
    x, ctx_1024, g_xattn, g_ffn = _rec_inputs()

    def _L0_xattn_setup():
        import jax, jax.numpy as jnp
        import numpy as np
        import math
        B, L, DM = (2, 512, 256)
        DS, DC, EXP = (16, 4, 2)
        DI = EXP * DM
        DR = math.ceil(DM / 16)
        DT_MIN, DT_MAX, DT_FLOOR = (0.001, 0.1, 0.0001)

        def _ssm_forward(hidden_states, z, in_proj_w, conv_w, conv_b, x_proj_w, dt_proj_w, dt_proj_b, A_log, D):
            b = hidden_states.shape[0]
            x = jnp.einsum('ed,bld->bel', in_proj_w, hidden_states)
            xp = jnp.pad(x, ((0, 0), (0, 0), (DC - 1, 0)))
            xc = jax.lax.conv_general_dilated(xp, conv_w[:, None, :], window_strides=(1,), padding='VALID', dimension_numbers=('NCH', 'OIH', 'NCH'), feature_group_count=DI)
            u = jax.nn.silu(xc + conv_b[None, :, None])
            x_dbl = jnp.einsum('ke,bel->bkl', x_proj_w, u)
            dt_lo = x_dbl[:, :DR]
            Bm = x_dbl[:, DR:DR + DS]
            Cm = x_dbl[:, DR + DS:]
            delta = jax.nn.softplus(jnp.einsum('er,brl->bel', dt_proj_w, dt_lo) + dt_proj_b[None, :, None])
            A = -jnp.exp(A_log)

            def step(state, xs):
                d_t, B_t, C_t, u_t = xs
                dA = jnp.exp(d_t[..., None] * A)
                state = state * dA + (d_t * u_t)[..., None] * B_t[:, None, :]
                y_t = jnp.einsum('ben,bn->be', state, C_t)
                return (state, y_t)
            xs = (jnp.moveaxis(delta, -1, 0), jnp.moveaxis(Bm, -1, 0), jnp.moveaxis(Cm, -1, 0), jnp.moveaxis(u, -1, 0))
            state0 = jnp.zeros((b, DI, DS), delta.dtype)
            _, ys = jax.lax.scan(step, state0, xs)
            y = jnp.moveaxis(ys, 0, -1)
            y = y + D[None, :, None] * u
            y = y * jax.nn.silu(z)
            return jnp.swapaxes(y, 1, 2)
        key = jax.random.key(seed)
        ks = jax.random.split(key, 8)
        hidden_states = jax.random.normal(ks[0], (B, L, DM), jnp.float32)
        z = jax.random.normal(ks[1], (B, DI, L), jnp.float32)
        in_proj_w = jax.random.normal(ks[2], (DI, DM), jnp.float32) * DM ** (-0.5)
        conv_w = jax.random.normal(ks[3], (DI, DC), jnp.float32) * DC ** (-0.5)
        conv_b = jnp.zeros((DI,), jnp.float32)
        x_proj_w = jax.random.normal(ks[4], (DR + 2 * DS, DI), jnp.float32) * DI ** (-0.5)
        dt_std = DR ** (-0.5)
        dt_proj_w = jax.random.uniform(ks[5], (DI, DR), jnp.float32, -dt_std, dt_std)
        dt = jnp.exp(jax.random.uniform(ks[6], (DI,), jnp.float32) * (math.log(DT_MAX) - math.log(DT_MIN)) + math.log(DT_MIN))
        dt = jnp.clip(dt, DT_FLOOR)
        dt_proj_b = dt + jnp.log(-jnp.expm1(-dt))
        A_log = jnp.log(jnp.broadcast_to(jnp.arange(1, DS + 1, dtype=jnp.float32), (DI, DS)))
        D = jnp.ones((DI,), jnp.float32)
        return dict(hidden_states=hidden_states, z=z, in_proj_w=in_proj_w, conv_w=conv_w, conv_b=conv_b, x_proj_w=x_proj_w, dt_proj_w=dt_proj_w, dt_proj_b=dt_proj_b, A_log=A_log, D=D)
    _L0_xattn_all = _L0_xattn_setup()
    _L0_xattn_in = {k: v for k, v in _L0_xattn_all.items() if k in ('in_proj_w', 'conv_w', 'conv_b', 'x_proj_w', 'dt_proj_w', 'dt_proj_b', 'A_log', 'D')}
    del _L0_xattn_all

    def _L0_ffn_setup():
        import jax, jax.numpy as jnp
        import numpy as np
        K = 2

        def gelu(v):
            return jax.nn.gelu(v, approximate=False)
        key = jax.random.key(seed)
        ks = jax.random.split(key, 10)
        B, S, D, H, E = (4, 512, 512, 256, 8)
        SH = 2 * H
        u = lambda k_, shape, b: jax.random.uniform(k_, shape, jnp.float32, -b, b)
        return {'x': jax.random.normal(ks[0], (B, S, D), jnp.float32), 'gate_w': u(ks[1], (D, E), 1.0 / D), 'w1': u(ks[2], (E, D, H), 1.0 / D), 'b1': u(ks[3], (E, H), 1.0 / np.sqrt(D)), 'w2': u(ks[4], (E, H, D), 1.0 / H), 'b2': u(ks[5], (E, D), 1.0 / np.sqrt(H)), 'shared_w1': u(ks[6], (D, SH), 1.0 / D), 'shared_b1': u(ks[7], (SH,), 1.0 / np.sqrt(D)), 'shared_w2': u(ks[8], (SH, D), 1.0 / SH), 'shared_b2': u(ks[9], (D,), 1.0 / np.sqrt(SH))}
    _L0_ffn_all = _L0_ffn_setup()
    _L0_ffn_in = {k: v for k, v in _L0_ffn_all.items() if k in ('gate_w', 'w1', 'b1', 'w2', 'b2', 'shared_w1', 'shared_b1', 'shared_w2', 'shared_b2')}
    del _L0_ffn_all

    def _L1_xattn_setup():
        import jax, jax.numpy as jnp
        import numpy as np
        key = jax.random.key(seed)
        ks = jax.random.split(key, 6)
        B, L, N, C, D = (8, 128, 512, 256, 128)
        return {'teacher_logits': jax.random.normal(ks[0], (B, L, N), dtype=jnp.float32), 'teacher_features': jax.random.normal(ks[1], (B, N, C), dtype=jnp.float32), 'Wq': jax.random.normal(ks[2], (D, C), dtype=jnp.float32) * (1.0 / np.sqrt(C)), 'bq': jnp.zeros((D,), dtype=jnp.float32), 'Wk': jax.random.normal(ks[3], (D, C), dtype=jnp.float32) * (1.0 / np.sqrt(C)), 'bk': jnp.zeros((D,), dtype=jnp.float32)}
    _L1_xattn_all = _L1_xattn_setup()
    _L1_xattn_in = {k: v for k, v in _L1_xattn_all.items() if k in ('Wq', 'bq', 'Wk', 'bk')}
    del _L1_xattn_all

    def _L1_ffn_setup():
        import jax, jax.numpy as jnp
        import numpy as np
        B, S, D, H = (4, 512, 512, 2048)

        def fwht(x):
            orig_shape = x.shape
            n = orig_shape[-1]
            x = x.reshape(-1, n)
            h = 1
            while h < n:
                xb = x.reshape(-1, n // (2 * h), 2, h)
                a = xb[:, :, 0, :]
                b = xb[:, :, 1, :]
                x = jnp.stack([a + b, a - b], axis=2).reshape(-1, n)
                h *= 2
            scale = jnp.asarray(1.0 / np.sqrt(n), dtype=x.dtype)
            return (x * scale).reshape(orig_shape)
        key = jax.random.key(seed)
        kx, k1, k2, k3 = jax.random.split(key, 4)
        x = jax.random.normal(kx, (B, S, D), dtype=jnp.float32)
        W1 = jax.random.normal(k1, (H, D), dtype=jnp.float32) * (1.0 / np.sqrt(D))
        W2 = jax.random.normal(k2, (D, H), dtype=jnp.float32) * (1.0 / np.sqrt(H))
        W3 = jax.random.normal(k3, (H, D), dtype=jnp.float32) * (1.0 / np.sqrt(D))
        return {'x': x, 'W1': W1, 'W2': W2, 'W3': W3}
    _L1_ffn_all = _L1_ffn_setup()
    _L1_ffn_in = {k: v for k, v in _L1_ffn_all.items() if k in ('W1', 'W2', 'W3')}
    del _L1_ffn_all
    return {'x': x, 'ctx_1024': ctx_1024, 'g_xattn': g_xattn, 'g_ffn': g_ffn, 'L0_xattn_in_proj_w': _L0_xattn_in['in_proj_w'], 'L0_xattn_conv_w': _L0_xattn_in['conv_w'], 'L0_xattn_conv_b': _L0_xattn_in['conv_b'], 'L0_xattn_x_proj_w': _L0_xattn_in['x_proj_w'], 'L0_xattn_dt_proj_w': _L0_xattn_in['dt_proj_w'], 'L0_xattn_dt_proj_b': _L0_xattn_in['dt_proj_b'], 'L0_xattn_A_log': _L0_xattn_in['A_log'], 'L0_xattn_D': _L0_xattn_in['D'], 'L0_ffn_gate_w': _L0_ffn_in['gate_w'], 'L0_ffn_w1': _L0_ffn_in['w1'], 'L0_ffn_b1': _L0_ffn_in['b1'], 'L0_ffn_w2': _L0_ffn_in['w2'], 'L0_ffn_b2': _L0_ffn_in['b2'], 'L0_ffn_shared_w1': _L0_ffn_in['shared_w1'], 'L0_ffn_shared_b1': _L0_ffn_in['shared_b1'], 'L0_ffn_shared_w2': _L0_ffn_in['shared_w2'], 'L0_ffn_shared_b2': _L0_ffn_in['shared_b2'], 'L1_xattn_Wq': _L1_xattn_in['Wq'], 'L1_xattn_bq': _L1_xattn_in['bq'], 'L1_xattn_Wk': _L1_xattn_in['Wk'], 'L1_xattn_bk': _L1_xattn_in['bk'], 'L1_ffn_W1': _L1_ffn_in['W1'], 'L1_ffn_W2': _L1_ffn_in['W2'], 'L1_ffn_W3': _L1_ffn_in['W3']}

def reference(x, ctx_1024, g_xattn, g_ffn, L0_xattn_in_proj_w, L0_xattn_conv_w, L0_xattn_conv_b, L0_xattn_x_proj_w, L0_xattn_dt_proj_w, L0_xattn_dt_proj_b, L0_xattn_A_log, L0_xattn_D, L0_ffn_gate_w, L0_ffn_w1, L0_ffn_b1, L0_ffn_w2, L0_ffn_b2, L0_ffn_shared_w1, L0_ffn_shared_b1, L0_ffn_shared_w2, L0_ffn_shared_b2, L1_xattn_Wq, L1_xattn_bq, L1_xattn_Wk, L1_xattn_bk, L1_ffn_W1, L1_ffn_W2, L1_ffn_W3):
    import jax
    import jax.numpy as jnp

    def _L0_xattn_ref(hidden_states, z, in_proj_w, conv_w, conv_b, x_proj_w, dt_proj_w, dt_proj_b, A_log, D):
        import jax, jax.numpy as jnp
        import numpy as np
        import math
        B, L, DM = (2, 512, 256)
        DS, DC, EXP = (16, 4, 2)
        DI = EXP * DM
        DR = math.ceil(DM / 16)
        DT_MIN, DT_MAX, DT_FLOOR = (0.001, 0.1, 0.0001)

        def _ssm_forward(hidden_states, z, in_proj_w, conv_w, conv_b, x_proj_w, dt_proj_w, dt_proj_b, A_log, D):
            b = hidden_states.shape[0]
            x = jnp.einsum('ed,bld->bel', in_proj_w, hidden_states)
            xp = jnp.pad(x, ((0, 0), (0, 0), (DC - 1, 0)))
            xc = jax.lax.conv_general_dilated(xp, conv_w[:, None, :], window_strides=(1,), padding='VALID', dimension_numbers=('NCH', 'OIH', 'NCH'), feature_group_count=DI)
            u = jax.nn.silu(xc + conv_b[None, :, None])
            x_dbl = jnp.einsum('ke,bel->bkl', x_proj_w, u)
            dt_lo = x_dbl[:, :DR]
            Bm = x_dbl[:, DR:DR + DS]
            Cm = x_dbl[:, DR + DS:]
            delta = jax.nn.softplus(jnp.einsum('er,brl->bel', dt_proj_w, dt_lo) + dt_proj_b[None, :, None])
            A = -jnp.exp(A_log)

            def step(state, xs):
                d_t, B_t, C_t, u_t = xs
                dA = jnp.exp(d_t[..., None] * A)
                state = state * dA + (d_t * u_t)[..., None] * B_t[:, None, :]
                y_t = jnp.einsum('ben,bn->be', state, C_t)
                return (state, y_t)
            xs = (jnp.moveaxis(delta, -1, 0), jnp.moveaxis(Bm, -1, 0), jnp.moveaxis(Cm, -1, 0), jnp.moveaxis(u, -1, 0))
            state0 = jnp.zeros((b, DI, DS), delta.dtype)
            _, ys = jax.lax.scan(step, state0, xs)
            y = jnp.moveaxis(ys, 0, -1)
            y = y + D[None, :, None] * u
            y = y * jax.nn.silu(z)
            return jnp.swapaxes(y, 1, 2)
        return _ssm_forward(hidden_states, z, in_proj_w, conv_w, conv_b, x_proj_w, dt_proj_w, dt_proj_b, A_log, D)

    def _L0_ffn_ref(x, gate_w, w1, b1, w2, b2, shared_w1, shared_b1, shared_w2, shared_b2):
        import jax, jax.numpy as jnp
        import numpy as np
        K = 2

        def gelu(v):
            return jax.nn.gelu(v, approximate=False)
        B, S, D = x.shape
        E = gate_w.shape[1]
        xf = x.reshape(-1, D)
        logits = xf @ gate_w
        top_logits, top_idx = jax.lax.top_k(logits, K)
        top_gates = jax.nn.softmax(top_logits, axis=-1)
        gates = jnp.sum(jax.nn.one_hot(top_idx, E, dtype=xf.dtype) * top_gates[..., None], axis=1)
        h = gelu(jnp.einsum('nd,edh->neh', xf, w1) + b1)
        out_e = jnp.einsum('neh,ehd->ned', h, w2) + b2
        routed = jnp.einsum('ne,ned->nd', gates, out_e)
        shared = gelu(xf @ shared_w1 + shared_b1) @ shared_w2 + shared_b2
        return (routed + shared).reshape(B, S, D)

    def _L1_xattn_ref(teacher_logits, teacher_features, Wq, bq, Wk, bk):
        import jax, jax.numpy as jnp
        import numpy as np
        query = jnp.einsum('bnc,dc->bnd', teacher_features, Wq) + bq
        key = jnp.einsum('bnc,dc->bnd', teacher_features, Wk) + bk
        energy = jnp.einsum('bnd,bmd->bnm', query, key)
        attention = jax.nn.softmax(energy, axis=-1)
        x_m = jnp.einsum('bln,bmn->blm', teacher_logits, attention)
        return x_m

    def _L1_ffn_ref(x, W1, W2, W3):
        import jax, jax.numpy as jnp
        import numpy as np
        B, S, D, H = (4, 512, 512, 2048)

        def fwht(x):
            orig_shape = x.shape
            n = orig_shape[-1]
            x = x.reshape(-1, n)
            h = 1
            while h < n:
                xb = x.reshape(-1, n // (2 * h), 2, h)
                a = xb[:, :, 0, :]
                b = xb[:, :, 1, :]
                x = jnp.stack([a + b, a - b], axis=2).reshape(-1, n)
                h *= 2
            scale = jnp.asarray(1.0 / np.sqrt(n), dtype=x.dtype)
            return (x * scale).reshape(orig_shape)
        up_gate = jnp.einsum('bsd,hd->bsh', x, W1)
        up_lin = jnp.einsum('bsd,hd->bsh', x, W3)
        hidden = jax.nn.silu(up_gate) * up_lin
        hidden = fwht(hidden)
        out = jnp.einsum('bsh,dh->bsd', hidden, W2)
        return out
    x = x + jnp.tanh(g_xattn[0]) * _L0_xattn_ref(ctx_1024, _layernorm(x, axis=-1), L0_xattn_in_proj_w, L0_xattn_conv_w, L0_xattn_conv_b, L0_xattn_x_proj_w, L0_xattn_dt_proj_w, L0_xattn_dt_proj_b, L0_xattn_A_log, L0_xattn_D)
    x = x + jnp.tanh(g_ffn[0]) * _L0_ffn_ref(_layernorm(x, axis=-1), L0_ffn_gate_w, L0_ffn_w1, L0_ffn_b1, L0_ffn_w2, L0_ffn_b2, L0_ffn_shared_w1, L0_ffn_shared_b1, L0_ffn_shared_w2, L0_ffn_shared_b2)
    x = x + jnp.tanh(g_xattn[1]) * _L1_xattn_ref(_layernorm(x, axis=-1), ctx_1024, L1_xattn_Wq, L1_xattn_bq, L1_xattn_Wk, L1_xattn_bk)
    x = x + jnp.tanh(g_ffn[1]) * _L1_ffn_ref(_layernorm(x, axis=-1), L1_ffn_W1, L1_ffn_W2, L1_ffn_W3)
    return x

_drawn_inputs = setup_inputs


def setup_inputs(seed=0):
    import zlib

    import numpy as np

    out = dict(_drawn_inputs(seed))
    spreads = {'g_ffn': (-1.0, 0.2),
     'L0_xattn_conv_b': (0.0, 0.1),
     'L0_xattn_D': (1.0, 0.2),
     'L1_xattn_bq': (0.0, 0.1),
     'L1_xattn_bk': (0.0, 2.0)}
    factors = {'L0_xattn_dt_proj_w': 6.528,
     'L0_xattn_dt_proj_b': 3.03,
     'L0_ffn_gate_w': 3.329,
     'L0_ffn_w1': 26.434,
     'L0_ffn_b1': 27.614,
     'L0_ffn_w2': 8.0,
     'L0_ffn_b2': 2.815,
     'L0_ffn_shared_w1': 26.695,
     'L0_ffn_shared_b1': 28.826,
     'L0_ffn_shared_w2': 8.0,
     'L0_ffn_shared_b2': 2.92,
     'L0_xattn_A_log': 3.069}
    for name, (base, spread) in spreads.items():
        noise = np.random.default_rng([zlib.crc32(name.encode()), seed]).standard_normal(out[name].shape)
        drawn = base * np.exp(spread * noise) if base else spread * noise
        out[name] = jnp.asarray(drawn.astype(out[name].dtype))
    for name, factor in factors.items():
        out[name] = (out[name] * factor).astype(out[name].dtype)
    return out
```

```python
from contextlib import ExitStack

import concourse.bass as bass
from concourse import mybir

F32 = mybir.dt.float32
F16 = mybir.dt.float16
U32 = mybir.dt.uint32
ALU = mybir.AluOpType
ACT = mybir.ActivationFunctionType
AX_X = mybir.AxisListType.X

P = 128
B, L, D = 4, 512, 512
C = 256
DI, NS, DR, TAPS = 512, 16, 16, 4
NE, HE, SH = 8, 256, 512
H = 2048
ET, LT, DT, CT = DI // P, L // P, D // P, C // P
HT = (NE * HE + SH) // P
GR = HT // 2
FT = H // P
WS = 64.0
EPS = 1e-5
SLOTS = 8


def scan_block(nc, w, x, ctx_t, x1, b_rows):
    SCANS, ADDS = NS * ET, (NS + 1) * LT
    GAPS = (2, 10, 12, 14, NS)
    CONV = 8
    with ExitStack() as stack:
        def sb(name, shape, dt=F32):
            return stack.enter_context(nc.sbuf_tensor("s_" + name, shape, dt))

        def sem(name):
            return stack.enter_context(nc.semaphore("scan_" + name))

        ident = sb("ident", [P, P])
        gates = sb("gates", [P, 4])
        tanh_g = sb("tanh_g", [P, 4])
        w_tap = sb("w_tap", [P, TAPS, CT, DI])
        w_x = sb("w_x", [P, ET, 64])
        w_dt = sb("w_dt", [DR, DI])
        cols = sb("cols", [P, 3, ET])
        a_log = sb("a_log", [P, ET, NS])
        a_exp = sb("a_exp", [P, ET, NS])
        a_neg = sb("a_neg", [P, ET, NS])
        half = sb("half", [P, LT])
        ctx_pad = sb("ctx_pad", [P, CT, TAPS - 1 + L])
        xs = sb("xs", [P, 2, LT, D])
        xn = sb("xn", [P, LT, D])
        stat = sb("stat", [P, LT, 6])
        mv = sb("mv", [P, LT, 2])
        var_eps = sb("var_eps", [P, LT])
        rstd = sb("rstd", [P, LT])
        sz = sb("sz", [P, LT, DI])
        u = sb("u", [P, ET, L])
        proj = sb("proj", [64, L])
        b_all = sb("b_all", [P, NS, L])
        c_col = sb("c_col", [P, 2, LT, 64])
        sp_y = sb("sp_y", [P, ET, L])
        sp_l = sb("sp_l", [P, ET, L])
        sp_r = sb("sp_r", [P, ET, L])
        delta = sb("delta", [P, ET, L])
        du = sb("du", [P, ET, L])
        decay = sb("decay", [P, 2, ET, L])
        drive = sb("drive", [P, 2, ET, L])
        state = sb("state", [P, 2, ET, L])
        acc = sb("acc", [P, LT, DI])
        work = [stack.enter_context(nc.psum_tensor(f"scan_work{i}", [P, 512], F32)) for i in range(4)]
        turned = [stack.enter_context(nc.psum_tensor(f"scan_turned{i}", [P, 512], F32)) for i in range(4)]
        w_in = sp_y[:, 0:CT, :]
        tap_rows = sp_l

        consts = sem("consts")
        pad_zero = sem("pad_zero")
        half_set = sem("half_set")
        taps_done = sem("taps_done")
        a_done = sem("a_done")
        tanh_done = sem("tanh_done")
        ctx_in = sem("ctx_in")
        x_in = [sem("x_in_even"), sem("x_in_odd")]
        stat_done = sem("stat_done")
        mv_done = sem("mv_done")
        var_done = sem("var_done")
        rstd_done = sem("rstd_done")
        xn_done = sem("xn_done")
        conv_done = sem("conv_done")
        u_done = sem("u_done")
        xproj_done = sem("xproj_done")
        proj_done = sem("proj_done")
        rows_out = sem("rows_out")
        rows_in = [sem(f"rows_in{q}") for q in range(len(GAPS))]
        cT_done = sem("cT_done")
        c_done = sem("c_done")
        dt_done = sem("dt_done")
        relu_done = sem("relu_done")
        exp_done = sem("exp_done")
        ln_done = sem("ln_done")
        soft = sem("soft")
        sum_done = sem("sum_done")
        delta_done = sem("delta_done")
        du_done = sem("du_done")
        skip_done = sem("skip_done")
        zT_done = sem("zT_done")
        sz_done = sem("sz_done")
        decay_done = sem("decay_done")
        drive_done = sem("drive_done")
        scan_done = sem("scan_done")
        half_free = sem("half_free")
        turned_done = sem("turned_done")
        add_done = sem("add_done")
        mul_done = sem("mul_done")
        x1_done = sem("x1_done")
        x1_out = [sem("x1_out_even"), sem("x1_out_odd")]
        CONSTS = 9
        block = stack.enter_context(nc.Block())

        def segments(eng, b, step, gap):
            lo = 0
            for q, hi in enumerate(GAPS):
                if q == 0:
                    for n in range(lo, hi):
                        step(n, n % 2)
                else:
                    with eng.Fori(lo // 2, hi // 2) as pair:
                        for k in (0, 1):
                            step(pair * 2 + k, k)
                lo = hi
                gap(q)

        @block.sync
        def _(sp):
            sp.dma_start(w_in, w["w_in"]).then_inc(consts, 16)
            sp.dma_start(tap_rows[:], w["conv_w"].partition_broadcast(P)).then_inc(consts, 16)
            for dst, src in ((ident[:], "ident"), (w_x[:], "w_x"), (w_dt[:], "w_dt"), (cols[:], "scan_cols"),
                             (a_log[:], "a_log")):
                sp.dma_start(dst, w[src]).then_inc(consts, 16)
            sp.dma_start(gates[:, 0:2], w["g_xattn"].partition_broadcast(P)).then_inc(consts, 16)
            sp.dma_start(gates[:, 2:4], w["g_ffn"].partition_broadcast(P)).then_inc(consts, 16)

            def load(b):
                if b:
                    sp.wait_ge(conv_done, ET * b)
                sp.dma_start(ctx_pad[:, :, TAPS - 1:], ctx_t[b].rearrange("(c p) l -> p c l", p=P)).then_inc(ctx_in, 16)
                if b >= 2:
                    sp.wait_ge(x1_out[b % 2], 16 * (b // 2))
                sp.dma_start(xs[:, b % 2], x[b].rearrange("(t p) d -> p t d", p=P)).then_inc(x_in[b % 2], 16)

            def spread_b(b):
                sp.wait_ge(proj_done, b + 1)
                sp.dma_start(b_rows[b], proj[32:48, :]).then_inc(rows_out, 16)
                sp.wait_ge(rows_out, 16 * (b + 1))
                lo = 0
                for q, hi in enumerate(GAPS):
                    if b:
                        sp.wait_ge(drive_done, SCANS * (b - 1) + ET * hi)
                    sp.dma_start(b_all[:, lo:hi, :], b_rows[b, lo:hi, :].partition_broadcast(P)).then_inc(rows_in[q], 16)
                    lo = hi

            load(0)
            spread_b(0)
            for b in range(B):
                if b + 1 < B:
                    load(b + 1)
                    spread_b(b + 1)
                sp.wait_ge(x1_done, LT * (b + 1))
                sp.dma_start(x1[b].rearrange("(t p) d -> p t d", p=P), xs[:, b % 2]).then_inc(x1_out[b % 2], 16)
            sp.wait_ge(x1_out[0], 16 * (B // 2))
            sp.wait_ge(x1_out[1], 16 * (B // 2))

        @block.gpsimd
        def _(pool):
            nc.gpsimd.memset(ctx_pad[:, :, 0:TAPS - 1], 0.0).then_inc(pad_zero, 1)
            nc.gpsimd.memset(half[:], -0.5).then_inc(half_set, 1)
            pool.wait_ge(half_set, 1)

            def rstd_of(b):
                pool.wait_ge(var_done, b + 1)
                nc.gpsimd.tensor_tensor(rstd[:], var_eps[:], half[:], ALU.pow).then_inc(rstd_done, 1)

            def sum_of(b):
                pool.wait_ge(ln_done, b + 1)
                for e in range(ET):
                    nc.gpsimd.tensor_tensor(sp_r[:, e, :], sp_r[:, e, :], sp_l[:, e, :], ALU.add).then_inc(sum_done, 1)

            def du_of(b):
                for e in range(ET):
                    pool.wait_ge(delta_done, ET * b + e + 1)
                    nc.gpsimd.tensor_tensor(du[:, e, :], delta[:, e, :], u[:, e, :], ALU.mult).then_inc(du_done, 1)
                pool.wait_ge(du_done, ET * (b + 1))

            rstd_of(0)
            sum_of(0)
            du_of(0)
            for b in range(B):
                def step(n, half_of):
                    row = b_all[:, n, :] if isinstance(n, int) else \
                        b_all[:, bass.ds(n, 1), :].rearrange("p o l -> p (o l)")
                    for e in range(ET):
                        if b or not isinstance(n, int) or n >= 2:
                            pool.wait_ge(scan_done, n * ET + (SCANS * b - 2 * ET + e + 1))
                            pool.sem_inc(half_free, 1)
                        nc.gpsimd.tensor_tensor(drive[:, half_of, e, :], du[:, e, :], row, ALU.mult)\
                            .then_inc(drive_done, 1)

                def gap(q):
                    if q + 1 < len(GAPS):
                        pool.wait_ge(rows_in[q + 1], 16 * (b + 1))
                    if b + 1 < B and q == 1:
                        rstd_of(b + 1)
                    if b + 1 < B and q == 4:
                        sum_of(b + 1)
                        du_of(b + 1)

                pool.wait_ge(rows_in[0], 16 * (b + 1))
                segments(pool, b, step, gap)

        @block.scalar
        def _(act):
            act.wait_ge(consts, 16 * CONSTS)
            nc.scalar.activation(tanh_g[:], gates[:], ACT.Tanh).then_inc(tanh_done, 1)
            nc.scalar.activation(a_exp[:], a_log[:], ACT.Exp).then_inc(a_done, 1)
            act.wait_ge(a_done, 1)
            nc.scalar.mul(a_neg[:], a_exp[:], -1.0).then_inc(a_done, 1)
            act.wait_ge(a_done, 2)

            def u_of(b):
                if b:
                    act.wait_ge(du_done, ET * b)
                    act.wait_ge(turned_done, ADDS * (b - 1) + LT)
                for e in range(ET):
                    act.wait_ge(conv_done, ET * b + e + 1)
                    nc.scalar.activation(u[:, e, :], work[e][:], ACT.Silu, bias=cols[:, 0, e:e + 1]).then_inc(u_done, 1)

            def proj_of(b):
                act.wait_ge(xproj_done, b + 1)
                if b:
                    act.wait_ge(rows_out, 16 * b)
                    act.wait_ge(dt_done, ET * b)
                    act.wait_ge(cT_done, b)
                nc.scalar.activation(proj[:], work[0][0:64, :], ACT.Copy).then_inc(proj_done, 1)

            def relu_of(b):
                act.wait_ge(cT_done, b + 1)
                nc.scalar.activation(c_col[:, b % 2], work[1][:, 0:LT * 64].rearrange("p (t c) -> p t c", t=LT), ACT.Copy)\
                    .then_inc(c_done, 1)
                if b:
                    act.wait_ge(turned_done, ADDS * (b - 1) + LT)
                    act.wait_ge(delta_done, ET * b)
                for e in range(ET):
                    act.wait_ge(dt_done, ET * b + e + 1)
                    bank = work[(e + 2) % 4]
                    nc.scalar.activation(sp_y[:, e, :], bank[:], ACT.Abs, bias=cols[:, 1, e:e + 1]).then_inc(relu_done, 1)
                    nc.scalar.activation(sp_r[:, e, :], bank[:], ACT.Relu, bias=cols[:, 1, e:e + 1]).then_inc(relu_done, 1)

            def ln_of(b):
                act.wait_ge(relu_done, 2 * ET * (b + 1))
                nc.scalar.activation(sp_y[:], sp_y[:], ACT.Exp, scale=-1.0).then_inc(exp_done, 1)
                act.wait_ge(exp_done, b + 1)
                nc.scalar.activation(sp_l[:], sp_y[:], ACT.Ln, bias=1.0).then_inc(ln_done, 1)

            def skip_of(b):
                act.wait_ge(soft, 2 * ET * b + 2 * ET)
                act.wait_ge(u_done, ET * (b + 1))
                for e in range(ET):
                    nc.scalar.activation(sp_y[:, e, :], u[:, e, :], ACT.Copy, scale=cols[:, 2, e:e + 1])\
                        .then_inc(skip_done, 1)

            def sz_of(b):
                if b:
                    act.wait_ge(mul_done, LT * b)
                for j in range(LT):
                    act.wait_ge(zT_done, LT * b + j + 1)
                    nc.scalar.activation(sz[:, j, :], work[j][:], ACT.Silu).then_inc(sz_done, 1)

            act.wait_ge(taps_done, TAPS * CT)
            u_of(0)
            proj_of(0)
            relu_of(0)
            ln_of(0)
            skip_of(0)
            for b in range(B):
                def step(n, half_of):
                    for e in range(ET):
                        scale = a_neg[:, e, n:n + 1] if isinstance(n, int) else a_neg[:, e, bass.ds(n, 1)]
                        if b or not isinstance(n, int) or n >= 2:
                            act.wait_ge(scan_done, n * ET + (SCANS * b - 2 * ET + e + 1))
                        nc.scalar.activation(decay[:, half_of, e, :], delta[:, e, :], ACT.Exp, scale=scale)\
                            .then_inc(decay_done, 1)

                def gap(q):
                    if q == 0:
                        sz_of(b)
                    if b + 1 < B:
                        if q == 1:
                            u_of(b + 1)
                        if q == 2:
                            proj_of(b + 1)
                        if q == 3:
                            relu_of(b + 1)
                            ln_of(b + 1)
                        if q == 4:
                            skip_of(b + 1)

                act.wait_ge(delta_done, ET * (b + 1))
                segments(act, b, step, gap)

        @block.vector
        def _(dve):
            dve.wait_ge(consts, 16 * CONSTS)
            for k in range(TAPS):
                for c in range(CT):
                    nc.vector.tensor_tensor(w_tap[:, k, c, :], w_in[:, c, :], tap_rows[:, k, :], ALU.mult).then_inc(taps_done, 1)
            dve.wait_ge(tanh_done, 1)

            def stats_of(b):
                dve.wait_ge(x_in[b % 2], 16 * (b // 2 + 1))
                if b:
                    dve.wait_ge(xn_done, LT * b)
                for i in range(LT):
                    nc.vector.bn_stats(stat[:, i, :], xs[:, b % 2, i, :]).then_inc(stat_done, 1)
                for i in range(LT):
                    dve.wait_ge(stat_done, LT * b + i + 1)
                    nc.vector.bn_aggr(mv[:, i, :], stat[:, i, :]).then_inc(mv_done, 1)
                dve.wait_ge(mv_done, LT * (b + 1))
                nc.vector.tensor_scalar_add(var_eps[:], mv[:, :, 1], EPS).then_inc(var_done, 1)

            def norm_of(b):
                dve.wait_ge(rstd_done, b + 1)
                if b:
                    dve.wait_ge(zT_done, LT * b)
                for i in range(LT):
                    nc.vector.tensor_scalar(xn[:, i, :], xs[:, b % 2, i, :], mv[:, i, 0:1], rstd[:, i:i + 1],
                                            ALU.subtract, ALU.mult).then_inc(xn_done, 1)

            def delta_of(b):
                dve.wait_ge(ln_done, b + 1)
                base = 2 * ET * b
                for e in range(ET):
                    nc.vector.tensor_scalar(delta[:, e, :], sp_y[:, e, :], 1.0, 1.0, ALU.add, ALU.subtract).then_inc(soft, 1)
                for e in range(ET):
                    dve.wait_ge(soft, base + e + 1)
                    nc.vector.tensor_tensor(delta[:, e, :], sp_y[:, e, :], delta[:, e, :], ALU.subtract).then_inc(soft, 1)
                for e in range(ET):
                    dve.wait_ge(soft, base + ET + e + 1)
                    dve.wait_ge(sum_done, ET * b + e + 1)
                    nc.vector.tensor_tensor(delta[:, e, :], sp_r[:, e, :], delta[:, e, :], ALU.add).then_inc(delta_done, 1)

            def x1_of(b):
                dve.wait_ge(sz_done, LT * (b + 1))
                for i in range(LT):
                    dve.wait_ge(add_done, ADDS * b + LT * NS + i + 1)
                    nc.vector.tensor_tensor(acc[:, i, :], acc[:, i, :], sz[:, i, :], ALU.mult).then_inc(mul_done, 1)
                for i in range(LT):
                    dve.wait_ge(mul_done, LT * b + i + 1)
                    nc.vector.scalar_tensor_tensor(xs[:, b % 2, i, :], acc[:, i, :], tanh_g[:, 0:1], xs[:, b % 2, i, :],
                                                   ALU.mult, ALU.add).then_inc(x1_done, 1)

            stats_of(0)
            norm_of(0)
            delta_of(0)
            for b in range(B):
                def adds(n):
                    for i in range(LT):
                        dve.wait_ge(turned_done, (n + 1) * LT + (ADDS * b + i + 1))
                        if isinstance(n, int) and n < 0:
                            if b:
                                dve.wait_ge(x1_done, LT * b)
                            nc.vector.tensor_copy(acc[:, i, :], turned[i][:]).then_inc(add_done, 1)
                        else:
                            col = c_col[:, b % 2, i, 48 + n:49 + n] if isinstance(n, int) else \
                                c_col[:, b % 2, i, bass.ds(n + 48, 1)]
                            dve.wait_ge(add_done, n * LT + (ADDS * b + i + 1))
                            nc.vector.scalar_tensor_tensor(acc[:, i, :], turned[i][:], col, acc[:, i, :],
                                                           ALU.mult, ALU.add).then_inc(add_done, 1)

                def step(n, half_of):
                    if isinstance(n, int) and n < 2:
                        if b:
                            dve.wait_ge(turned_done, ADDS * b - LT + LT * n)
                    else:
                        dve.wait_ge(turned_done, n * LT + ADDS * b)
                    for e in range(ET):
                        dve.wait_ge(decay_done, n * ET + (SCANS * b + e + 1))
                        dve.wait_ge(drive_done, n * ET + (SCANS * b + e + 1))
                        nc.vector.tensor_tensor_scan(state[:, half_of, e, :], decay[:, half_of, e, :],
                                                     drive[:, half_of, e, :], 0.0, ALU.mult, ALU.add).then_inc(scan_done, 1)
                    adds(n - 1)

                def gap(q):
                    if q == 4:
                        adds(NS - 1)
                        if b + 1 < B:
                            delta_of(b + 1)
                        x1_of(b)
                    if b + 1 < B:
                        if q == 0:
                            stats_of(b + 1)
                        if q == 2:
                            norm_of(b + 1)

                if b == 0:
                    dve.wait_ge(c_done, 1)
                else:
                    dve.wait_ge(c_done, b + 1)
                segments(dve, b, step, gap)

        @block.tensor
        def _(pe):
            pe.wait_ge(consts, 16 * CONSTS)
            pe.wait_ge(pad_zero, 1)
            pe.wait_ge(taps_done, TAPS * CT)

            def conv_of(b, part):
                if part == 0:
                    pe.wait_ge(ctx_in, 16 * (b + 1))
                share = ET * TAPS // CONV
                for n in range(part * share, (part + 1) * share):
                    e, k = n // TAPS, n % TAPS
                    if b and k == 0:
                        pe.wait_ge(sz_done, LT * (b - 1) + e + 1)
                    for c in range(CT):
                        mm = nc.tensor.matmul(work[e][:], w_tap[:, k, c, e * P:(e + 1) * P], ctx_pad[:, c, k:k + L],
                                              start=(k == 0 and c == 0), stop=(k == TAPS - 1 and c == CT - 1))
                    if k == TAPS - 1:
                        mm.then_inc(conv_done, 1)

            def xproj_of(b):
                for e in range(ET):
                    pe.wait_ge(u_done, ET * b + e + 1)
                    mm = nc.tensor.matmul(work[0][0:64, :], w_x[:, e, :], u[:, e, :], start=(e == 0), stop=(e == ET - 1))
                mm.then_inc(xproj_done, 1)

            def turn_proj(b):
                pe.wait_ge(proj_done, b + 1)
                for i in range(LT):
                    mm = nc.tensor.transpose(work[1][:, i * 64:(i + 1) * 64], proj[:, i * P:(i + 1) * P], ident[0:64, 0:64])
                mm.then_inc(cT_done, 1)
                for e in range(ET):
                    if e == 3:
                        pe.wait_ge(c_done, b + 1)
                    mm = nc.tensor.matmul(work[(e + 2) % 4][:], w_dt[:, e * P:(e + 1) * P], proj[0:DR, :], start=True, stop=True)
                    mm.then_inc(dt_done, 1)

            def turn_z(b):
                for j in range(LT):
                    pe.wait_ge(relu_done, 2 * ET * (b + 1))
                    pe.wait_ge(xn_done, LT * (b + 1))
                    for i in range(LT):
                        mm = nc.tensor.transpose(work[j][:, i * P:(i + 1) * P], xn[:, i, j * P:(j + 1) * P], ident[:])
                    mm.then_inc(zT_done, 1)

            def turn(src, n, b):
                for i in range(LT):
                    if b or not (isinstance(n, int) and n < 0):
                        pe.wait_ge(add_done, n * LT + (ADDS * b + i + 1))
                    for e in range(ET):
                        mm = nc.tensor.transpose(turned[i][:, e * P:(e + 1) * P], src(e)[:, i * P:(i + 1) * P], ident[:])
                    mm.then_inc(turned_done, 1)

            for part in range(CONV):
                conv_of(0, part)
            xproj_of(0)
            turn_proj(0)
            for b in range(B):
                pe.wait_ge(skip_done, ET * (b + 1))
                turn(lambda e: sp_y[:, e, :], -1, b)
                for n in range(NS):
                    pe.wait_ge(scan_done, SCANS * b + ET * (n + 1))
                    turn(lambda e: state[:, n % 2, e, :], n, b)
                    if n == 0:
                        turn_z(b)
                    if b + 1 < B:
                        if n < CONV:
                            conv_of(b + 1, n)
                        if n == 9:
                            xproj_of(b + 1)
                        if n == 11:
                            turn_proj(b + 1)


def moe_block(nc, w, x1, x2, w_mix):
    PAIRS = GR
    CUTS = (3, 6, PAIRS - 1)
    with ExitStack() as stack:
        def sb(name, shape, dt=F32):
            return stack.enter_context(nc.sbuf_tensor("m_" + name, shape, dt))

        def sem(name):
            return stack.enter_context(nc.semaphore("moe_" + name))

        ident = sb("ident", [P, P])
        gates = sb("gates", [P, 2])
        tanh_g = sb("tanh_g", [P, 2])
        scale_out = sb("scale_out", [P, 1])
        iota = sb("iota", [P, NE])
        half = sb("half", [P, LT])
        b_up = sb("b_up", [P, HT])
        pick = sb("pick", [GR, GR * P])
        pick16 = sb("pick16", [GR, GR * P], F16)
        small = sb("small", [P, DT * NE])
        b_down = sb("b_down", [GR, D])
        gw = sb("gw", [P, 2, DT * NE], F16)
        bd = sb("bd", [GR, 2, D], F16)
        raw_up = sb("raw_up", [P, 2, 2, DT * P])
        raw_dn = sb("raw_dn", [P, 2, 2, D])
        up = sb("up", [P, 2, HT, DT, P], F16)
        dn = sb("dn", [P, 2, HT, D], F16)
        xs = sb("xs", [P, 2, LT, D])
        xn = sb("xn", [P, LT, D])
        stat = sb("stat", [P, LT, 6])
        mv = sb("mv", [P, LT, 2])
        var_eps = sb("var_eps", [P, LT])
        rstd = sb("rstd", [P, LT])
        xt = sb("xt", [P, 2, 2, DT, L], F16)
        logit = sb("logit", [P, LT, NE])
        top = sb("top", [P, LT, 8])
        top_at = sb("top_at", [P, LT, 8], U32)
        at = sb("at", [P, LT, 2])
        e1 = sb("e1", [P, LT])
        ge = sb("ge", [P, 4, LT])
        gate = sb("gate", [P, LT, GR])
        second = sb("second", [P, LT, NE])
        gt = sb("gt", [GR, 2, 2, L], F16)
        hid = sb("hid", [P, 2, L])
        gated = sb("gated", [P, 2, L])
        h16 = sb("h16", [P, 2, 2, L], F16)
        mix = sb("mix", [P, 2, FT, P])
        bank_up = [stack.enter_context(nc.psum_tensor(f"moe_up{i}", [P, 512], F32)) for i in range(2)]
        bank_gate = stack.enter_context(nc.psum_tensor("moe_gate", [P, 512], F32))
        bank_prep = stack.enter_context(nc.psum_tensor("moe_prep", [P, 512], F32))
        bank_out = [stack.enter_context(nc.psum_tensor(f"moe_out{i}", [P, 512], F32)) for i in range(LT)]

        consts = sem("consts")
        x_in = [sem("x_in_even"), sem("x_in_odd")]
        raw_in = [sem("raw_in_even"), sem("raw_in_odd")]
        split_hi = sem("split_hi")
        split_lo = sem("split_lo")
        small_hi = sem("small_hi")
        small_lo = sem("small_lo")
        half_set = sem("half_set")
        tanh_done = sem("tanh_done")
        var_done = sem("var_done")
        rstd_done = sem("rstd_done")
        xn_done = sem("xn_done")
        xT_done = sem("xT_done")
        xT_hi = sem("xT_hi")
        xT_lo = sem("xT_lo")
        logit_done = sem("logit_done")
        diff_done = sem("diff_done")
        e1_done = sem("e1_done")
        gate_done = sem("gate_done")
        gateT_done = sem("gateT_done")
        gt_hi = sem("gt_hi")
        gt_lo = sem("gt_lo")
        picked = sem("picked")
        up_done = sem("up_done")
        gelu_done = sem("gelu_done")
        gated_done = sem("gated_done")
        hi_done = sem("hi_done")
        h_done = sem("h_done")
        down_done = sem("down_done")
        x2_done = sem("x2_done")
        x2_out = [sem("x2_out_even"), sem("x2_out_odd")]
        chain = sem("chain")
        mix_in = sem("mix_in")
        mixed = sem("mixed")
        mix_out = sem("mix_out")
        CONSTS = 8
        block = stack.enter_context(nc.Block())

        def pairs(eng, b, body, gap):
            lo = 0
            for q, hi in enumerate(CUTS):
                if b == 0:
                    for j in range(lo, hi):
                        body(j)
                else:
                    with eng.Fori(lo, hi) as j:
                        body(j)
                lo = hi
                gap(q)

        @block.sync
        def _(sp):
            def load(b):
                if b >= 2:
                    sp.wait_ge(x2_out[b % 2], 16 * (b // 2))
                sp.dma_start(xs[:, b % 2], x1[b].rearrange("(t p) d -> p t d", p=P)).then_inc(x_in[b % 2], 16)

            load(0)
            for dst, src in ((ident, "ident"), (iota, "iota"), (b_up, "b_up"), (pick, "pick"), (small, "gate_w"),
                             (b_down, "b_down")):
                sp.dma_start(dst[:], w[src]).then_inc(consts, 16)
            sp.dma_start(gates[:, 0:1], w["g_ffn"][0:1].partition_broadcast(P)).then_inc(consts, 16)
            sp.dma_start(gates[:, 1:2], w["g_ffn"][1:2].partition_broadcast(P)).then_inc(consts, 16)
            load(1)
            for j in range(PAIRS):
                if j >= 2:
                    sp.wait_ge(split_hi, 2 * (j - 1))
                    sp.wait_ge(split_lo, 2 * (j - 1))
                sp.dma_start(raw_up[:, j % 2], w["w_up"][:, 2 * j:2 * j + 2, :]).then_inc(raw_in[j % 2], 16)
                sp.dma_start(raw_dn[:, j % 2], w["w_down"][:, 2 * j:2 * j + 2, :]).then_inc(raw_in[j % 2], 16)
            for b in range(B):
                if 2 <= b + 1 < B:
                    load(b + 1)
                sp.wait_ge(x2_done, LT * (b + 1))
                sp.dma_start(x2[b].rearrange("(t p) d -> p t d", p=P), xs[:, b % 2]).then_inc(x2_out[b % 2], 16)
            sp.wait_ge(x2_out[0], 16 * (B // 2))
            sp.wait_ge(x2_out[1], 16 * (B // 2))

        @block.gpsimd
        def _(pool):
            nc.gpsimd.memset(half[:], -0.5).then_inc(half_set, 1)
            nc.gpsimd.memset(gate[:, :, NE:GR], 1.0).then_inc(half_set, 1)
            pool.wait_ge(half_set, 2)
            stage = [0]

            def mix_quarter(c):
                if c:
                    pool.wait_ge(mix_out, 16 * c)
                pool.dma_start(mix[:, 0], w["w_out"][:, :, c * P:(c + 1) * P]).then_inc(mix_in, 16)
                pool.wait_ge(mix_in, 16 * (c + 1))
                span, side = 1, 0
                while span < FT:
                    src = mix[:, side].rearrange("p (g two s) d -> p g two (s d)", two=2, s=span)
                    dst = mix[:, 1 - side].rearrange("p (g two s) d -> p g two (s d)", two=2, s=span)
                    for half_of, op in ((0, ALU.add), (1, ALU.subtract)):
                        nc.gpsimd.tensor_tensor(dst[:, :, half_of, :], src[:, :, 0, :], src[:, :, 1, :], op)\
                            .then_inc(mixed, 1)
                    stage[0] += 2
                    pool.wait_ge(mixed, stage[0])
                    span, side = 2 * span, 1 - side
                pool.dma_start(w_mix[:, :, c * P:(c + 1) * P], mix[:, side]).then_inc(mix_out, 16)

            for b in range(B):
                pool.wait_ge(var_done, b + 1)
                nc.gpsimd.tensor_tensor(rstd[:], var_eps[:], half[:], ALU.pow).then_inc(rstd_done, 1)
                if b < B - 1:
                    mix_quarter(b)
            mix_quarter(B - 1)
            pool.wait_ge(mix_out, 16 * B)

        @block.scalar
        def _(act):
            def split(j):
                act.wait_ge(raw_in[j % 2], 32 * (j // 2 + 1))
                nc.scalar.activation(up[:, 0, 2 * j:2 * j + 2].rearrange("p t c q -> p t (c q)"), raw_up[:, j % 2], ACT.Copy, scale=WS)\
                    .then_inc(split_hi, 1)
                nc.scalar.activation(dn[:, 0, 2 * j:2 * j + 2], raw_dn[:, j % 2], ACT.Copy, scale=WS).then_inc(split_hi, 1)

            def turn_hi(b):
                for c in range(DT):
                    act.wait_ge(xT_done, DT * b + c + 1)
                    if b >= 2 and c == 0:
                        act.wait_ge(down_done, HT * (b - 1))
                    nc.scalar.activation(xt[:, b % 2, 0, c, :], bank_prep[:], ACT.Copy).then_inc(xT_hi, 1)

            def second_gate(b):
                act.wait_ge(diff_done, b + 1)
                nc.scalar.activation(e1[:], ge[:, 0, :], ACT.Exp, scale=1.0 / WS).then_inc(e1_done, 1)

            def gates_hi(b):
                act.wait_ge(gateT_done, b + 1)
                nc.scalar.activation(gt[:, b % 2, 0, :], bank_prep[0:GR, :], ACT.Copy).then_inc(gt_hi, 1)

            def tile(t, side, b, first):
                act.wait_ge(up_done, t + (HT * b + 1))
                if not first:
                    act.wait_ge(gated_done, t + (HT * b - 1))
                bias = b_up[:, t:t + 1] if isinstance(t, int) else b_up[:, bass.ds(t, 1)]
                nc.scalar.activation(hid[:, side, :], bank_up[side][:], ACT.Gelu, bias=bias, scale=1.0 / WS).then_inc(gelu_done, 1)

            act.wait_ge(consts, 16 * CONSTS)
            nc.scalar.activation(tanh_g[:], gates[:], ACT.Tanh).then_inc(tanh_done, 1)
            nc.scalar.activation(gw[:, 0, :], small[:], ACT.Copy, scale=WS).then_inc(small_hi, 1)
            nc.scalar.activation(bd[:, 0, :], b_down[:], ACT.Copy, scale=WS).then_inc(small_hi, 1)
            nc.scalar.activation(pick16[:], pick[:], ACT.Copy).then_inc(small_hi, 1)
            split(0)
            turn_hi(0)
            second_gate(0)
            gates_hi(0)
            for b in range(B):
                def body(j):
                    if b == 0:
                        split(j + 1)
                    for k in (0, 1):
                        tile(j * 2 + k, k, b, b == 0 and isinstance(j, int) and j == 0)

                def gap(q):
                    if b + 1 < B:
                        if q == 0:
                            turn_hi(b + 1)
                        if q == 1:
                            second_gate(b + 1)
                            gates_hi(b + 1)

                pairs(act, b, body, gap)
                for t in (HT - 2, HT - 1):
                    tile(t, t % 2, b, False)

        @block.vector
        def _(dve):
            links = [0]

            def link(ins):
                links[0] += 1
                ins.then_inc(chain, 1)
                dve.wait_ge(chain, links[0])

            def split(j):
                dve.wait_ge(split_hi, 2 * j + 2)
                nc.vector.scalar_tensor_tensor(up[:, 1, 2 * j:2 * j + 2].rearrange("p t c q -> p t (c q)"), raw_up[:, j % 2], WS,
                                               up[:, 0, 2 * j:2 * j + 2].rearrange("p t c q -> p t (c q)"),
                                               ALU.mult, ALU.subtract).then_inc(split_lo, 1)
                nc.vector.scalar_tensor_tensor(dn[:, 1, 2 * j:2 * j + 2], raw_dn[:, j % 2], WS, dn[:, 0, 2 * j:2 * j + 2],
                                               ALU.mult, ALU.subtract).then_inc(split_lo, 1)

            def norm_of(b):
                dve.wait_ge(x_in[b % 2], 16 * (b // 2 + 1))
                if b:
                    dve.wait_ge(xT_done, DT * b)
                for i in range(LT):
                    ins = nc.vector.bn_stats(stat[:, i, :], xs[:, b % 2, i, :])
                link(ins)
                for i in range(LT):
                    ins = nc.vector.bn_aggr(mv[:, i, :], stat[:, i, :])
                link(ins)
                nc.vector.tensor_scalar_add(var_eps[:], mv[:, :, 1], EPS).then_inc(var_done, 1)
                dve.wait_ge(rstd_done, b + 1)
                for i in range(LT):
                    nc.vector.tensor_scalar(xn[:, i, :], xs[:, b % 2, i, :], mv[:, i, 0:1], rstd[:, i:i + 1],
                                            ALU.subtract, ALU.mult).then_inc(xn_done, 1)

            def turn_lo(b):
                for c in range(DT):
                    dve.wait_ge(xT_hi, DT * b + c + 1)
                    nc.vector.tensor_tensor(xt[:, b % 2, 1, c, :], bank_prep[:], xt[:, b % 2, 0, c, :], ALU.subtract).then_inc(xT_lo, 1)

            def route(b):
                dve.wait_ge(logit_done, b + 1)
                link(nc.vector.tensor_copy(logit[:].rearrange("p t e -> p (t e)"), bank_prep[:, 0:LT * NE]))
                for i in range(LT):
                    ins = nc.vector.max(top[:, i, :], logit[:, i, :])
                link(ins)
                nc.vector.tensor_tensor(ge[:, 0, :], top[:, :, 1], top[:, :, 0], ALU.subtract).then_inc(diff_done, 1)
                for i in range(LT):
                    ins = nc.vector.max_index(top_at[:, i, :], top[:, i, :], logit[:, i, :])
                link(ins)
                nc.vector.tensor_copy(at[:], top_at[:, :, 0:2])
                dve.wait_ge(e1_done, b + 1)
                link(nc.vector.tensor_scalar_add(ge[:, 1, :], e1[:], 1.0))
                link(nc.vector.reciprocal(ge[:, 2, :], ge[:, 1, :]))
                link(nc.vector.tensor_tensor(ge[:, 3, :], e1[:], ge[:, 2, :], ALU.mult))
                if b:
                    dve.wait_ge(gateT_done, b)
                for i in range(LT):
                    nc.vector.tensor_scalar(gate[:, i, 0:NE], iota[:], at[:, i, 0:1], ge[:, 2, i:i + 1], ALU.is_equal, ALU.mult)
                    ins = nc.vector.tensor_scalar(second[:, i, :], iota[:], at[:, i, 1:2], ge[:, 3, i:i + 1], ALU.is_equal, ALU.mult)
                link(ins)
                nc.vector.tensor_tensor(gate[:, :, 0:NE], gate[:, :, 0:NE], second[:], ALU.add).then_inc(gate_done, 1)

            def gates_lo(b):
                dve.wait_ge(gt_hi, b + 1)
                nc.vector.tensor_tensor(gt[:, b % 2, 1, :], bank_prep[0:GR, :], gt[:, b % 2, 0, :], ALU.subtract).then_inc(gt_lo, 1)

            def tile(t, side, b, first):
                dve.wait_ge(gelu_done, t + (HT * b + 1))
                if side == 0:
                    dve.wait_ge(picked, tile.pair(t, b))
                nc.vector.tensor_tensor(gated[:, side, :], hid[:, side, :], bank_gate[:], ALU.mult).then_inc(gated_done, 1)
                dve.wait_ge(gated_done, t + (HT * b + 1))
                if not first:
                    dve.wait_ge(down_done, t + (HT * b - 1))
                nc.vector.tensor_copy(h16[:, side, 0, :], gated[:, side, :]).then_inc(hi_done, 1)
                dve.wait_ge(hi_done, t + (HT * b + 1))
                nc.vector.tensor_tensor(h16[:, side, 1, :], gated[:, side, :], h16[:, side, 0, :], ALU.subtract).then_inc(h_done, 1)

            def x2_of(b):
                for i in range(LT):
                    if i == 0:
                        dve.wait_ge(down_done, HT * (b + 1))
                    nc.vector.scalar_tensor_tensor(xs[:, b % 2, i, :], bank_out[i][:], scale_out[:], xs[:, b % 2, i, :],
                                                   ALU.mult, ALU.add).then_inc(x2_done, 1)

            dve.wait_ge(consts, 16 * CONSTS)
            dve.wait_ge(tanh_done, 1)
            nc.vector.tensor_scalar_mul(scale_out[:], tanh_g[:, 0:1], 1.0 / WS)
            dve.wait_ge(small_hi, 2)
            nc.vector.scalar_tensor_tensor(gw[:, 1, :], small[:], WS, gw[:, 0, :], ALU.mult, ALU.subtract).then_inc(small_lo, 1)
            nc.vector.scalar_tensor_tensor(bd[:, 1, :], b_down[:], WS, bd[:, 0, :], ALU.mult, ALU.subtract).then_inc(small_lo, 1)
            norm_of(0)
            split(0)
            turn_lo(0)
            dve.wait_ge(half_set, 2)
            route(0)
            gates_lo(0)
            for b in range(B):
                def body(j):
                    if b == 0:
                        split(j + 1)
                    tile.pair = lambda t, b: j + (PAIRS * b + 1)
                    for k in (0, 1):
                        tile(j * 2 + k, k, b, b == 0 and isinstance(j, int) and j == 0)

                def gap(q):
                    if b + 1 < B:
                        if q == 0:
                            norm_of(b + 1)
                            turn_lo(b + 1)
                        if q == 1:
                            route(b + 1)
                            gates_lo(b + 1)

                pairs(dve, b, body, gap)
                tile.pair = lambda t, b: PAIRS * (b + 1)
                for t in (HT - 2, HT - 1):
                    tile(t, t % 2, b, False)
                x2_of(b)

        @block.tensor
        def _(pe):
            def turn(b):
                for c in range(DT):
                    pe.wait_ge(xn_done, LT * (b + 1))
                    if c or b:
                        pe.wait_ge(xT_lo, DT * b + c)
                    if b and c == 0:
                        pe.wait_ge(gt_lo, b)
                    for i in range(LT):
                        mm = nc.tensor.transpose(bank_prep[:, i * P:(i + 1) * P], xn[:, i, c * P:(c + 1) * P], ident[:])
                    mm.then_inc(xT_done, 1)

            def logits(b):
                pe.wait_ge(xT_lo, DT * (b + 1))
                pe.wait_ge(small_lo, 2)
                for i in range(LT):
                    n = 0
                    for c in range(DT):
                        for xh, wh in ((0, 0), (0, 1), (1, 0)):
                            mm = nc.tensor.matmul(bank_prep[:, i * NE:(i + 1) * NE], xt[:, b % 2, xh, c, i * P:(i + 1) * P],
                                                  gw[:, wh, c * NE:(c + 1) * NE], start=(n == 0), stop=(n == 3 * DT - 1))
                            n += 1
                mm.then_inc(logit_done, 1)

            def turn_gates(b):
                pe.wait_ge(gate_done, b + 1)
                for i in range(LT):
                    mm = nc.tensor.transpose(bank_prep[0:GR, i * P:(i + 1) * P], gate[:, i, :], ident[:])
                mm.then_inc(gateT_done, 1)

            def start_out(b):
                pe.wait_ge(gt_lo, b + 1)
                if b:
                    pe.wait_ge(x2_done, LT * b)
                for i in range(LT):
                    for n, (gh, bh) in enumerate(((0, 0), (0, 1), (1, 0))):
                        nc.tensor.matmul(bank_out[i][:], gt[:, b % 2, gh, i * P:(i + 1) * P], bd[:, bh, :],
                                         start=(n == 0), stop=False)

            def spread_gate(j, b, first=False):
                if not first:
                    pe.wait_ge(gated_done, j * 2 + HT * b)
                for hl in (0, 1):
                    lhs = pick16[:, j * P:(j + 1) * P] if isinstance(j, int) else pick16[:, bass.ds(j * P, P)]
                    mm = nc.tensor.matmul(bank_gate[:], lhs, gt[:, b % 2, hl, :], start=(hl == 0), stop=(hl == 1))
                mm.then_inc(picked, 1)

            def tile_up(t, side, b):
                if b == 0:
                    pe.wait_ge(split_lo, 2 * (t // 2) + 2)
                if b or t >= 2:
                    pe.wait_ge(gelu_done, t + (HT * b - 1))
                n = 0
                for c in range(DT):
                    for wh, xh in ((0, 0), (0, 1), (1, 0)):
                        wt = up[:, wh, t, c, :] if isinstance(t, int) else \
                            up[:, wh, bass.ds(t, 1), c, :].rearrange("p o q -> p (o q)")
                        mm = nc.tensor.matmul(bank_up[side][:], wt, xt[:, b % 2, xh, c, :], start=(n == 0), stop=(n == 3 * DT - 1))
                        n += 1
                mm.then_inc(up_done, 1)

            def tile_down(t, side, b, last=False):
                pe.wait_ge(h_done, t + (HT * b + 1))
                for i in range(LT):
                    for n, (hh, wh) in enumerate(((0, 0), (0, 1), (1, 0))):
                        wt = dn[:, wh, t, :] if isinstance(t, int) else \
                            dn[:, wh, bass.ds(t, 1), :].rearrange("p o d -> p (o d)")
                        mm = nc.tensor.matmul(bank_out[i][:], h16[:, side, hh, i * P:(i + 1) * P], wt,
                                              start=False, stop=(last and n == 2))
                mm.then_inc(down_done, 1)

            pe.wait_ge(consts, 16 * CONSTS)
            turn(0)
            logits(0)
            turn_gates(0)
            for b in range(B):
                def body(j):
                    tile_down(j * 2, 0, b)
                    tile_up(j * 2 + 2, 0, b)
                    tile_down(j * 2 + 1, 1, b)
                    spread_gate(j + 1, b)
                    tile_up(j * 2 + 3, 1, b)

                def gap(q):
                    if b + 1 < B:
                        if q == 0:
                            turn(b + 1)
                        if q == 1:
                            logits(b + 1)
                            turn_gates(b + 1)

                start_out(b)
                spread_gate(0, b, first=b == 0)
                tile_up(0, 0, b)
                tile_up(1, 1, b)
                pairs(pe, b, body, gap)
                tile_down(HT - 2, 0, b)
                tile_down(HT - 1, 1, b, last=True)


def ffn_block(nc, w, ctx_t, x2, w_mix, out):
    PAIRS = FT // 2
    CUTS = (2, 4, 6, PAIRS - 1)
    MIX = WS * float(H) ** -0.5
    USES = 11
    with ExitStack() as stack:
        def sb(name, shape, dt=F32):
            return stack.enter_context(nc.sbuf_tensor("f_" + name, shape, dt))

        def sem(name):
            return stack.enter_context(nc.semaphore("ffn_" + name))

        ident = sb("ident", [P, P])
        hada = sb("hada", [P, P])
        gates = sb("gates", [P, 2])
        tanh_g = sb("tanh_g", [P, 2])
        scale_out = sb("scale_out", [P, 1])
        half = sb("half", [P, LT])
        w_q = sb("w_q", [P, CT, P])
        w_k = sb("w_k", [P, CT, P])
        b_qk = sb("b_qk", [P, 2])
        raw = sb("raw", [P, 2, 2, DT * P])
        raw_mix = sb("raw_mix", [P, 4, D])
        wg = sb("wg", [P, 2, FT, DT, P], F16)
        wl = sb("wl", [P, 2, FT, DT, P], F16)
        wo = sb("wo", [P, 2, FT, D], F16)
        ctxs = sb("ctxs", [P, CT, L])
        qk = sb("qk", [P, 2, L])
        xs = sb("xs", [P, 2, LT, D])
        xn = sb("xn", [P, LT, D])
        stat = sb("stat", [P, LT, 6])
        mv = sb("mv", [P, LT, 2])
        var_eps = sb("var_eps", [P, LT])
        rstd = sb("rstd", [P, LT])
        neg_max = sb("neg_max", [P, LT])
        total = sb("total", [P, LT])
        inv = sb("inv", [P, LT])
        energy = sb("energy", [P, LT, L])
        prob = sb("prob", [P, LT, L])
        probT = sb("probT", [P, LT, L])
        xt32 = sb("xt32", [P, DT, L])
        xt = sb("xt", [P, 2, 2, DT, L], F16)
        sg = sb("sg", [P, 2, L])
        hid = sb("hid", [P, 2, L])
        h16 = sb("h16", [P, 2, 2, L], F16)
        bank_g = stack.enter_context(nc.psum_tensor("ffn_g", [P, 512], F32))
        bank_u = stack.enter_context(nc.psum_tensor("ffn_u", [P, 512], F32))
        prep = [stack.enter_context(nc.psum_tensor(f"ffn_prep{i}", [P, 512], F32)) for i in range(2)]
        bank_out = [stack.enter_context(nc.psum_tensor(f"ffn_out{i}", [P, 512], F32)) for i in range(LT)]

        consts = sem("consts")
        x_in = [sem("x_in_even"), sem("x_in_odd")]
        ctx_in = sem("ctx_in")
        raw_in = [sem("raw_in_even"), sem("raw_in_odd")]
        mix_in = [sem(f"mix_in{i}") for i in range(4)]
        mix_done = sem("mix_done")
        mix_hi = sem("mix_hi")
        mix_lo = sem("mix_lo")
        split_hi = sem("split_hi")
        split_lo = sem("split_lo")
        half_set = sem("half_set")
        tanh_done = sem("tanh_done")
        var_done = sem("var_done")
        rstd_done = sem("rstd_done")
        xn_done = sem("xn_done")
        filled = [sem("filled0"), sem("filled1")]
        qk_done = sem("qk_done")
        max_done = sem("max_done")
        energy_done = sem("energy_done")
        exp_done = sem("exp_done")
        prob_done = sem("prob_done")
        xt32_done = sem("xt32_done")
        probT_done = sem("probT_done")
        x3_done = sem("x3_done")
        xT_hi = sem("xT_hi")
        xT_lo = sem("xT_lo")
        g_done = sem("g_done")
        u_done = sem("u_done")
        silu_done = sem("silu_done")
        hid_done = sem("hid_done")
        hi_done = sem("hi_done")
        h_done = sem("h_done")
        down_done = sem("down_done")
        out_done = sem("out_done")
        out_sent = [sem("out_sent_even"), sem("out_sent_odd")]
        chain = sem("chain")
        CONSTS = 8
        Q, K, ENERGY, XT32, PROBT, PRODUCT, XT = 0, 1, 2, 6, 10, 14, 18
        block = stack.enter_context(nc.Block())

        def bank(use):
            return prep[use % 2]

        def full(eng, use, b):
            eng.wait_ge(filled[use % 2], USES * b + use // 2 + 1)

        def read_last(eng, use, b):
            if use < ENERGY:
                eng.wait_ge(qk_done, 2 * b + use + 1)
            elif use < XT32:
                eng.wait_ge(energy_done, LT * b + use - ENERGY + 1)
            elif use < PROBT:
                eng.wait_ge(xt32_done, DT * b + use - XT32 + 1)
            elif use < PRODUCT:
                eng.wait_ge(probT_done, LT * b + use - PROBT + 1)
            elif use < XT:
                eng.wait_ge(x3_done, LT * b + use - PRODUCT + 1)
            else:
                eng.wait_ge(xT_lo, DT * b + use - XT + 1)

        def empty(eng, use, b):
            if use >= 2:
                read_last(eng, use - 2, b)
            elif b:
                read_last(eng, use - 2 + 2 * USES, b - 1)

        def pairs(eng, b, body, gap):
            lo = 0
            for q, hi in enumerate(CUTS):
                if b == 0:
                    for j in range(lo, hi):
                        body(j)
                else:
                    if lo == 0:
                        body(0)
                    with eng.Fori(max(lo, 1), hi) as j:
                        body(j)
                lo = hi
                gap(q)

        @block.sync
        def _(sp):
            def load(b):
                if b:
                    sp.wait_ge(filled[1], USES * (b - 1) + K // 2 + 1)
                sp.dma_start(ctxs[:], ctx_t[b].rearrange("(c p) l -> p c l", p=P)).then_inc(ctx_in, 16)
                if b >= 2:
                    sp.wait_ge(out_sent[b % 2], 16 * (b // 2))
                sp.dma_start(xs[:, b % 2], x2[b].rearrange("(t p) d -> p t d", p=P)).then_inc(x_in[b % 2], 16)

            load(0)
            for dst, src in ((ident[:], "ident"), (hada[:], "hadamard"), (w_q[:], "w_q"), (w_k[:], "w_k"),
                             (b_qk[:, 0:1], "b_q"), (b_qk[:, 1:2], "b_k")):
                sp.dma_start(dst, w[src]).then_inc(consts, 16)
            sp.dma_start(gates[:, 0:1], w["g_xattn"][1:2].partition_broadcast(P)).then_inc(consts, 16)
            sp.dma_start(gates[:, 1:2], w["g_ffn"][1:2].partition_broadcast(P)).then_inc(consts, 16)
            for t in range(FT):
                if t >= 4:
                    sp.wait_ge(mix_done, t - 3)
                sp.dma_start(raw_mix[:, t % 4], w_mix[:, t, :]).then_inc(mix_in[t % 4], 16)
            load(1)
            for t in range(FT):
                if t >= 2:
                    sp.wait_ge(split_hi, 2 * (t - 1))
                    sp.wait_ge(split_lo, 2 * (t - 1))
                sp.dma_start(raw[:, t % 2, 0], w["w_gate"][:, t, :]).then_inc(raw_in[t % 2], 16)
                sp.dma_start(raw[:, t % 2, 1], w["w_lin"][:, t, :]).then_inc(raw_in[t % 2], 16)
            for b in range(B):
                if 2 <= b + 1 < B:
                    load(b + 1)
                sp.wait_ge(out_done, LT * (b + 1))
                sp.dma_start(out[b].rearrange("(t p) d -> p t d", p=P), xs[:, b % 2]).then_inc(out_sent[b % 2], 16)
            sp.wait_ge(out_sent[0], 16 * (B // 2))
            sp.wait_ge(out_sent[1], 16 * (B // 2))

        @block.gpsimd
        def _(pool):
            nc.gpsimd.memset(half[:], -0.5).then_inc(half_set, 1)
            pool.wait_ge(half_set, 1)
            for n in range(2 * B):
                pool.wait_ge(var_done, n + 1)
                nc.gpsimd.tensor_tensor(rstd[:], var_eps[:], half[:], ALU.pow).then_inc(rstd_done, 1)

        @block.scalar
        def _(act):
            def split(t):
                act.wait_ge(raw_in[t % 2], 32 * (t // 2 + 1))
                nc.scalar.activation(wg[:, 0, t].rearrange("p c q -> p (c q)"), raw[:, t % 2, 0], ACT.Copy, scale=WS).then_inc(split_hi, 1)
                nc.scalar.activation(wl[:, 0, t].rearrange("p c q -> p (c q)"), raw[:, t % 2, 1], ACT.Copy, scale=WS).then_inc(split_hi, 1)

            def mix(group):
                for t in range(4 * group, 4 * group + 4):
                    act.wait_ge(mix_done, t + 1)
                    nc.scalar.activation(wo[:, 0, t, :], bank_out[t % 4][:], ACT.Copy, scale=MIX).then_inc(mix_hi, 1)

            def attend(b):
                if b:
                    full(act, ENERGY + 3, b - 1)
                full(act, Q, b)
                nc.scalar.activation(qk[:, 0, :], bank(Q)[:], ACT.Identity, bias=b_qk[:, 0:1]).then_inc(qk_done, 1)
                full(act, K, b)
                nc.scalar.activation(qk[:, 1, :], bank(K)[:], ACT.Identity, bias=b_qk[:, 1:2]).then_inc(qk_done, 1)
                for i in range(LT):
                    full(act, ENERGY + i, b)
                    if b and i == 0:
                        act.wait_ge(exp_done, LT * b)
                    nc.scalar.activation(energy[:, i, :], bank(ENERGY + i)[:], ACT.Copy).then_inc(energy_done, 1)
                for i in range(LT):
                    act.wait_ge(max_done, LT * b + i + 1)
                    if b and i == 0:
                        full(act, PROBT + 3, b - 1)
                    nc.scalar.activation(prob[:, i, :], energy[:, i, :], ACT.Exp, bias=neg_max[:, i:i + 1],
                                         accum_out=total[:, i:i + 1]).then_inc(exp_done, 1)

            def copy_xt32(b):
                for c in range(DT):
                    full(act, XT32 + c, b)
                    if b and c == 0:
                        act.wait_ge(x3_done, LT * b)
                    nc.scalar.activation(xt32[:, c, :], bank(XT32 + c)[:], ACT.Copy).then_inc(xt32_done, 1)

            def copy_probT(b):
                for c in range(LT):
                    full(act, PROBT + c, b)
                    if b and c == 0:
                        act.wait_ge(x3_done, LT * b)
                    nc.scalar.activation(probT[:, c, :], bank(PROBT + c)[:], ACT.Copy).then_inc(probT_done, 1)

            def turn_hi(b):
                for c in range(DT):
                    full(act, XT + c, b)
                    if b >= 2 and c == 0:
                        act.wait_ge(down_done, FT * (b - 1))
                    nc.scalar.activation(xt[:, b % 2, 0, c, :], bank(XT + c)[:], ACT.Copy).then_inc(xT_hi, 1)

            def tile(t, side, b, first):
                act.wait_ge(g_done, t + (FT * b + 1))
                if not first:
                    act.wait_ge(hid_done, t + (FT * b - 1))
                nc.scalar.activation(sg[:, side, :], bank_g[:], ACT.Silu, scale=1.0 / WS).then_inc(silu_done, 1)

            act.wait_ge(consts, 16 * CONSTS)
            nc.scalar.activation(tanh_g[:], gates[:], ACT.Tanh).then_inc(tanh_done, 1)
            attend(0)
            mix(0)
            copy_xt32(0)
            mix(1)
            copy_probT(0)
            mix(2)
            mix(3)
            split(0)
            turn_hi(0)
            for b in range(B):
                def body(j):
                    for k in (0, 1):
                        if b == 0:
                            split(2 * j + k + 1)
                        tile(j * 2 + k, k, b, b == 0 and isinstance(j, int) and j == 0)

                def gap(q):
                    if b + 1 < B:
                        if q == 0:
                            attend(b + 1)
                            copy_xt32(b + 1)
                        if q == 1:
                            copy_probT(b + 1)
                        if q == 3:
                            turn_hi(b + 1)

                pairs(act, b, body, gap)
                if b == 0:
                    split(FT - 1)
                for t in (FT - 2, FT - 1):
                    tile(t, t % 2, b, False)

        @block.vector
        def _(dve):
            links = [0]

            def link(ins):
                links[0] += 1
                ins.then_inc(chain, 1)
                dve.wait_ge(chain, links[0])

            def split(t):
                dve.wait_ge(split_hi, 2 * t + 2)
                for n, dst in enumerate((wg, wl)):
                    nc.vector.scalar_tensor_tensor(dst[:, 1, t].rearrange("p c q -> p (c q)"), raw[:, t % 2, n], WS,
                                                   dst[:, 0, t].rearrange("p c q -> p (c q)"), ALU.mult, ALU.subtract).then_inc(split_lo, 1)

            def mix(group):
                for t in range(4 * group, 4 * group + 4):
                    dve.wait_ge(mix_hi, t + 1)
                    nc.vector.scalar_tensor_tensor(wo[:, 1, t, :], bank_out[t % 4][:], MIX, wo[:, 0, t, :], ALU.mult, ALU.subtract)\
                        .then_inc(mix_lo, 1)

            def norm_of(n, b, ready, target):
                dve.wait_ge(ready, target)
                for i in range(LT):
                    ins = nc.vector.bn_stats(stat[:, i, :], xs[:, b % 2, i, :])
                link(ins)
                for i in range(LT):
                    ins = nc.vector.bn_aggr(mv[:, i, :], stat[:, i, :])
                link(ins)
                nc.vector.tensor_scalar_add(var_eps[:], mv[:, :, 1], EPS).then_inc(var_done, 1)
                dve.wait_ge(rstd_done, n + 1)
                if n:
                    use, of = (XT32 + 3, b) if n % 2 else (XT + 3, b - 1)
                    dve.wait_ge(filled[use % 2], USES * of + use // 2 + 1)
                for i in range(LT):
                    nc.vector.tensor_scalar(xn[:, i, :], xs[:, b % 2, i, :], mv[:, i, 0:1], rstd[:, i:i + 1],
                                            ALU.subtract, ALU.mult).then_inc(xn_done, 1)

            def attend(b):
                for i in range(LT):
                    dve.wait_ge(energy_done, LT * b + i + 1)
                    link(nc.vector.reduce_max(neg_max[:, i:i + 1], energy[:, i, :], AX_X))
                    nc.vector.tensor_scalar_mul(neg_max[:, i:i + 1], neg_max[:, i:i + 1], -1.0).then_inc(max_done, 1)
                for i in range(LT):
                    dve.wait_ge(exp_done, LT * b + i + 1)
                    link(nc.vector.reciprocal(inv[:, i:i + 1], total[:, i:i + 1]))
                    nc.vector.tensor_scalar_mul(prob[:, i, :], prob[:, i, :], inv[:, i:i + 1]).then_inc(prob_done, 1)

            def x3_of(b):
                for i in range(LT):
                    full(dve, PRODUCT + i, b)
                    nc.vector.scalar_tensor_tensor(xs[:, b % 2, i, :], bank(PRODUCT + i)[:], tanh_g[:, 0:1], xs[:, b % 2, i, :],
                                                   ALU.mult, ALU.add).then_inc(x3_done, 1)

            def turn_lo(b):
                for c in range(DT):
                    dve.wait_ge(xT_hi, DT * b + c + 1)
                    nc.vector.tensor_tensor(xt[:, b % 2, 1, c, :], bank(XT + c)[:], xt[:, b % 2, 0, c, :], ALU.subtract)\
                        .then_inc(xT_lo, 1)

            def tile(t, side, b, first):
                dve.wait_ge(silu_done, t + (FT * b + 1))
                dve.wait_ge(u_done, t + (FT * b + 1))
                nc.vector.scalar_tensor_tensor(hid[:, side, :], bank_u[:], 1.0 / WS, sg[:, side, :], ALU.mult, ALU.mult).then_inc(hid_done, 1)
                dve.wait_ge(hid_done, t + (FT * b + 1))
                if not first:
                    dve.wait_ge(down_done, t + (FT * b - 1))
                nc.vector.tensor_copy(h16[:, side, 0, :], hid[:, side, :]).then_inc(hi_done, 1)
                dve.wait_ge(hi_done, t + (FT * b + 1))
                nc.vector.tensor_tensor(h16[:, side, 1, :], hid[:, side, :], h16[:, side, 0, :], ALU.subtract).then_inc(h_done, 1)

            def out_of(b):
                dve.wait_ge(down_done, FT * (b + 1))
                for i in range(LT):
                    nc.vector.scalar_tensor_tensor(xs[:, b % 2, i, :], bank_out[i][:], scale_out[:], xs[:, b % 2, i, :],
                                                   ALU.mult, ALU.add).then_inc(out_done, 1)

            dve.wait_ge(tanh_done, 1)
            nc.vector.tensor_scalar_mul(scale_out[:], tanh_g[:, 1:2], 1.0 / WS)
            norm_of(0, 0, x_in[0], 16)
            attend(0)
            mix(0)
            mix(1)
            mix(2)
            x3_of(0)
            mix(3)
            split(0)
            norm_of(1, 0, x3_done, LT)
            turn_lo(0)
            for b in range(B):
                def body(j):
                    for k in (0, 1):
                        if b == 0:
                            split(2 * j + k + 1)
                        tile(j * 2 + k, k, b, b == 0 and isinstance(j, int) and j == 0)

                def gap(q):
                    if b + 1 < B:
                        if q == 0:
                            norm_of(2 * b + 2, b + 1, x_in[(b + 1) % 2], 16 * ((b + 1) // 2 + 1))
                            attend(b + 1)
                        if q == 1:
                            x3_of(b + 1)
                        if q == 2:
                            norm_of(2 * b + 3, b + 1, x3_done, LT * (b + 2))
                        if q == 3:
                            turn_lo(b + 1)

                pairs(dve, b, body, gap)
                if b == 0:
                    split(FT - 1)
                for t in (FT - 2, FT - 1):
                    tile(t, t % 2, b, False)
                out_of(b)

        @block.tensor
        def _(pe):
            def fill(mm, use):
                mm.then_inc(filled[use % 2], 1)

            def energies(b):
                pe.wait_ge(ctx_in, 16 * (b + 1))
                for use, weight in ((Q, w_q), (K, w_k)):
                    empty(pe, use, b)
                    for c in range(CT):
                        mm = nc.tensor.matmul(bank(use)[:], weight[:, c, :], ctxs[:, c, :], start=(c == 0), stop=(c == CT - 1))
                    fill(mm, use)
                pe.wait_ge(qk_done, 2 * (b + 1))
                for i in range(LT):
                    empty(pe, ENERGY + i, b)
                    fill(nc.tensor.matmul(bank(ENERGY + i)[:], qk[:, 0, i * P:(i + 1) * P], qk[:, 1, :], start=True, stop=True),
                         ENERGY + i)

            def turn_x(first, norm, b):
                pe.wait_ge(xn_done, LT * (norm + 1))
                for c in range(DT):
                    empty(pe, first + c, b)
                    for i in range(LT):
                        mm = nc.tensor.transpose(bank(first + c)[:, i * P:(i + 1) * P], xn[:, i, c * P:(c + 1) * P], ident[:])
                    fill(mm, first + c)

            def turn_prob(b):
                pe.wait_ge(prob_done, LT * (b + 1))
                for c in range(LT):
                    empty(pe, PROBT + c, b)
                    for i in range(LT):
                        mm = nc.tensor.transpose(bank(PROBT + c)[:, i * P:(i + 1) * P], prob[:, i, c * P:(c + 1) * P], ident[:])
                    fill(mm, PROBT + c)

            def product(b):
                pe.wait_ge(xt32_done, DT * (b + 1))
                pe.wait_ge(probT_done, LT * (b + 1))
                for i in range(LT):
                    empty(pe, PRODUCT + i, b)
                    for c in range(DT):
                        mm = nc.tensor.matmul(bank(PRODUCT + i)[:], xt32[:, c, i * P:(i + 1) * P], probT[:, c, :],
                                              start=(c == 0), stop=(c == DT - 1))
                    fill(mm, PRODUCT + i)

            def mix(group):
                for t in range(4 * group, 4 * group + 4):
                    pe.wait_ge(mix_in[t % 4], 16 * (t // 4 + 1))
                    if t >= 4:
                        pe.wait_ge(mix_lo, t - 3)
                    nc.tensor.matmul(bank_out[t % 4][:], hada[:], raw_mix[:, t % 4], start=True, stop=True).then_inc(mix_done, 1)

            def at(m, t):
                return m[:, t] if isinstance(t, int) else m[:, bass.ds(t, 1)].rearrange("p o n -> p (o n)")

            def tile_up(t, b, first=False):
                if b == 0:
                    pe.wait_ge(split_lo, 2 * (t + 1))
                if not first:
                    pe.wait_ge(hid_done, t + FT * b)
                for weight, dst, done in ((wg, bank_g, g_done), (wl, bank_u, u_done)):
                    n = 0
                    for c in range(DT):
                        for wh, xh in ((0, 0), (0, 1), (1, 0)):
                            mm = nc.tensor.matmul(dst[:], at(weight[:, wh, :, c, :], t), xt[:, b % 2, xh, c, :],
                                                  start=(n == 0), stop=(n == 3 * DT - 1))
                            n += 1
                    mm.then_inc(done, 1)

            def tile_down(t, side, b, first=False, last=False):
                pe.wait_ge(h_done, t + (FT * b + 1))
                for i in range(LT):
                    for n, (hh, wh) in enumerate(((0, 0), (0, 1), (1, 0))):
                        mm = nc.tensor.matmul(bank_out[i][:], h16[:, side, hh, i * P:(i + 1) * P], at(wo[:, wh], t),
                                              start=(first and n == 0), stop=(last and n == 2))
                mm.then_inc(down_done, 1)

            pe.wait_ge(consts, 16 * CONSTS)
            energies(0)
            mix(0)
            turn_x(XT32, 0, 0)
            mix(1)
            turn_prob(0)
            mix(2)
            product(0)
            mix(3)
            turn_x(XT, 1, 0)
            for b in range(B):
                def body(j):
                    first = isinstance(j, int) and j == 0
                    tile_up(j * 2 + 1, b)
                    if first:
                        if b:
                            pe.wait_ge(out_done, LT * b)
                        else:
                            pe.wait_ge(mix_lo, FT)
                    tile_down(j * 2, 0, b, first=first)
                    tile_up(j * 2 + 2, b)
                    tile_down(j * 2 + 1, 1, b)

                def gap(q):
                    if b + 1 < B:
                        if q == 0:
                            energies(b + 1)
                            turn_x(XT32, 2 * b + 2, b + 1)
                        if q == 1:
                            turn_prob(b + 1)
                            product(b + 1)
                        if q == 3:
                            turn_x(XT, 2 * b + 3, b + 1)

                pe.wait_ge(xT_lo, DT * (b + 1))
                tile_up(0, b, first=b == 0)
                pairs(pe, b, body, gap)
                tile_up(FT - 1, b)
                tile_down(FT - 2, 0, b)
                tile_down(FT - 1, 1, b, last=True)


def layout(a):
    import numpy as np

    def tiles(m, p=P):
        return np.ascontiguousarray(m.reshape(m.shape[0] // p, p, m.shape[1]).transpose(1, 0, 2))

    def col(v):
        return np.ascontiguousarray(v.reshape(-1, P).T)

    def zeros(*shape):
        return np.zeros(shape, np.float32)

    hadamard = np.array([[1.0]], np.float32)
    while hadamard.shape[0] < P:
        hadamard = np.block([[hadamard, hadamard], [hadamard, -hadamard]])
    xp = a["L0_xattn_x_proj_w"].T
    w_x = np.concatenate([xp[:, :DR], zeros(DI, DR), xp[:, DR:]], axis=1)
    up = [a["L0_ffn_w1"][e] for e in range(NE)] + [a["L0_ffn_shared_w1"]]
    down = [a["L0_ffn_w2"][e] for e in range(NE)] + [a["L0_ffn_shared_w2"]]
    up, down = np.concatenate(up, axis=1), np.concatenate(down, axis=0)
    pick = zeros(GR, GR, P)
    for e in range(GR):
        pick[e, e] = 1.0
    return {
        "x": a["x"], "g_xattn": a["g_xattn"], "g_ffn": a["g_ffn"],
        "ctx_t": np.ascontiguousarray(a["ctx_1024"].transpose(0, 2, 1)),
        "ident": np.eye(P, dtype=np.float32),
        "w_in": tiles(a["L0_xattn_in_proj_w"].T),
        "conv_w": np.ascontiguousarray(a["L0_xattn_conv_w"].T),
        "w_x": tiles(w_x),
        "w_dt": np.ascontiguousarray(a["L0_xattn_dt_proj_w"].T),
        "scan_cols": np.stack([col(a["L0_xattn_conv_b"]), col(a["L0_xattn_dt_proj_b"]), col(a["L0_xattn_D"])], axis=1),
        "a_log": tiles(a["L0_xattn_A_log"]),
        "gate_w": tiles(a["L0_ffn_gate_w"]).reshape(P, DT * NE),
        "w_up": np.ascontiguousarray(up.reshape(DT, P, HT, P).transpose(1, 2, 0, 3)).reshape(P, HT, DT * P),
        "w_down": np.ascontiguousarray(down.reshape(HT, P, D).transpose(1, 0, 2)),
        "b_up": col(np.concatenate([a["L0_ffn_b1"].reshape(-1), a["L0_ffn_shared_b1"]])),
        "b_down": np.concatenate([a["L0_ffn_b2"], a["L0_ffn_shared_b2"][None], zeros(1, D)]),
        "iota": np.tile(np.arange(NE, dtype=np.float32), (P, 1)),
        "pick": pick.reshape(GR, GR * P),
        "w_q": tiles(a["L1_xattn_Wq"].T), "w_k": tiles(a["L1_xattn_Wk"].T),
        "b_q": col(a["L1_xattn_bq"]), "b_k": col(a["L1_xattn_bk"]),
        "w_gate": np.ascontiguousarray(a["L1_ffn_W1"].T.reshape(DT, P, FT, P).transpose(1, 2, 0, 3)).reshape(P, FT, DT * P),
        "w_lin": np.ascontiguousarray(a["L1_ffn_W3"].T.reshape(DT, P, FT, P).transpose(1, 2, 0, 3)).reshape(P, FT, DT * P),
        "w_out": tiles(a["L1_ffn_W2"].T),
        "hadamard": hadamard,
    }


def program(nc, w, out):
    x1 = nc.dram_tensor("x1_scratch", [B, L, D], F32, kind="Internal").ap()
    x2 = nc.dram_tensor("x2_scratch", [B, L, D], F32, kind="Internal").ap()
    b_rows = nc.dram_tensor("b_rows_scratch", [B, NS, L], F32, kind="Internal").ap()
    w_mix = nc.dram_tensor("w_mix_scratch", [P, FT, D], F32, kind="Internal").ap()
    scan_block(nc, w, w["x"], w["ctx_t"], x1, b_rows)
    moe_block(nc, w, x1, x2, w_mix)
    ffn_block(nc, w, w["ctx_t"], x2, w_mix, out)


def kernel(**inputs):
    import numpy as np
    import concourse.bacc as bacc
    from concourse.bass_utils import run_bass_kernel_spmd

    nc = bacc.Bacc("TRN2", target_bir_lowering=False, num_devices=1)
    arrays = {name: np.ascontiguousarray(a) for name, a in layout({k: np.asarray(v) for k, v in inputs.items()}).items()}
    w = {name: nc.dram_tensor(name, a.shape, mybir.dt.from_np(a.dtype), kind="ExternalInput").ap() for name, a in arrays.items()}
    out = nc.dram_tensor("out", [B, L, D], F32, kind="ExternalOutput").ap()
    program(nc, w, out)
    result = run_bass_kernel_spmd(nc, [arrays], core_ids=[0])
    return result.results[0]["out"]
```

```python
from contextlib import ExitStack

import concourse.bass as bass
from concourse import mybir

F32 = mybir.dt.float32
F16 = mybir.dt.float16
U32 = mybir.dt.uint32
ALU = mybir.AluOpType
ACT = mybir.ActivationFunctionType
AX_X = mybir.AxisListType.X

P = 128
B, L, D = 4, 512, 512
C = 256
DI, NS, DR, TAPS = 512, 16, 16, 4
NE, HE, SH = 8, 256, 512
H = 2048
ET, LT, DT, CT = DI // P, L // P, D // P, C // P
HT = (NE * HE + SH) // P
GR = HT // 2
FT = H // P
TT = B * LT
RT = 2 * TT + NE - 1
WS = 64.0
EPS = 1e-5
SLOTS = 8


def scan_block(nc, w, x, ctx_t, x1, b_rows):
    SCANS, ADDS = NS * ET, (NS + 1) * LT
    GAPS = (2, 10, 12, 14, NS)
    CONV = 8
    with ExitStack() as stack:
        def sb(name, shape, dt=F32):
            return stack.enter_context(nc.sbuf_tensor("s_" + name, shape, dt))

        def sem(name):
            return stack.enter_context(nc.semaphore("scan_" + name))

        ident = sb("ident", [P, P])
        gates = sb("gates", [P, 4])
        tanh_g = sb("tanh_g", [P, 4])
        w_tap = sb("w_tap", [P, TAPS, CT, DI])
        w_x = sb("w_x", [P, ET, 64])
        w_dt = sb("w_dt", [DR, DI])
        cols = sb("cols", [P, 3, ET])
        a_log = sb("a_log", [P, ET, NS])
        a_exp = sb("a_exp", [P, ET, NS])
        a_neg = sb("a_neg", [P, ET, NS])
        half = sb("half", [P, LT])
        ctx_pad = sb("ctx_pad", [P, CT, TAPS - 1 + L])
        xs = sb("xs", [P, 2, LT, D])
        xn = sb("xn", [P, LT, D])
        stat = sb("stat", [P, LT, 6])
        mv = sb("mv", [P, LT, 2])
        var_eps = sb("var_eps", [P, LT])
        rstd = sb("rstd", [P, LT])
        sz = sb("sz", [P, LT, DI])
        u = sb("u", [P, ET, L])
        proj = sb("proj", [64, L])
        b_all = sb("b_all", [P, NS, L])
        c_col = sb("c_col", [P, 2, LT, 64])
        sp_y = sb("sp_y", [P, ET, L])
        sp_l = sb("sp_l", [P, ET, L])
        sp_r = sb("sp_r", [P, ET, L])
        delta = sb("delta", [P, ET, L])
        du = sb("du", [P, ET, L])
        decay = sb("decay", [P, 2, ET, L])
        drive = sb("drive", [P, 2, ET, L])
        state = sb("state", [P, 2, ET, L])
        acc = sb("acc", [P, LT, DI])
        work = [stack.enter_context(nc.psum_tensor(f"scan_work{i}", [P, 512], F32)) for i in range(4)]
        turned = [stack.enter_context(nc.psum_tensor(f"scan_turned{i}", [P, 512], F32)) for i in range(4)]
        w_in = sp_y[:, 0:CT, :]
        tap_rows = sp_l

        consts = sem("consts")
        pad_zero = sem("pad_zero")
        half_set = sem("half_set")
        taps_done = sem("taps_done")
        a_done = sem("a_done")
        tanh_done = sem("tanh_done")
        ctx_in = sem("ctx_in")
        x_in = [sem("x_in_even"), sem("x_in_odd")]
        stat_done = sem("stat_done")
        mv_done = sem("mv_done")
        var_done = sem("var_done")
        rstd_done = sem("rstd_done")
        xn_done = sem("xn_done")
        conv_done = sem("conv_done")
        u_done = sem("u_done")
        xproj_done = sem("xproj_done")
        proj_done = sem("proj_done")
        rows_out = sem("rows_out")
        rows_in = [sem(f"rows_in{q}") for q in range(len(GAPS))]
        cT_done = sem("cT_done")
        c_done = sem("c_done")
        dt_done = sem("dt_done")
        relu_done = sem("relu_done")
        exp_done = sem("exp_done")
        ln_done = sem("ln_done")
        soft = sem("soft")
        sum_done = sem("sum_done")
        delta_done = sem("delta_done")
        du_done = sem("du_done")
        skip_done = sem("skip_done")
        zT_done = sem("zT_done")
        sz_done = sem("sz_done")
        decay_done = sem("decay_done")
        drive_done = sem("drive_done")
        scan_done = sem("scan_done")
        half_free = sem("half_free")
        turned_done = sem("turned_done")
        add_done = sem("add_done")
        mul_done = sem("mul_done")
        x1_done = sem("x1_done")
        x1_out = [sem("x1_out_even"), sem("x1_out_odd")]
        CONSTS = 9
        block = stack.enter_context(nc.Block())

        def segments(eng, b, step, gap):
            lo = 0
            for q, hi in enumerate(GAPS):
                if q == 0:
                    for n in range(lo, hi):
                        step(n, n % 2)
                else:
                    with eng.Fori(lo // 2, hi // 2) as pair:
                        for k in (0, 1):
                            step(pair * 2 + k, k)
                lo = hi
                gap(q)

        @block.sync
        def _(sp):
            sp.dma_start(w_in, w["w_in"]).then_inc(consts, 16)
            sp.dma_start(tap_rows[:], w["conv_w"].partition_broadcast(P)).then_inc(consts, 16)
            for dst, src in ((ident[:], "ident"), (w_x[:], "w_x"), (w_dt[:], "w_dt"), (cols[:], "scan_cols"),
                             (a_log[:], "a_log")):
                sp.dma_start(dst, w[src]).then_inc(consts, 16)
            sp.dma_start(gates[:, 0:2], w["g_xattn"].partition_broadcast(P)).then_inc(consts, 16)
            sp.dma_start(gates[:, 2:4], w["g_ffn"].partition_broadcast(P)).then_inc(consts, 16)

            def load(b):
                if b:
                    sp.wait_ge(conv_done, ET * b)
                sp.dma_start(ctx_pad[:, :, TAPS - 1:], ctx_t[b].rearrange("(c p) l -> p c l", p=P)).then_inc(ctx_in, 16)
                if b >= 2:
                    sp.wait_ge(x1_out[b % 2], 16 * (b // 2))
                sp.dma_start(xs[:, b % 2], x[b].rearrange("(t p) d -> p t d", p=P)).then_inc(x_in[b % 2], 16)

            def spread_b(b):
                sp.wait_ge(proj_done, b + 1)
                sp.dma_start(b_rows[b], proj[32:48, :]).then_inc(rows_out, 16)
                sp.wait_ge(rows_out, 16 * (b + 1))
                lo = 0
                for q, hi in enumerate(GAPS):
                    if b:
                        sp.wait_ge(drive_done, SCANS * (b - 1) + ET * hi)
                    sp.dma_start(b_all[:, lo:hi, :], b_rows[b, lo:hi, :].partition_broadcast(P)).then_inc(rows_in[q], 16)
                    lo = hi

            load(0)
            spread_b(0)
            for b in range(B):
                if b + 1 < B:
                    load(b + 1)
                    spread_b(b + 1)
                sp.wait_ge(x1_done, LT * (b + 1))
                sp.dma_start(x1[b].rearrange("(t p) d -> p t d", p=P), xs[:, b % 2]).then_inc(x1_out[b % 2], 16)
            sp.wait_ge(x1_out[0], 16 * (B // 2))
            sp.wait_ge(x1_out[1], 16 * (B // 2))

        @block.gpsimd
        def _(pool):
            nc.gpsimd.memset(ctx_pad[:, :, 0:TAPS - 1], 0.0).then_inc(pad_zero, 1)
            nc.gpsimd.memset(half[:], -0.5).then_inc(half_set, 1)
            pool.wait_ge(half_set, 1)

            def rstd_of(b):
                pool.wait_ge(var_done, b + 1)
                nc.gpsimd.tensor_tensor(rstd[:], var_eps[:], half[:], ALU.pow).then_inc(rstd_done, 1)

            def sum_of(b):
                pool.wait_ge(ln_done, b + 1)
                for e in range(ET):
                    nc.gpsimd.tensor_tensor(sp_r[:, e, :], sp_r[:, e, :], sp_l[:, e, :], ALU.add).then_inc(sum_done, 1)

            def du_of(b):
                for e in range(ET):
                    pool.wait_ge(delta_done, ET * b + e + 1)
                    nc.gpsimd.tensor_tensor(du[:, e, :], delta[:, e, :], u[:, e, :], ALU.mult).then_inc(du_done, 1)
                pool.wait_ge(du_done, ET * (b + 1))

            rstd_of(0)
            sum_of(0)
            du_of(0)
            for b in range(B):
                def step(n, half_of):
                    row = b_all[:, n, :] if isinstance(n, int) else \
                        b_all[:, bass.ds(n, 1), :].rearrange("p o l -> p (o l)")
                    for e in range(ET):
                        if b or not isinstance(n, int) or n >= 2:
                            pool.wait_ge(scan_done, n * ET + (SCANS * b - 2 * ET + e + 1))
                            pool.sem_inc(half_free, 1)
                        nc.gpsimd.tensor_tensor(drive[:, half_of, e, :], du[:, e, :], row, ALU.mult)\
                            .then_inc(drive_done, 1)

                def gap(q):
                    if q + 1 < len(GAPS):
                        pool.wait_ge(rows_in[q + 1], 16 * (b + 1))
                    if b + 1 < B and q == 1:
                        rstd_of(b + 1)
                    if b + 1 < B and q == 4:
                        sum_of(b + 1)
                        du_of(b + 1)

                pool.wait_ge(rows_in[0], 16 * (b + 1))
                segments(pool, b, step, gap)

        @block.scalar
        def _(act):
            act.wait_ge(consts, 16 * CONSTS)
            nc.scalar.activation(tanh_g[:], gates[:], ACT.Tanh).then_inc(tanh_done, 1)
            nc.scalar.activation(a_exp[:], a_log[:], ACT.Exp).then_inc(a_done, 1)
            act.wait_ge(a_done, 1)
            nc.scalar.mul(a_neg[:], a_exp[:], -1.0).then_inc(a_done, 1)
            act.wait_ge(a_done, 2)

            def u_of(b):
                if b:
                    act.wait_ge(du_done, ET * b)
                    act.wait_ge(turned_done, ADDS * (b - 1) + LT)
                for e in range(ET):
                    act.wait_ge(conv_done, ET * b + e + 1)
                    nc.scalar.activation(u[:, e, :], work[e][:], ACT.Silu, bias=cols[:, 0, e:e + 1]).then_inc(u_done, 1)

            def proj_of(b):
                act.wait_ge(xproj_done, b + 1)
                if b:
                    act.wait_ge(rows_out, 16 * b)
                    act.wait_ge(dt_done, ET * b)
                    act.wait_ge(cT_done, b)
                nc.scalar.activation(proj[:], work[0][0:64, :], ACT.Copy).then_inc(proj_done, 1)

            def relu_of(b):
                act.wait_ge(cT_done, b + 1)
                nc.scalar.activation(c_col[:, b % 2], work[1][:, 0:LT * 64].rearrange("p (t c) -> p t c", t=LT), ACT.Copy)\
                    .then_inc(c_done, 1)
                if b:
                    act.wait_ge(turned_done, ADDS * (b - 1) + LT)
                    act.wait_ge(delta_done, ET * b)
                for e in range(ET):
                    act.wait_ge(dt_done, ET * b + e + 1)
                    bank = work[(e + 2) % 4]
                    nc.scalar.activation(sp_y[:, e, :], bank[:], ACT.Abs, bias=cols[:, 1, e:e + 1]).then_inc(relu_done, 1)
                    nc.scalar.activation(sp_r[:, e, :], bank[:], ACT.Relu, bias=cols[:, 1, e:e + 1]).then_inc(relu_done, 1)

            def ln_of(b):
                act.wait_ge(relu_done, 2 * ET * (b + 1))
                nc.scalar.activation(sp_y[:], sp_y[:], ACT.Exp, scale=-1.0).then_inc(exp_done, 1)
                act.wait_ge(exp_done, b + 1)
                nc.scalar.activation(sp_l[:], sp_y[:], ACT.Ln, bias=1.0).then_inc(ln_done, 1)

            def skip_of(b):
                act.wait_ge(soft, 2 * ET * b + 2 * ET)
                act.wait_ge(u_done, ET * (b + 1))
                for e in range(ET):
                    nc.scalar.activation(sp_y[:, e, :], u[:, e, :], ACT.Copy, scale=cols[:, 2, e:e + 1])\
                        .then_inc(skip_done, 1)

            def sz_of(b):
                if b:
                    act.wait_ge(mul_done, LT * b)
                for j in range(LT):
                    act.wait_ge(zT_done, LT * b + j + 1)
                    nc.scalar.activation(sz[:, j, :], work[j][:], ACT.Silu).then_inc(sz_done, 1)

            act.wait_ge(taps_done, TAPS * CT)
            u_of(0)
            proj_of(0)
            relu_of(0)
            ln_of(0)
            skip_of(0)
            for b in range(B):
                def step(n, half_of):
                    for e in range(ET):
                        scale = a_neg[:, e, n:n + 1] if isinstance(n, int) else a_neg[:, e, bass.ds(n, 1)]
                        if b or not isinstance(n, int) or n >= 2:
                            act.wait_ge(scan_done, n * ET + (SCANS * b - 2 * ET + e + 1))
                        nc.scalar.activation(decay[:, half_of, e, :], delta[:, e, :], ACT.Exp, scale=scale)\
                            .then_inc(decay_done, 1)

                def gap(q):
                    if q == 0:
                        sz_of(b)
                    if b + 1 < B:
                        if q == 1:
                            u_of(b + 1)
                        if q == 2:
                            proj_of(b + 1)
                        if q == 3:
                            relu_of(b + 1)
                            ln_of(b + 1)
                        if q == 4:
                            skip_of(b + 1)

                act.wait_ge(delta_done, ET * (b + 1))
                segments(act, b, step, gap)

        @block.vector
        def _(dve):
            dve.wait_ge(consts, 16 * CONSTS)
            for k in range(TAPS):
                for c in range(CT):
                    nc.vector.tensor_tensor(w_tap[:, k, c, :], w_in[:, c, :], tap_rows[:, k, :], ALU.mult).then_inc(taps_done, 1)
            dve.wait_ge(tanh_done, 1)

            def stats_of(b):
                dve.wait_ge(x_in[b % 2], 16 * (b // 2 + 1))
                if b:
                    dve.wait_ge(xn_done, LT * b)
                for i in range(LT):
                    nc.vector.bn_stats(stat[:, i, :], xs[:, b % 2, i, :]).then_inc(stat_done, 1)
                for i in range(LT):
                    dve.wait_ge(stat_done, LT * b + i + 1)
                    nc.vector.bn_aggr(mv[:, i, :], stat[:, i, :]).then_inc(mv_done, 1)
                dve.wait_ge(mv_done, LT * (b + 1))
                nc.vector.tensor_scalar_add(var_eps[:], mv[:, :, 1], EPS).then_inc(var_done, 1)

            def norm_of(b):
                dve.wait_ge(rstd_done, b + 1)
                if b:
                    dve.wait_ge(zT_done, LT * b)
                for i in range(LT):
                    nc.vector.tensor_scalar(xn[:, i, :], xs[:, b % 2, i, :], mv[:, i, 0:1], rstd[:, i:i + 1],
                                            ALU.subtract, ALU.mult).then_inc(xn_done, 1)

            def delta_of(b):
                dve.wait_ge(ln_done, b + 1)
                base = 2 * ET * b
                for e in range(ET):
                    nc.vector.tensor_scalar(delta[:, e, :], sp_y[:, e, :], 1.0, 1.0, ALU.add, ALU.subtract).then_inc(soft, 1)
                for e in range(ET):
                    dve.wait_ge(soft, base + e + 1)
                    nc.vector.tensor_tensor(delta[:, e, :], sp_y[:, e, :], delta[:, e, :], ALU.subtract).then_inc(soft, 1)
                for e in range(ET):
                    dve.wait_ge(soft, base + ET + e + 1)
                    dve.wait_ge(sum_done, ET * b + e + 1)
                    nc.vector.tensor_tensor(delta[:, e, :], sp_r[:, e, :], delta[:, e, :], ALU.add).then_inc(delta_done, 1)

            def x1_of(b):
                dve.wait_ge(sz_done, LT * (b + 1))
                for i in range(LT):
                    dve.wait_ge(add_done, ADDS * b + LT * NS + i + 1)
                    nc.vector.tensor_tensor(acc[:, i, :], acc[:, i, :], sz[:, i, :], ALU.mult).then_inc(mul_done, 1)
                for i in range(LT):
                    dve.wait_ge(mul_done, LT * b + i + 1)
                    nc.vector.scalar_tensor_tensor(xs[:, b % 2, i, :], acc[:, i, :], tanh_g[:, 0:1], xs[:, b % 2, i, :],
                                                   ALU.mult, ALU.add).then_inc(x1_done, 1)

            stats_of(0)
            norm_of(0)
            delta_of(0)
            for b in range(B):
                def adds(n):
                    for i in range(LT):
                        dve.wait_ge(turned_done, (n + 1) * LT + (ADDS * b + i + 1))
                        if isinstance(n, int) and n < 0:
                            if b:
                                dve.wait_ge(x1_done, LT * b)
                            nc.vector.tensor_copy(acc[:, i, :], turned[i][:]).then_inc(add_done, 1)
                        else:
                            col = c_col[:, b % 2, i, 48 + n:49 + n] if isinstance(n, int) else \
                                c_col[:, b % 2, i, bass.ds(n + 48, 1)]
                            dve.wait_ge(add_done, n * LT + (ADDS * b + i + 1))
                            nc.vector.scalar_tensor_tensor(acc[:, i, :], turned[i][:], col, acc[:, i, :],
                                                           ALU.mult, ALU.add).then_inc(add_done, 1)

                def step(n, half_of):
                    if isinstance(n, int) and n < 2:
                        if b:
                            dve.wait_ge(turned_done, ADDS * b - LT + LT * n)
                    else:
                        dve.wait_ge(turned_done, n * LT + ADDS * b)
                    for e in range(ET):
                        dve.wait_ge(decay_done, n * ET + (SCANS * b + e + 1))
                        dve.wait_ge(drive_done, n * ET + (SCANS * b + e + 1))
                        nc.vector.tensor_tensor_scan(state[:, half_of, e, :], decay[:, half_of, e, :],
                                                     drive[:, half_of, e, :], 0.0, ALU.mult, ALU.add).then_inc(scan_done, 1)
                    adds(n - 1)

                def gap(q):
                    if q == 4:
                        adds(NS - 1)
                        if b + 1 < B:
                            delta_of(b + 1)
                        x1_of(b)
                    if b + 1 < B:
                        if q == 0:
                            stats_of(b + 1)
                        if q == 2:
                            norm_of(b + 1)

                if b == 0:
                    dve.wait_ge(c_done, 1)
                else:
                    dve.wait_ge(c_done, b + 1)
                segments(dve, b, step, gap)

        @block.tensor
        def _(pe):
            pe.wait_ge(consts, 16 * CONSTS)
            pe.wait_ge(pad_zero, 1)
            pe.wait_ge(taps_done, TAPS * CT)

            def conv_of(b, part):
                if part == 0:
                    pe.wait_ge(ctx_in, 16 * (b + 1))
                share = ET * TAPS // CONV
                for n in range(part * share, (part + 1) * share):
                    e, k = n // TAPS, n % TAPS
                    if b and k == 0:
                        pe.wait_ge(sz_done, LT * (b - 1) + e + 1)
                    for c in range(CT):
                        mm = nc.tensor.matmul(work[e][:], w_tap[:, k, c, e * P:(e + 1) * P], ctx_pad[:, c, k:k + L],
                                              start=(k == 0 and c == 0), stop=(k == TAPS - 1 and c == CT - 1))
                    if k == TAPS - 1:
                        mm.then_inc(conv_done, 1)

            def xproj_of(b):
                for e in range(ET):
                    pe.wait_ge(u_done, ET * b + e + 1)
                    mm = nc.tensor.matmul(work[0][0:64, :], w_x[:, e, :], u[:, e, :], start=(e == 0), stop=(e == ET - 1))
                mm.then_inc(xproj_done, 1)

            def turn_proj(b):
                pe.wait_ge(proj_done, b + 1)
                for i in range(LT):
                    mm = nc.tensor.transpose(work[1][:, i * 64:(i + 1) * 64], proj[:, i * P:(i + 1) * P], ident[0:64, 0:64])
                mm.then_inc(cT_done, 1)
                for e in range(ET):
                    if e == 3:
                        pe.wait_ge(c_done, b + 1)
                    mm = nc.tensor.matmul(work[(e + 2) % 4][:], w_dt[:, e * P:(e + 1) * P], proj[0:DR, :], start=True, stop=True)
                    mm.then_inc(dt_done, 1)

            def turn_z(b):
                for j in range(LT):
                    pe.wait_ge(relu_done, 2 * ET * (b + 1))
                    pe.wait_ge(xn_done, LT * (b + 1))
                    for i in range(LT):
                        mm = nc.tensor.transpose(work[j][:, i * P:(i + 1) * P], xn[:, i, j * P:(j + 1) * P], ident[:])
                    mm.then_inc(zT_done, 1)

            def turn(src, n, b):
                for i in range(LT):
                    if b or not (isinstance(n, int) and n < 0):
                        pe.wait_ge(add_done, n * LT + (ADDS * b + i + 1))
                    for e in range(ET):
                        mm = nc.tensor.transpose(turned[i][:, e * P:(e + 1) * P], src(e)[:, i * P:(i + 1) * P], ident[:])
                    mm.then_inc(turned_done, 1)

            for part in range(CONV):
                conv_of(0, part)
            xproj_of(0)
            turn_proj(0)
            for b in range(B):
                pe.wait_ge(skip_done, ET * (b + 1))
                turn(lambda e: sp_y[:, e, :], -1, b)
                for n in range(NS):
                    pe.wait_ge(scan_done, SCANS * b + ET * (n + 1))
                    turn(lambda e: state[:, n % 2, e, :], n, b)
                    if n == 0:
                        turn_z(b)
                    if b + 1 < B:
                        if n < CONV:
                            conv_of(b + 1, n)
                        if n == 9:
                            xproj_of(b + 1)
                        if n == 11:
                            turn_proj(b + 1)


def moe_block(nc, w, x1, x1s, xn_rows, expert_out, token_table, routes, scales, w_mix):
    ORDER = [NE, NE + 1] + list(range(NE))
    SPLIT_AT = {2: 2, 5: 3, 9: 4, 10: 5, 11: 6, 12: 7, 13: 8, 14: 9}
    TURN_AFTER = {0: 1, 3: 2, 6: 3}
    LOGITS_AFTER = {1: 1, 4: 2, 7: 3}
    RANK_AFTER = 8
    ST = SH // P
    SHARED = B * ST
    USES = DT + 1
    RANK_USE, TABLE_USE, ROWS_USE = USES * B, USES * B + 1, USES * B + 2
    MIXC = D // 8
    with ExitStack() as stack:
        def sb(name, shape, dt=F32):
            return stack.enter_context(nc.sbuf_tensor("m_" + name, shape, dt))

        def sem(name):
            return stack.enter_context(nc.semaphore("moe_" + name))

        ident = sb("ident", [P, P])
        lower = sb("lower", [P, P])
        gates = sb("gates", [P, 2])
        tanh_g = sb("tanh_g", [P, 2])
        scale_out = sb("scale_out", [P, 1])
        expert_no = sb("expert_no", [P, NE, TT])
        thresholds = sb("thresholds", [P, TT])
        tile_no = sb("tile_no", [P, RT])
        token_no = sb("token_no", [P, TT])
        half = sb("half", [P, TT])
        b_up = sb("b_up", [P, HT])
        pick16 = sb("pick16", [GR, GR * P], F16)
        small = sb("small", [P, DT * NE])
        b_down = sb("b_down", [GR, D])
        gw = sb("gw", [P, 2, DT * NE], F16)
        bd = sb("bd", [GR, 2, D], F16)
        lower16 = sb("lower16", [P, P], F16)
        ones16 = sb("ones16", [P, P], F16)
        raw_up = sb("raw_up", [P, 2, 2, DT * P])
        raw_dn = sb("raw_dn", [P, 2, 2, D])
        up = sb("up", [P, 2, HT, DT, P], F16)
        dn = sb("dn", [P, 2, HT, D], F16)
        xs = sb("xs", [P, B, LT, D])
        xn = sb("xn", [P, 2, LT, D])
        pick = xn[0:GR, 1].rearrange("p t d -> p (t d)")[:, 0:GR * P]
        stat = sb("stat", [P, TT, 6])
        mv = sb("mv", [P, TT, 2])
        var_eps = sb("var_eps", [P, TT])
        rstd = sb("rstd", [P, TT])
        xt = sb("xt", [P, 3, 2, DT, L], F16)
        logit = sb("logit", [P, TT, NE])
        top = sb("top", [P, TT, 8])
        top_at = sb("top_at", [P, TT, 8], U32)
        at = sb("at", [P, TT, 2])
        diff = sb("diff", [P, TT])
        e1 = sb("e1", [P, TT])
        ge = sb("ge", [P, 3, TT])
        scaled = sb("scaled", [P, 2, TT])
        chosen = sb("chosen", [P, 2, NE, TT])
        member = sb("member", [P, NE, TT])
        member16 = sb("member16", [P, NE, TT], F16)
        restart = sb("restart", [P, NE, TT])
        upto = sb("upto", [P, NE, TT])
        upto16 = sb("upto16", [P, NE, TT], F16)
        rank = sb("rank", [P, NE, TT])
        count = sb("count", [P, NE])
        filled = sb("filled", [P, NE, TT])
        tiles = sb("tiles", [P, NE])
        ends = sb("ends", [P, NE])
        base = sb("base", [P, NE])
        place = sb("place", [P, 2, NE, TT])
        where = sb("where", [P, 2, TT])
        where_u = sb("where_u", [P, 2, TT], U32)
        passed = sb("passed", [P, RT, NE])
        owner = sb("owner", [P, RT])
        owner_u = sb("owner_u", [P, RT], U32)
        no_token = sb("no_token", [RT, P])
        table = sb("table", [RT, P])
        table_u = sb("table_u", [P, RT], U32)
        hid = sb("hid", [P, 2, L])
        h16 = sb("h16", [P, 2, 2, L], F16)
        mix = sb("mix", [P, 2, FT, MIXC])
        bank_up = [stack.enter_context(nc.psum_tensor(f"moe_up{i}", [P, 512], F32)) for i in range(2)]
        prep = [stack.enter_context(nc.psum_tensor(f"moe_prep{i}", [P, 512], F32)) for i in range(2)]
        bank_out = [stack.enter_context(nc.psum_tensor(f"moe_out{i}", [P, 512], F32)) for i in range(LT)]

        consts = sem("consts")
        x_in = [sem(f"x_in{b}") for b in range(B)]
        raw_in = [sem("raw_in_even"), sem("raw_in_odd")]
        split_hi = sem("split_hi")
        split_lo = sem("split_lo")
        small_hi = sem("small_hi")
        small_lo = sem("small_lo")
        filled_in = sem("filled_in")
        zeroed = sem("zeroed")
        tanh_done = sem("tanh_done")
        var_done = sem("var_done")
        rstd_done = sem("rstd_done")
        xn_done = sem("xn_done")
        xn_sent = [sem("xn_sent_even"), sem("xn_sent_odd")]
        xT_done = sem("xT_done")
        xT_hi = sem("xT_hi")
        prep_read = sem("prep_read")
        logit_done = sem("logit_done")
        diff_done = sem("diff_done")
        e1_done = sem("e1_done")
        member_done = sem("member_done")
        rank_done = sem("rank_done")
        where_done = sem("where_done")
        owner_done = sem("owner_done")
        scaled_done = sem("scaled_done")
        routes_out = sem("routes_out")
        scattered = sem("scattered")
        table_in = sem("table_in")
        table_turned = sem("table_turned")
        table_done = sem("table_done")
        up_done = sem("up_done")
        gelu_done = sem("gelu_done")
        hi_done = sem("hi_done")
        h_done = sem("h_done")
        down_done = sem("down_done")
        x1s_done = sem("x1s_done")
        x1s_out = sem("x1s_out")
        rows_in = [sem("rows_in_even"), sem("rows_in_odd")]
        rows_turned = sem("rows_turned")
        rows_hi = sem("rows_hi")
        e_up = sem("e_up")
        e_gelu = sem("e_gelu")
        e_hi = sem("e_hi")
        e_lo = sem("e_lo")
        e_down = sem("e_down")
        out_free = sem("out_free")
        y_free = [sem("y_free_even"), sem("y_free_odd")]
        chain = sem("chain")
        mix_in = sem("mix_in")
        mixed = sem("mixed")
        mix_out = sem("mix_out")
        CONSTS = 12
        block = stack.enter_context(nc.Block())

        def over(ap, axis, shape):
            return ap.unsqueeze(axis).broadcast_to(shape)

        def experts(engine, cells):
            return nc.values_load_multi_w_load_instructions(
                cells, engines=[engine], min_val=0, max_val=NE,
                skip_runtime_bounds_check_because="an expert's number is a sum of NE comparisons, each zero or one")[1]

        def tiles_of(eng, body):
            body(0, 0, 0)
            body(1, 1, 0)
            with eng.Fori(1, (RT - 1) // 2) as i:
                body(i * 2, 0, i)
                body(i * 2 + 1, 1, i)
            body(RT - 1, 0, (RT - 1) // 2)

        @block.sync
        def _(sp):
            def raw(k):
                j = ORDER[k]
                if k >= 2:
                    sp.wait_ge(split_hi, 2 * (k - 1))
                    sp.wait_ge(split_lo, 2 * (k - 1))
                sp.dma_start(raw_up[:, k % 2], w["w_up"][:, 2 * j:2 * j + 2, :]).then_inc(raw_in[k % 2], 16)
                sp.dma_start(raw_dn[:, k % 2], w["w_down"][:, 2 * j:2 * j + 2, :]).then_inc(raw_in[k % 2], 16)

            def send_xn(b):
                sp.wait_ge(xn_done, LT * (b + 1))
                sp.dma_start(xn_rows[b * L:(b + 1) * L].rearrange("(t p) d -> p t d", p=P), xn[:, b % 2])\
                    .then_inc(xn_sent[b % 2], 16)

            def send_x1s(b):
                sp.wait_ge(x1s_done, LT * (b + 1))
                sp.dma_start(x1s[b].rearrange("(t p) d -> p t d", p=P), xs[:, b]).then_inc(x1s_out, 16)

            sp.dma_start(xs[:, 0], x1[0].rearrange("(t p) d -> p t d", p=P)).then_inc(x_in[0], 16)
            for dst, src in ((ident, "ident"), (small, "gate_w"), (b_up, "b_up"), (pick, "pick"), (b_down, "b_down"),
                             (lower, "lower"), (expert_no, "expert_no"), (thresholds, "thresholds"), (tile_no, "tile_no"),
                             (token_no, "token_no")):
                sp.dma_start(dst if src == "pick" else dst[:], w[src]).then_inc(consts, 16)
            sp.dma_start(gates[:, 0:1], w["g_ffn"][0:1].partition_broadcast(P)).then_inc(consts, 16)
            sp.dma_start(gates[:, 1:2], w["g_ffn"][1:2].partition_broadcast(P)).then_inc(consts, 16)
            raw(0)
            raw(1)
            for b in range(1, B):
                sp.dma_start(xs[:, b], x1[b].rearrange("(t p) d -> p t d", p=P)).then_inc(x_in[b], 16)
            sp.wait_ge(filled_in, 4)
            sp.dma_start(token_table.rearrange("(t p) o -> t (p o)", p=P), no_token[:]).then_inc(zeroed, 16)
            send_xn(0)
            send_xn(1)
            raw(2)
            raw(3)
            for g in range(SHARED):
                if g + 1 in TURN_AFTER and g:
                    send_xn(TURN_AFTER[g + 1])
                if g in SPLIT_AT and SPLIT_AT[g] + 2 < len(ORDER):
                    raw(SPLIT_AT[g] + 2)
                if g % ST == 0 and g:
                    send_x1s(g // ST - 1)
            sp.wait_ge(where_done, 1)
            sp.dma_start(routes, where_u[:]).then_inc(routes_out, 16)
            sp.wait_ge(scaled_done, 1)
            sp.dma_start(scales, scaled[:]).then_inc(routes_out, 16)
            sp.wait_ge(scattered, 16 * 2 * TT)
            sp.dma_start(table[:], token_table.rearrange("(t p) o -> t (p o)", p=P)).then_inc(table_in, 16)
            send_x1s(B - 1)

            def send_y(t, side, n):
                sp.wait_ge(out_free, t + 3)
                at_tile = expert_out[t] if isinstance(t, int) else expert_out[bass.ds(t, 1)].rearrange("o p d -> (o p) d")
                sp.dma_start(at_tile, xs[:, 0, side, :]).then_inc(y_free[side], 16)

            sp.wait_ge(x1s_out, 16 * B)
            sp.sem_inc(y_free[0], 16)
            sp.sem_inc(y_free[1], 16)
            tiles_of(sp, send_y)
            sp.wait_ge(y_free[0], 16 * ((RT + 1) // 2) + 16)
            sp.wait_ge(y_free[1], 16 * (RT // 2) + 16)
            sp.wait_ge(routes_out, 32)

        @block.gpsimd
        def _(pool):
            STAGES = 4
            GROUPS = D // MIXC

            def load_mix(c):
                if c:
                    pool.wait_ge(mixed, 2 * STAGES * c)
                pool.dma_start(mix[:, c % 2], w["w_out"][:, :, c * MIXC:(c + 1) * MIXC]).then_inc(mix_in, 16)

            def mix_stage(c, stage):
                if stage == 0:
                    pool.wait_ge(mix_in, 16 * (c + 1))
                    if c:
                        pool.wait_ge(mix_out, 16 * c)
                else:
                    pool.wait_ge(mixed, 2 * (STAGES * c + stage))
                span, side = 1 << stage, (c + stage) % 2
                src = mix[:, side].rearrange("p (g two s) d -> p g two (s d)", two=2, s=span)
                dst = mix[:, 1 - side].rearrange("p (g two s) d -> p g two (s d)", two=2, s=span)
                for half_of, op in ((0, ALU.add), (1, ALU.subtract)):
                    nc.gpsimd.tensor_tensor(dst[:, :, half_of, :], src[:, :, 0, :], src[:, :, 1, :], op).then_inc(mixed, 1)

            def store_mix(c):
                pool.wait_ge(mixed, 2 * STAGES * (c + 1))
                pool.dma_start(w_mix[:, :, c * MIXC:(c + 1) * MIXC], mix[:, c % 2]).then_inc(mix_out, 16)
                if c + 1 < GROUPS:
                    load_mix(c + 1)

            nc.gpsimd.memset(half[:], -0.5).then_inc(filled_in, 1)
            nc.gpsimd.memset(restart[:], 1.0).then_inc(filled_in, 1)
            nc.gpsimd.memset(ones16[:], 1.0).then_inc(filled_in, 1)
            nc.gpsimd.memset(no_token[:], 0.0).then_inc(filled_in, 1)
            pool.wait_ge(filled_in, 4)
            nc.gpsimd.memset(restart[:, :, 0], 0.0).then_inc(filled_in, 1)
            load_mix(0)
            pool.wait_ge(var_done, 1)
            nc.gpsimd.tensor_tensor(rstd[:, 0:LT], var_eps[:, 0:LT], half[:, 0:LT], ALU.pow).then_inc(rstd_done, 1)
            pool.wait_ge(var_done, 2)
            nc.gpsimd.tensor_tensor(rstd[:, LT:2 * LT], var_eps[:, LT:2 * LT], half[:, LT:2 * LT], ALU.pow).then_inc(rstd_done, 1)
            BEFORE = GROUPS // 2
            for c in range(BEFORE):
                for stage in range(STAGES):
                    mix_stage(c, stage)
                store_mix(c)
                if c == 0:
                    pool.wait_ge(var_done, 3)
                    nc.gpsimd.tensor_tensor(rstd[:, 2 * LT:TT], var_eps[:, 2 * LT:TT], half[:, 2 * LT:TT], ALU.pow).then_inc(rstd_done, 1)
            pool.wait_ge(where_done, 1)
            pool.wait_ge(zeroed, 16)
            for k in (0, 1):
                for t in range(TT):
                    pool.indirect_dma_start(token_table, bass.IndirectOffsetOnAxis(where_u[:, k, t:t + 1], 0),
                                            token_no[:, t:t + 1], None).then_inc(scattered, 16)
            pool.wait_ge(table_done, 1)
            pool.wait_ge(xn_sent[0], 16 * (B // 2))
            pool.wait_ge(xn_sent[1], 16 * (B // 2))
            for t in range(RT):
                if t >= 2:
                    pool.wait_ge(rows_turned, t - 1)
                pool.indirect_dma_start(xn[:, t % 2, 0, :], None, xn_rows,
                                        bass.IndirectOffsetOnAxis(table_u[:, t:t + 1], 0)).then_inc(rows_in[t % 2], 16)
                c, part = BEFORE + (t - 2) // (2 * STAGES), (t - 2) % (2 * STAGES)
                if t >= 2 and c < GROUPS:
                    if part % 2 == 0:
                        mix_stage(c, part // 2)
                    if part == 2 * STAGES - 1:
                        store_mix(c)
            pool.wait_ge(mix_out, 16 * GROUPS)

        @block.scalar
        def _(act):
            def split(k):
                j = ORDER[k]
                act.wait_ge(raw_in[k % 2], 32 * (k // 2 + 1))
                nc.scalar.activation(up[:, 0, 2 * j:2 * j + 2].rearrange("p t c q -> p t (c q)"), raw_up[:, k % 2], ACT.Copy, scale=WS)\
                    .then_inc(split_hi, 1)
                nc.scalar.activation(dn[:, 0, 2 * j:2 * j + 2], raw_dn[:, k % 2], ACT.Copy, scale=WS).then_inc(split_hi, 1)

            def turn_hi(b):
                for c in range(DT):
                    act.wait_ge(xT_done, DT * b + c + 1)
                    if b >= 3 and c == 0:
                        act.wait_ge(up_done, ST * (b - 2))
                    nc.scalar.activation(xt[:, b % 3, 0, c, :], prep[(USES * b + c) % 2][:], ACT.Copy).then_inc(xT_hi, 1)

            def shared(g):
                act.wait_ge(up_done, g + 1)
                if g >= 2:
                    act.wait_ge(h_done, g - 1)
                h = NE * 2 + g % ST
                nc.scalar.activation(hid[:, g % 2, :], bank_up[g % 2][:], ACT.Gelu, bias=b_up[:, h:h + 1], scale=1.0 / WS)\
                    .then_inc(gelu_done, 1)
                act.wait_ge(gelu_done, g + 1)
                if g >= 2:
                    act.wait_ge(down_done, g - 1)
                nc.scalar.activation(h16[:, g % 2, 0, :], hid[:, g % 2, :], ACT.Copy).then_inc(hi_done, 1)

            act.wait_ge(consts, 16 * CONSTS)
            nc.scalar.activation(tanh_g[:], gates[:], ACT.Tanh).then_inc(tanh_done, 1)
            nc.scalar.activation(gw[:, 0, :], small[:], ACT.Copy, scale=WS).then_inc(small_hi, 1)
            nc.scalar.activation(bd[:, 0, :], b_down[:], ACT.Copy, scale=WS).then_inc(small_hi, 1)
            nc.scalar.activation(pick16[:], pick, ACT.Copy).then_inc(small_hi, 1)
            nc.scalar.activation(lower16[:], lower[:], ACT.Copy).then_inc(small_hi, 1)
            split(0)
            turn_hi(0)
            split(1)
            for g in range(SHARED):
                shared(g)
                if g - 1 in TURN_AFTER:
                    turn_hi(TURN_AFTER[g - 1])
                if g in SPLIT_AT:
                    split(SPLIT_AT[g])
                if g == RANK_AFTER + 1:
                    act.wait_ge(diff_done, 1)
                    nc.scalar.activation(e1[:], diff[:], ACT.Exp, scale=1.0 / WS).then_inc(e1_done, 1)

            def rows_split(t, side):
                act.wait_ge(rows_turned, t + 1)
                if not isinstance(t, int) or t >= 2:
                    act.wait_ge(e_up, t - 1)
                nc.scalar.activation(xt[:, side, 0, :, 0:P], prep[side][:].rearrange("p (c q) -> p c q", q=P), ACT.Copy)\
                    .then_inc(rows_hi, 1)

            def routed(t, side, n):
                cell = owner_u[0:1, t:t + 1] if isinstance(t, int) else owner_u[0:1, bass.ds(t, 1)]
                e = experts(mybir.EngineType.Activation, cell)[0]
                if not isinstance(t, int) or t + 1 < RT:
                    rows_split(t + 1, 1 - side)
                act.wait_ge(e_up, t + 1)
                if not isinstance(t, int) or t >= 2:
                    act.wait_ge(e_lo, t - 1)
                for m in (0, 1):
                    ins = nc.scalar.activation(hid[:, side, m * P:(m + 1) * P], bank_up[side][:, m * P:(m + 1) * P], ACT.Gelu,
                                               bias=b_up[:, bass.ds(e * 2 + m, 1)], scale=1.0 / WS)
                ins.then_inc(e_gelu, 1)
                act.wait_ge(e_gelu, t + 1)
                if not isinstance(t, int) or t >= 2:
                    act.wait_ge(e_down, t - 1)
                nc.scalar.activation(h16[:, side, 0, 0:2 * P], hid[:, side, 0:2 * P], ACT.Copy).then_inc(e_hi, 1)

            act.wait_ge(owner_done, 1)
            act.wait_ge(h_done, SHARED)
            act.wait_ge(down_done, SHARED)
            rows_split(0, 0)
            tiles_of(act, routed)

        @block.vector
        def _(dve):
            links = [0]

            def link(ins):
                links[0] += 1
                ins.then_inc(chain, 1)
                dve.wait_ge(chain, links[0])

            def split(k):
                j = ORDER[k]
                dve.wait_ge(split_hi, 2 * k + 2)
                nc.vector.scalar_tensor_tensor(up[:, 1, 2 * j:2 * j + 2].rearrange("p t c q -> p t (c q)"), raw_up[:, k % 2], WS,
                                               up[:, 0, 2 * j:2 * j + 2].rearrange("p t c q -> p t (c q)"),
                                               ALU.mult, ALU.subtract).then_inc(split_lo, 1)
                nc.vector.scalar_tensor_tensor(dn[:, 1, 2 * j:2 * j + 2], raw_dn[:, k % 2], WS, dn[:, 0, 2 * j:2 * j + 2],
                                               ALU.mult, ALU.subtract).then_inc(split_lo, 1)

            def stats_of(b):
                dve.wait_ge(x_in[b], 16)
                for i in range(LT):
                    ins = nc.vector.bn_stats(stat[:, LT * b + i, :], xs[:, b, i, :])
                link(ins)
                for i in range(LT):
                    ins = nc.vector.bn_aggr(mv[:, LT * b + i, :], stat[:, LT * b + i, :])
                link(ins)

            def norm_of(b):
                dve.wait_ge(rstd_done, min(b, 2) + 1)
                if b == 1:
                    dve.wait_ge(small_hi, 3)
                if b >= 2:
                    dve.wait_ge(xT_done, DT * (b - 1))
                    dve.wait_ge(xn_sent[b % 2], 16)
                for i in range(LT):
                    t = LT * b + i
                    nc.vector.tensor_scalar(xn[:, b % 2, i, :], xs[:, b, i, :], mv[:, t, 0:1], rstd[:, t:t + 1],
                                            ALU.subtract, ALU.mult).then_inc(xn_done, 1)

            def turn_lo(b):
                for c in range(DT):
                    dve.wait_ge(xT_hi, DT * b + c + 1)
                    nc.vector.tensor_tensor(xt[:, b % 3, 1, c, :], prep[(USES * b + c) % 2][:], xt[:, b % 3, 0, c, :], ALU.subtract)\
                        .then_inc(prep_read, 1)

            def route(b):
                dve.wait_ge(logit_done, b + 1)
                rows = slice(LT * b, LT * (b + 1))
                nc.vector.tensor_copy(logit[:, rows].rearrange("p t e -> p (t e)"), prep[(USES * b + DT) % 2][:, 0:LT * NE])\
                    .then_inc(prep_read, 1)
                dve.wait_ge(prep_read, USES * (b + 1))
                for t in range(LT * b, LT * (b + 1)):
                    ins = nc.vector.max(top[:, t, :], logit[:, t, :])
                link(ins)
                for t in range(LT * b, LT * (b + 1)):
                    ins = nc.vector.max_index(top_at[:, t, :], top[:, t, :], logit[:, t, :])
                link(ins)

            def members():
                nc.vector.tensor_tensor(diff[:], top[:, :, 1], top[:, :, 0], ALU.subtract).then_inc(diff_done, 1)
                link(nc.vector.tensor_copy(at[:], top_at[:, :, 0:2]))
                for k in (0, 1):
                    ins = nc.vector.tensor_tensor(chosen[:, k], expert_no[:], over(at[:, :, k], 1, [P, NE, TT]), ALU.is_equal)
                link(ins)
                link(nc.vector.tensor_tensor(member[:], chosen[:, 0], chosen[:, 1], ALU.add))
                nc.vector.tensor_copy(member16[:], member[:]).then_inc(member_done, 1)
                dve.wait_ge(filled_in, 5)
                link(nc.vector.tensor_tensor_scan(upto[:].rearrange("p e t -> p (e t)"), restart[:].rearrange("p e t -> p (e t)"),
                                                  member[:].rearrange("p e t -> p (e t)"), 0.0, ALU.mult, ALU.add))
                nc.vector.tensor_copy(upto16[:], upto[:]).then_inc(member_done, 1)

            def places():
                dve.wait_ge(rank_done, 1)
                nc.vector.tensor_copy(rank[:].rearrange("p e t -> p (e t)"), prep[RANK_USE % 2][:, 0:NE * TT])
                nc.vector.tensor_copy(count[:], prep[RANK_USE % 2][:, NE * TT:NE * TT + NE]).then_inc(prep_read, 1)
                dve.wait_ge(prep_read, RANK_USE + 1)
                link(nc.vector.tensor_tensor(filled[:], over(count[:], 2, [P, NE, TT]), over(thresholds[:], 1, [P, NE, TT]), ALU.is_gt))
                link(nc.vector.reduce_sum(tiles[:], filled[:], AX_X))
                link(nc.vector.tensor_tensor_scan(ends[:], restart[:, 0:NE, 1], tiles[:], 0.0, ALU.mult, ALU.add))
                link(nc.vector.tensor_tensor(base[:], ends[:], tiles[:], ALU.subtract))
                link(nc.vector.scalar_tensor_tensor(rank[:], over(base[:], 2, [P, NE, TT]), float(P), rank[:], ALU.mult, ALU.add))
                for k in (0, 1):
                    ins = nc.vector.tensor_tensor(place[:, k], chosen[:, k], rank[:], ALU.mult)
                link(ins)
                for k in (0, 1):
                    ins = nc.vector.reduce_sum(where[:, k, :], place[:, k].rearrange("p e t -> p t e"), AX_X)
                link(ins)
                nc.vector.tensor_copy(where_u[:], where[:]).then_inc(where_done, 1)
                link(nc.vector.tensor_tensor(passed[:], over(ends[:], 1, [P, RT, NE]), over(tile_no[:], 2, [P, RT, NE]), ALU.is_le))
                link(nc.vector.reduce_sum(owner[:], passed[:], AX_X))
                nc.vector.tensor_copy(owner_u[:], owner[:]).then_inc(owner_done, 1)

            def token_gates():
                dve.wait_ge(e1_done, 1)
                link(nc.vector.tensor_scalar_add(ge[:, 0, :], e1[:], 1.0))
                link(nc.vector.reciprocal(ge[:, 1, :], ge[:, 0, :]))
                link(nc.vector.tensor_tensor(ge[:, 2, :], e1[:], ge[:, 1, :], ALU.mult))
                nc.vector.tensor_scalar_mul(scaled[:], ge[:, 1:3, :], scale_out[:]).then_inc(scaled_done, 1)

            def shared_lo(g):
                dve.wait_ge(hi_done, g + 1)
                nc.vector.tensor_tensor(h16[:, g % 2, 1, :], hid[:, g % 2, :], h16[:, g % 2, 0, :], ALU.subtract).then_inc(h_done, 1)

            def x1s_of(b):
                dve.wait_ge(down_done, ST * (b + 1))
                for i in range(LT):
                    nc.vector.scalar_tensor_tensor(xs[:, b, i, :], bank_out[i][:], scale_out[:], xs[:, b, i, :],
                                                   ALU.mult, ALU.add).then_inc(x1s_done, 1)

            stats_of(0)
            nc.vector.tensor_scalar_add(var_eps[:, 0:LT], mv[:, 0:LT, 1], EPS).then_inc(var_done, 1)
            norm_of(0)
            dve.wait_ge(consts, 16 * CONSTS)
            dve.wait_ge(tanh_done, 1)
            link(nc.vector.tensor_scalar_mul(scale_out[:], tanh_g[:, 0:1], 1.0 / WS))
            dve.wait_ge(small_hi, 2)
            nc.vector.scalar_tensor_tensor(gw[:, 1, :], small[:], WS, gw[:, 0, :], ALU.mult, ALU.subtract).then_inc(small_lo, 1)
            nc.vector.scalar_tensor_tensor(bd[:, 1, :], b_down[:], WS, bd[:, 0, :], ALU.mult, ALU.subtract).then_inc(small_lo, 1)
            split(0)
            turn_lo(0)
            split(1)
            stats_of(1)
            nc.vector.tensor_scalar_add(var_eps[:, LT:2 * LT], mv[:, LT:2 * LT, 1], EPS).then_inc(var_done, 1)
            route(0)
            norm_of(1)
            for g in range(SHARED):
                shared_lo(g)
                if g < 2:
                    stats_of(2 + g)
                if g == 1:
                    nc.vector.tensor_scalar_add(var_eps[:, 2 * LT:TT], mv[:, 2 * LT:TT, 1], EPS).then_inc(var_done, 1)
                if g % ST == 0 and g:
                    x1s_of(g // ST - 1)
                if g - 1 in TURN_AFTER:
                    turn_lo(TURN_AFTER[g - 1])
                if g - 1 in LOGITS_AFTER:
                    route(LOGITS_AFTER[g - 1])
                    if g == RANK_AFTER:
                        members()
                if g + 1 in TURN_AFTER and g:
                    norm_of(TURN_AFTER[g + 1])
                if g == RANK_AFTER + 1:
                    places()
                    token_gates()
                if g in SPLIT_AT:
                    split(SPLIT_AT[g])
            x1s_of(B - 1)
            dve.wait_ge(x1s_done, LT * B)
            dve.sem_inc(out_free, 2)
            dve.wait_ge(table_turned, 1)
            nc.vector.tensor_copy(table_u[:], prep[TABLE_USE % 2][:, 0:RT]).then_inc(prep_read, 1)
            dve.wait_ge(prep_read, TABLE_USE + 1)
            dve.sem_inc(table_done, 1)

            def rows_split(t, side):
                dve.wait_ge(rows_hi, t + 1)
                nc.vector.tensor_tensor(xt[:, side, 1, :, 0:P], prep[side][:].rearrange("p (c q) -> p c q", q=P),
                                        xt[:, side, 0, :, 0:P], ALU.subtract).then_inc(prep_read, 1)

            def y_of(t, side, n):
                dve.wait_ge(e_down, t + 1)
                dve.wait_ge(y_free[side], n * 16 + 16)
                nc.vector.tensor_copy(xs[:, 0, side, :], bank_out[side][:]).then_inc(out_free, 1)

            def routed(t, side, n):
                if not isinstance(t, int) or t + 1 < RT:
                    rows_split(t + 1, 1 - side)
                if not isinstance(t, int) or t >= 2:
                    y_of(t - 2, side, n - 1)
                dve.wait_ge(e_hi, t + 1)
                nc.vector.tensor_tensor(h16[:, side, 1, 0:2 * P], hid[:, side, 0:2 * P], h16[:, side, 0, 0:2 * P], ALU.subtract)\
                    .then_inc(e_lo, 1)

            rows_split(0, 0)
            tiles_of(dve, routed)
            for t in (RT - 2, RT - 1):
                y_of(t, t % 2, t // 2)

        @block.tensor
        def _(pe):
            def bank(use):
                if use >= 2:
                    pe.wait_ge(prep_read, use - 1)
                return prep[use % 2]

            def turn(b):
                pe.wait_ge(xn_done, LT * (b + 1))
                for c in range(DT):
                    dst = bank(USES * b + c)
                    for i in range(LT):
                        mm = nc.tensor.transpose(dst[:, i * P:(i + 1) * P], xn[:, b % 2, i, c * P:(c + 1) * P], ident[:])
                    mm.then_inc(xT_done, 1)

            def logits(b):
                dst = bank(USES * b + DT)
                pe.wait_ge(prep_read, USES * b + DT)
                pe.wait_ge(small_lo, 2)
                for i in range(LT):
                    n = 0
                    for c in range(DT):
                        for xh, wh in ((0, 0), (0, 1), (1, 0)):
                            mm = nc.tensor.matmul(dst[:, i * NE:(i + 1) * NE], xt[:, b % 3, xh, c, i * P:(i + 1) * P],
                                                  gw[:, wh, c * NE:(c + 1) * NE], start=(n == 0), stop=(n == 3 * DT - 1))
                            n += 1
                mm.then_inc(logit_done, 1)

            def ranks():
                pe.wait_ge(member_done, 2)
                pe.wait_ge(small_hi, 4)
                pe.wait_ge(filled_in, 5)
                dst = bank(RANK_USE)
                flat = "p e t -> p (e t)"
                nc.tensor.matmul(dst[:, 0:NE * TT], lower16[:], member16[:].rearrange(flat), start=True, stop=False)
                nc.tensor.matmul(dst[:, 0:NE * TT], ones16[:], upto16[:].rearrange(flat), start=False, stop=True)
                nc.tensor.matmul(dst[:, NE * TT:NE * TT + NE], ones16[:], upto16[:, :, TT - 1], start=True, stop=True).then_inc(rank_done, 1)

            def shared_up(g):
                b = g // ST
                if g < 2:
                    pe.wait_ge(split_lo, 2 * (len(ORDER) - NE))
                pe.wait_ge(prep_read, USES * b + DT)
                if g >= 2:
                    pe.wait_ge(gelu_done, g - 1)
                n = 0
                for c in range(DT):
                    for wh, xh in ((0, 0), (0, 1), (1, 0)):
                        mm = nc.tensor.matmul(bank_up[g % 2][:], up[:, wh, NE * 2 + g % ST, c, :], xt[:, b % 3, xh, c, :],
                                              start=(n == 0), stop=(n == 3 * DT - 1))
                        n += 1
                mm.then_inc(up_done, 1)

            def shared_down(g):
                b = g // ST
                if g % ST == 0:
                    if g == 0:
                        pe.wait_ge(small_hi, 3)
                    else:
                        pe.wait_ge(x1s_done, LT * b)
                    for i in range(LT):
                        for hl in (0, 1):
                            nc.tensor.matmul(bank_out[i][:], pick16[:, NE * P:(NE + 1) * P], bd[:, hl, :], start=(hl == 0), stop=False)
                pe.wait_ge(h_done, g + 1)
                for i in range(LT):
                    for n, (hh, wh) in enumerate(((0, 0), (0, 1), (1, 0))):
                        mm = nc.tensor.matmul(bank_out[i][:], h16[:, g % 2, hh, i * P:(i + 1) * P], dn[:, wh, NE * 2 + g % ST, :],
                                              start=False, stop=(g % ST == ST - 1 and n == 2))
                mm.then_inc(down_done, 1)

            pe.wait_ge(consts, 16 * CONSTS)
            turn(0)
            logits(0)
            shared_up(0)
            for g in range(SHARED):
                if g + 1 < SHARED:
                    shared_up(g + 1)
                shared_down(g)
                if g in TURN_AFTER:
                    turn(TURN_AFTER[g])
                if g in LOGITS_AFTER:
                    logits(LOGITS_AFTER[g])
                if g == RANK_AFTER:
                    ranks()
            pe.wait_ge(table_in, 16)
            nc.tensor.transpose(bank(TABLE_USE)[:, 0:RT], table[:], ident[0:RT, 0:RT]).then_inc(table_turned, 1)

            def rows_turn(t, side, n):
                pe.wait_ge(rows_in[side], n * 16 + 16)
                pe.wait_ge(prep_read, t + (ROWS_USE - 1))
                for c in range(DT):
                    mm = nc.tensor.transpose(prep[side][:, c * P:(c + 1) * P], xn[:, side, 0, c * P:(c + 1) * P], ident[:])
                mm.then_inc(rows_turned, 1)

            def up_products(side, e):
                for m in (0, 1):
                    n = 0
                    for c in range(DT):
                        for wh, xh in ((0, 0), (0, 1), (1, 0)):
                            wt = up[:, wh, bass.ds(e * 2 + m, 1), c, :].rearrange("p o q -> p (o q)")
                            yield bank_up[side][:, m * P:(m + 1) * P], wt, xt[:, side, xh, c, 0:P], n == 0, n == 3 * DT - 1
                            n += 1

            def down_products(side, e):
                for hl in (0, 1):
                    yield bank_out[side][:], pick16[:, bass.ds(e * P, P)], bd[:, hl, :], hl == 0, False
                for m in (0, 1):
                    for n, (hh, wh) in enumerate(((0, 0), (0, 1), (1, 0))):
                        wt = dn[:, wh, bass.ds(e * 2 + m, 1), :].rearrange("p o d -> p (o d)")
                        yield bank_out[side][:], h16[:, side, hh, m * P:(m + 1) * P], wt, False, m == 1 and n == 2

            def product(dst, lhs, rhs, start, stop):
                return nc.tensor.matmul(dst, lhs, rhs, start=start, stop=stop)

            def routed(t, side, n):
                early = isinstance(t, int) and t < 2
                cells = owner_u[0:1, 0:3] if early else owner_u[0:1, t - 2:t + 1] if isinstance(t, int) \
                    else owner_u[0:1, bass.ds(t - 2, 3)]
                e = experts(mybir.EngineType.PE, cells)
                if not isinstance(t, int) or t + 1 < RT:
                    rows_turn(t + 1, 1 - side, n + side)
                pe.wait_ge(prep_read, t + (ROWS_USE + 1))
                if not early:
                    pe.wait_ge(e_gelu, t - 1)
                    pe.wait_ge(e_lo, t - 1)
                    pe.wait_ge(out_free, t - 1)
                ups = list(up_products(side, e[t if early else 2]))
                downs = [] if early else list(down_products(side, e[0]))
                for k in range(len(ups) // 4):
                    if downs:
                        product(*downs[k])
                    for args in ups[4 * k:4 * k + 4]:
                        mm = product(*args)
                mm.then_inc(e_up, 1)
                for args in downs[len(ups) // 4:]:
                    mm = product(*args)
                if downs:
                    mm.then_inc(e_down, 1)

            def last_down(t, side):
                e = experts(mybir.EngineType.PE, owner_u[0:1, t:t + 1])[0]
                pe.wait_ge(e_lo, t + 1)
                pe.wait_ge(out_free, t + 1)
                for args in down_products(side, e):
                    mm = product(*args)
                mm.then_inc(e_down, 1)

            pe.wait_ge(owner_done, 1)
            pe.wait_ge(split_lo, 2 * len(ORDER))
            pe.wait_ge(gelu_done, SHARED)
            rows_turn(0, 0, 0)
            tiles_of(pe, routed)
            for t in (RT - 2, RT - 1):
                last_down(t, t % 2)




def ffn_block(nc, w, ctx_t, x1s, expert_out, routes, scales, w_mix, out):
    EXPERTS_AT, NORM2_AT, QK_AT, ENERGY_AT, EXP_AT, XT32_AT, PROBT_AT, PRODUCT_AT, NORM3_AT, XT_AT = 0, 1, 1, 2, 4, 5, 7, 9, 10, 12
    MIX = WS * float(H) ** -0.5
    USES = 11
    with ExitStack() as stack:
        def sb(name, shape, dt=F32):
            return stack.enter_context(nc.sbuf_tensor("f_" + name, shape, dt))

        def sem(name):
            return stack.enter_context(nc.semaphore("ffn_" + name))

        ident = sb("ident", [P, P])
        hada = sb("hada", [P, P])
        gates = sb("gates", [P, 2])
        tanh_g = sb("tanh_g", [P, 2])
        scale_out = sb("scale_out", [P, 1])
        where = sb("where", [P, 2, TT], U32)
        gate = sb("gate", [P, 2, TT])
        half = sb("half", [P, LT])
        w_q = sb("w_q", [P, CT, P])
        w_k = sb("w_k", [P, CT, P])
        b_qk = sb("b_qk", [P, 2])
        raw = sb("raw", [P, 2, 2, DT * P])
        raw_mix = sb("raw_mix", [P, 4, D])
        wg = sb("wg", [P, 2, FT, DT, P], F16)
        wl = sb("wl", [P, 2, FT, DT, P], F16)
        wo = sb("wo", [P, 2, FT, D], F16)
        ctxs = sb("ctxs", [P, CT, L])
        qk = sb("qk", [P, 2, L])
        xs = sb("xs", [P, 2, LT, D])
        xn = sb("xn", [P, LT, D])
        stat = sb("stat", [P, LT, 6])
        mv = sb("mv", [P, LT, 2])
        var_eps = sb("var_eps", [P, LT])
        rstd = sb("rstd", [P, LT])
        neg_max = sb("neg_max", [P, LT])
        total = sb("total", [P, LT])
        inv = sb("inv", [P, LT])
        energy = sb("energy", [P, LT, L])
        prob = sb("prob", [P, LT, L])
        probT = sb("probT", [P, LT, L])
        xt32 = sb("xt32", [P, DT, L])
        xt = sb("xt", [P, 2, 2, DT, L], F16)
        sg = sb("sg", [P, 2, L])
        hid = sb("hid", [P, 2, L])
        h16 = sb("h16", [P, 2, 2, L], F16)
        bank_g = stack.enter_context(nc.psum_tensor("ffn_g", [P, 512], F32))
        bank_u = stack.enter_context(nc.psum_tensor("ffn_u", [P, 512], F32))
        prep = [stack.enter_context(nc.psum_tensor(f"ffn_prep{i}", [P, 512], F32)) for i in range(2)]
        bank_out = [stack.enter_context(nc.psum_tensor(f"ffn_out{i}", [P, 512], F32)) for i in range(LT)]

        consts = sem("consts")
        x_in = [sem("x_in_even"), sem("x_in_odd")]
        ctx_in = sem("ctx_in")
        routes_in = sem("routes_in")
        y_in = sem("y_in")
        x2_first = sem("x2_first")
        x2_done = sem("x2_done")
        raw_in = [sem("raw_in_even"), sem("raw_in_odd")]
        mix_in = [sem(f"mix_in{i}") for i in range(4)]
        mix_done = sem("mix_done")
        mix_hi = sem("mix_hi")
        mix_lo = sem("mix_lo")
        split_hi = sem("split_hi")
        split_lo = sem("split_lo")
        half_set = sem("half_set")
        tanh_done = sem("tanh_done")
        var_done = sem("var_done")
        rstd_done = sem("rstd_done")
        xn_done = sem("xn_done")
        filled = [sem("filled0"), sem("filled1")]
        qk_done = sem("qk_done")
        max_done = sem("max_done")
        energy_done = sem("energy_done")
        exp_done = sem("exp_done")
        prob_done = sem("prob_done")
        xt32_done = sem("xt32_done")
        probT_done = sem("probT_done")
        x3_done = sem("x3_done")
        xT_hi = sem("xT_hi")
        xT_lo = sem("xT_lo")
        g_done = sem("g_done")
        u_done = sem("u_done")
        silu_done = sem("silu_done")
        hid_done = sem("hid_done")
        hi_done = sem("hi_done")
        h_done = sem("h_done")
        down_done = sem("down_done")
        out_done = sem("out_done")
        out_sent = [sem("out_sent_even"), sem("out_sent_odd")]
        chain = sem("chain")
        CONSTS = 8
        Q, K, ENERGY, XT32, PROBT, PRODUCT, XT = 0, 1, 2, 6, 10, 14, 18
        block = stack.enter_context(nc.Block())

        def bank(use):
            return prep[use % 2]

        def full(eng, use, b):
            eng.wait_ge(filled[use % 2], USES * b + use // 2 + 1)

        def read_last(eng, use, b):
            if use < ENERGY:
                eng.wait_ge(qk_done, 2 * b + use + 1)
            elif use < XT32:
                eng.wait_ge(energy_done, LT * b + use - ENERGY + 1)
            elif use < PROBT:
                eng.wait_ge(xt32_done, DT * b + use - XT32 + 1)
            elif use < PRODUCT:
                eng.wait_ge(probT_done, LT * b + use - PROBT + 1)
            elif use < XT:
                eng.wait_ge(x3_done, LT * b + use - PRODUCT + 1)
            else:
                eng.wait_ge(xT_lo, DT * b + use - XT + 1)

        def empty(eng, use, b):
            if use >= 2:
                read_last(eng, use - 2, b)
            elif b:
                read_last(eng, use - 2 + 2 * USES, b - 1)

        def two(t, first):
            return (2 * (t - first), 2 * (t - first) + 1) if first <= t <= first + 1 else ()

        @block.sync
        def _(sp):
            def load(b):
                if b:
                    sp.wait_ge(filled[1], USES * (b - 1) + K // 2 + 1)
                sp.dma_start(ctxs[:], ctx_t[b].rearrange("(c p) l -> p c l", p=P)).then_inc(ctx_in, 16)
                if b >= 2:
                    sp.wait_ge(out_sent[b % 2], 16 * (b // 2))
                sp.dma_start(xs[:, b % 2], x1s[b].rearrange("(t p) d -> p t d", p=P)).then_inc(x_in[b % 2], 16)

            sp.dma_start(where[:], routes).then_inc(routes_in, 16)
            sp.dma_start(gate[:], scales).then_inc(routes_in, 16)
            load(0)
            for dst, src in ((ident[:], "ident"), (hada[:], "hadamard"), (w_q[:], "w_q"), (w_k[:], "w_k"),
                             (b_qk[:, 0:1], "b_q"), (b_qk[:, 1:2], "b_k")):
                sp.dma_start(dst, w[src]).then_inc(consts, 16)
            sp.dma_start(gates[:, 0:1], w["g_xattn"][1:2].partition_broadcast(P)).then_inc(consts, 16)
            sp.dma_start(gates[:, 1:2], w["g_ffn"][1:2].partition_broadcast(P)).then_inc(consts, 16)
            for t in range(FT):
                if t >= 4:
                    sp.wait_ge(mix_done, t - 3)
                sp.dma_start(raw_mix[:, t % 4], w_mix[:, t, :]).then_inc(mix_in[t % 4], 16)
            load(1)
            for t in range(FT):
                if t >= 2:
                    sp.wait_ge(split_hi, 2 * (t - 1))
                    sp.wait_ge(split_lo, 2 * (t - 1))
                sp.dma_start(raw[:, t % 2, 0], w["w_gate"][:, t, :]).then_inc(raw_in[t % 2], 16)
                sp.dma_start(raw[:, t % 2, 1], w["w_lin"][:, t, :]).then_inc(raw_in[t % 2], 16)
            for b in range(B):
                if 2 <= b + 1 < B:
                    load(b + 1)
                sp.wait_ge(out_done, LT * (b + 1))
                sp.dma_start(out[b].rearrange("(t p) d -> p t d", p=P), xs[:, b % 2]).then_inc(out_sent[b % 2], 16)
            sp.wait_ge(out_sent[0], 16 * (B // 2))
            sp.wait_ge(out_sent[1], 16 * (B // 2))

        @block.gpsimd
        def _(pool):
            nc.gpsimd.memset(half[:], -0.5).then_inc(half_set, 1)
            pool.wait_ge(half_set, 1)
            pool.wait_ge(routes_in, 32)
            for n in range(2 * B):
                if n % 2 == 0:
                    b = n // 2
                    if b:
                        full(pool, XT + 3, b - 1)
                        pool.wait_ge(x3_done, LT * b)
                    for k, dst in enumerate((xn, xt32)):
                        for i in range(LT):
                            t = LT * b + i
                            pool.indirect_dma_start(dst[:, i, :], None, expert_out.rearrange("t p d -> (t p) d"),
                                                    bass.IndirectOffsetOnAxis(where[:, k, t:t + 1], 0)).then_inc(y_in, 16)
                pool.wait_ge(var_done, n + 1)
                nc.gpsimd.tensor_tensor(rstd[:], var_eps[:], half[:], ALU.pow).then_inc(rstd_done, 1)

        @block.scalar
        def _(act):
            def split(t):
                act.wait_ge(raw_in[t % 2], 32 * (t // 2 + 1))
                nc.scalar.activation(wg[:, 0, t].rearrange("p c q -> p (c q)"), raw[:, t % 2, 0], ACT.Copy, scale=WS).then_inc(split_hi, 1)
                nc.scalar.activation(wl[:, 0, t].rearrange("p c q -> p (c q)"), raw[:, t % 2, 1], ACT.Copy, scale=WS).then_inc(split_hi, 1)

            def mix(group):
                for t in range(4 * group, 4 * group + 4):
                    act.wait_ge(mix_done, t + 1)
                    nc.scalar.activation(wo[:, 0, t, :], bank_out[t % 4][:], ACT.Copy, scale=MIX).then_inc(mix_hi, 1)

            def qk_of(b):
                if b:
                    full(act, ENERGY + 3, b - 1)
                full(act, Q, b)
                nc.scalar.activation(qk[:, 0, :], bank(Q)[:], ACT.Identity, bias=b_qk[:, 0:1]).then_inc(qk_done, 1)
                full(act, K, b)
                nc.scalar.activation(qk[:, 1, :], bank(K)[:], ACT.Identity, bias=b_qk[:, 1:2]).then_inc(qk_done, 1)

            def copy_energy(b, tiles):
                for i in tiles:
                    full(act, ENERGY + i, b)
                    if b and i == 0:
                        act.wait_ge(exp_done, LT * b)
                    nc.scalar.activation(energy[:, i, :], bank(ENERGY + i)[:], ACT.Copy).then_inc(energy_done, 1)

            def exp_of(b):
                for i in range(LT):
                    act.wait_ge(max_done, LT * b + i + 1)
                    if b and i == 0:
                        full(act, PROBT + 3, b - 1)
                    nc.scalar.activation(prob[:, i, :], energy[:, i, :], ACT.Exp, bias=neg_max[:, i:i + 1],
                                         accum_out=total[:, i:i + 1]).then_inc(exp_done, 1)

            def copy_xt32(b, tiles):
                for c in tiles:
                    full(act, XT32 + c, b)
                    if b and c == 0:
                        act.wait_ge(x3_done, LT * b)
                    nc.scalar.activation(xt32[:, c, :], bank(XT32 + c)[:], ACT.Copy).then_inc(xt32_done, 1)

            def copy_probT(b, tiles):
                for c in tiles:
                    full(act, PROBT + c, b)
                    if b and c == 0:
                        act.wait_ge(x3_done, LT * b)
                    nc.scalar.activation(probT[:, c, :], bank(PROBT + c)[:], ACT.Copy).then_inc(probT_done, 1)

            def turn_hi(b, tiles):
                for c in tiles:
                    full(act, XT + c, b)
                    if b >= 2 and c == 0:
                        act.wait_ge(down_done, FT * (b - 1))
                    nc.scalar.activation(xt[:, b % 2, 0, c, :], bank(XT + c)[:], ACT.Copy).then_inc(xT_hi, 1)

            def tile(t, side, b, first):
                act.wait_ge(g_done, t + (FT * b + 1))
                if not first:
                    act.wait_ge(hid_done, t + (FT * b - 1))
                nc.scalar.activation(sg[:, side, :], bank_g[:], ACT.Silu, scale=1.0 / WS).then_inc(silu_done, 1)

            act.wait_ge(consts, 16 * CONSTS)
            nc.scalar.activation(tanh_g[:], gates[:], ACT.Tanh).then_inc(tanh_done, 1)
            qk_of(0)
            copy_energy(0, range(LT))
            exp_of(0)
            mix(0)
            copy_xt32(0, range(DT))
            mix(1)
            copy_probT(0, range(LT))
            mix(2)
            mix(3)
            split(0)
            turn_hi(0, range(DT))
            for b in range(B):
                for t in range(FT):
                    if b == 0 and t + 1 < FT:
                        split(t + 1)
                    tile(t, t % 2, b, b == 0 and t < 2)
                    if b + 1 < B:
                        if t == QK_AT:
                            qk_of(b + 1)
                        copy_energy(b + 1, two(t, ENERGY_AT))
                        if t == EXP_AT:
                            exp_of(b + 1)
                        copy_xt32(b + 1, two(t, XT32_AT))
                        copy_probT(b + 1, two(t, PROBT_AT))
                        turn_hi(b + 1, two(t, XT_AT))

        @block.vector
        def _(dve):
            links = [0]

            def link(ins):
                links[0] += 1
                ins.then_inc(chain, 1)
                dve.wait_ge(chain, links[0])

            def split(t):
                dve.wait_ge(split_hi, 2 * t + 2)
                for n, dst in enumerate((wg, wl)):
                    nc.vector.scalar_tensor_tensor(dst[:, 1, t].rearrange("p c q -> p (c q)"), raw[:, t % 2, n], WS,
                                                   dst[:, 0, t].rearrange("p c q -> p (c q)"), ALU.mult, ALU.subtract).then_inc(split_lo, 1)

            def mix(group):
                for t in range(4 * group, 4 * group + 4):
                    dve.wait_ge(mix_hi, t + 1)
                    nc.vector.scalar_tensor_tensor(wo[:, 1, t, :], bank_out[t % 4][:], MIX, wo[:, 0, t, :], ALU.mult, ALU.subtract)\
                        .then_inc(mix_lo, 1)

            def add_experts(b):
                dve.wait_ge(x_in[b % 2], 16 * (b // 2 + 1))
                dve.wait_ge(y_in, 16 * 2 * LT * (b + 1))
                for i in range(LT):
                    t = LT * b + i
                    nc.vector.scalar_tensor_tensor(xs[:, b % 2, i, :], xn[:, i, :], gate[:, 0, t:t + 1], xs[:, b % 2, i, :],
                                                   ALU.mult, ALU.add).then_inc(x2_first, 1)
                dve.wait_ge(x2_first, LT * (b + 1))
                for i in range(LT):
                    t = LT * b + i
                    nc.vector.scalar_tensor_tensor(xs[:, b % 2, i, :], xt32[:, i, :], gate[:, 1, t:t + 1], xs[:, b % 2, i, :],
                                                   ALU.mult, ALU.add).then_inc(x2_done, 1)

            def norm_of(n, b, ready, target):
                dve.wait_ge(ready, target)
                for i in range(LT):
                    ins = nc.vector.bn_stats(stat[:, i, :], xs[:, b % 2, i, :])
                link(ins)
                for i in range(LT):
                    ins = nc.vector.bn_aggr(mv[:, i, :], stat[:, i, :])
                link(ins)
                nc.vector.tensor_scalar_add(var_eps[:], mv[:, :, 1], EPS).then_inc(var_done, 1)
                dve.wait_ge(rstd_done, n + 1)
                if n:
                    use, of = (XT32 + 3, b) if n % 2 else (XT + 3, b - 1)
                    dve.wait_ge(filled[use % 2], USES * of + use // 2 + 1)
                for i in range(LT):
                    nc.vector.tensor_scalar(xn[:, i, :], xs[:, b % 2, i, :], mv[:, i, 0:1], rstd[:, i:i + 1],
                                            ALU.subtract, ALU.mult).then_inc(xn_done, 1)

            def max_of(b, tiles):
                for i in tiles:
                    dve.wait_ge(energy_done, LT * b + i + 1)
                    link(nc.vector.reduce_max(neg_max[:, i:i + 1], energy[:, i, :], AX_X))
                    nc.vector.tensor_scalar_mul(neg_max[:, i:i + 1], neg_max[:, i:i + 1], -1.0).then_inc(max_done, 1)

            def normalise(b):
                for i in range(LT):
                    dve.wait_ge(exp_done, LT * b + i + 1)
                    link(nc.vector.reciprocal(inv[:, i:i + 1], total[:, i:i + 1]))
                    nc.vector.tensor_scalar_mul(prob[:, i, :], prob[:, i, :], inv[:, i:i + 1]).then_inc(prob_done, 1)

            def x3_of(b, tiles):
                for i in tiles:
                    full(dve, PRODUCT + i, b)
                    nc.vector.scalar_tensor_tensor(xs[:, b % 2, i, :], bank(PRODUCT + i)[:], tanh_g[:, 0:1], xs[:, b % 2, i, :],
                                                   ALU.mult, ALU.add).then_inc(x3_done, 1)

            def turn_lo(b, tiles):
                for c in tiles:
                    dve.wait_ge(xT_hi, DT * b + c + 1)
                    nc.vector.tensor_tensor(xt[:, b % 2, 1, c, :], bank(XT + c)[:], xt[:, b % 2, 0, c, :], ALU.subtract)\
                        .then_inc(xT_lo, 1)

            def tile(t, side, b, first):
                dve.wait_ge(silu_done, t + (FT * b + 1))
                dve.wait_ge(u_done, t + (FT * b + 1))
                nc.vector.scalar_tensor_tensor(hid[:, side, :], bank_u[:], 1.0 / WS, sg[:, side, :], ALU.mult, ALU.mult).then_inc(hid_done, 1)
                dve.wait_ge(hid_done, t + (FT * b + 1))
                if not first:
                    dve.wait_ge(down_done, t + (FT * b - 1))
                nc.vector.tensor_copy(h16[:, side, 0, :], hid[:, side, :]).then_inc(hi_done, 1)
                dve.wait_ge(hi_done, t + (FT * b + 1))
                nc.vector.tensor_tensor(h16[:, side, 1, :], hid[:, side, :], h16[:, side, 0, :], ALU.subtract).then_inc(h_done, 1)

            def out_of(b):
                dve.wait_ge(down_done, FT * (b + 1))
                for i in range(LT):
                    nc.vector.scalar_tensor_tensor(xs[:, b % 2, i, :], bank_out[i][:], scale_out[:], xs[:, b % 2, i, :],
                                                   ALU.mult, ALU.add).then_inc(out_done, 1)

            dve.wait_ge(tanh_done, 1)
            nc.vector.tensor_scalar_mul(scale_out[:], tanh_g[:, 1:2], 1.0 / WS)
            dve.wait_ge(routes_in, 32)
            add_experts(0)
            norm_of(0, 0, x2_done, LT)
            max_of(0, range(LT))
            normalise(0)
            mix(0)
            mix(1)
            mix(2)
            x3_of(0, range(LT))
            mix(3)
            split(0)
            norm_of(1, 0, x3_done, LT)
            turn_lo(0, range(DT))
            for b in range(B):
                for t in range(FT):
                    if b == 0 and t + 1 < FT:
                        split(t + 1)
                    tile(t, t % 2, b, b == 0 and t < 2)
                    if b + 1 < B:
                        if t == EXPERTS_AT:
                            add_experts(b + 1)
                        if t == NORM2_AT:
                            norm_of(2 * b + 2, b + 1, x2_done, LT * (b + 2))
                        max_of(b + 1, two(t, ENERGY_AT))
                        if t == EXP_AT:
                            normalise(b + 1)
                        x3_of(b + 1, two(t, PRODUCT_AT))
                        if t == NORM3_AT:
                            norm_of(2 * b + 3, b + 1, x3_done, LT * (b + 2))
                        turn_lo(b + 1, two(t, XT_AT))
                out_of(b)

        @block.tensor
        def _(pe):
            def fill(mm, use):
                mm.then_inc(filled[use % 2], 1)

            def queries(b):
                pe.wait_ge(ctx_in, 16 * (b + 1))
                for use, weight in ((Q, w_q), (K, w_k)):
                    empty(pe, use, b)
                    for c in range(CT):
                        mm = nc.tensor.matmul(bank(use)[:], weight[:, c, :], ctxs[:, c, :], start=(c == 0), stop=(c == CT - 1))
                    fill(mm, use)

            def energies(b, tiles):
                for i in tiles:
                    pe.wait_ge(qk_done, 2 * (b + 1))
                    empty(pe, ENERGY + i, b)
                    fill(nc.tensor.matmul(bank(ENERGY + i)[:], qk[:, 0, i * P:(i + 1) * P], qk[:, 1, :], start=True, stop=True),
                         ENERGY + i)

            def turn_x(first, norm, b, tiles):
                for c in tiles:
                    pe.wait_ge(xn_done, LT * (norm + 1))
                    empty(pe, first + c, b)
                    for i in range(LT):
                        mm = nc.tensor.transpose(bank(first + c)[:, i * P:(i + 1) * P], xn[:, i, c * P:(c + 1) * P], ident[:])
                    fill(mm, first + c)

            def turn_prob(b, tiles):
                for c in tiles:
                    pe.wait_ge(prob_done, LT * (b + 1))
                    empty(pe, PROBT + c, b)
                    for i in range(LT):
                        mm = nc.tensor.transpose(bank(PROBT + c)[:, i * P:(i + 1) * P], prob[:, i, c * P:(c + 1) * P], ident[:])
                    fill(mm, PROBT + c)

            def product(b, tiles):
                for i in tiles:
                    pe.wait_ge(xt32_done, DT * (b + 1))
                    pe.wait_ge(probT_done, LT * (b + 1))
                    empty(pe, PRODUCT + i, b)
                    for c in range(DT):
                        mm = nc.tensor.matmul(bank(PRODUCT + i)[:], xt32[:, c, i * P:(i + 1) * P], probT[:, c, :],
                                              start=(c == 0), stop=(c == DT - 1))
                    fill(mm, PRODUCT + i)

            def mix(group):
                for t in range(4 * group, 4 * group + 4):
                    pe.wait_ge(mix_in[t % 4], 16 * (t // 4 + 1))
                    if t >= 4:
                        pe.wait_ge(mix_lo, t - 3)
                    nc.tensor.matmul(bank_out[t % 4][:], hada[:], raw_mix[:, t % 4], start=True, stop=True).then_inc(mix_done, 1)

            def at(m, t):
                return m[:, t] if isinstance(t, int) else m[:, bass.ds(t, 1)].rearrange("p o n -> p (o n)")

            def tile_up(t, b, first=False):
                if b == 0:
                    pe.wait_ge(split_lo, 2 * (t + 1))
                if not first:
                    pe.wait_ge(hid_done, t + FT * b)
                for weight, dst, done in ((wg, bank_g, g_done), (wl, bank_u, u_done)):
                    n = 0
                    for c in range(DT):
                        for wh, xh in ((0, 0), (0, 1), (1, 0)):
                            mm = nc.tensor.matmul(dst[:], at(weight[:, wh, :, c, :], t), xt[:, b % 2, xh, c, :],
                                                  start=(n == 0), stop=(n == 3 * DT - 1))
                            n += 1
                    mm.then_inc(done, 1)

            def tile_down(t, side, b, first=False, last=False):
                pe.wait_ge(h_done, t + (FT * b + 1))
                for i in range(LT):
                    for n, (hh, wh) in enumerate(((0, 0), (0, 1), (1, 0))):
                        mm = nc.tensor.matmul(bank_out[i][:], h16[:, side, hh, i * P:(i + 1) * P], at(wo[:, wh], t),
                                              start=(first and n == 0), stop=(last and n == 2))
                mm.then_inc(down_done, 1)

            pe.wait_ge(consts, 16 * CONSTS)
            queries(0)
            energies(0, range(LT))
            mix(0)
            turn_x(XT32, 0, 0, range(DT))
            mix(1)
            turn_prob(0, range(LT))
            mix(2)
            product(0, range(LT))
            mix(3)
            turn_x(XT, 1, 0, range(DT))
            for b in range(B):
                pe.wait_ge(xT_lo, DT * (b + 1))
                for t in range(FT + 1):
                    if t < FT:
                        tile_up(t, b, first=b == 0 and t == 0)
                    if t == 1:
                        if b:
                            pe.wait_ge(out_done, LT * b)
                        else:
                            pe.wait_ge(mix_lo, FT)
                    if t:
                        tile_down(t - 1, (t - 1) % 2, b, first=t == 1, last=t == FT)
                    if b + 1 < B:
                        if t == QK_AT:
                            queries(b + 1)
                        energies(b + 1, two(t, ENERGY_AT))
                        turn_x(XT32, 2 * b + 2, b + 1, two(t, XT32_AT))
                        turn_prob(b + 1, two(t, PROBT_AT))
                        product(b + 1, two(t, PRODUCT_AT))
                        turn_x(XT, 2 * b + 3, b + 1, two(t, XT_AT))


def layout(a):
    import numpy as np

    def tiles(m, p=P):
        return np.ascontiguousarray(m.reshape(m.shape[0] // p, p, m.shape[1]).transpose(1, 0, 2))

    def col(v):
        return np.ascontiguousarray(v.reshape(-1, P).T)

    def zeros(*shape):
        return np.zeros(shape, np.float32)

    hadamard = np.array([[1.0]], np.float32)
    while hadamard.shape[0] < P:
        hadamard = np.block([[hadamard, hadamard], [hadamard, -hadamard]])
    xp = a["L0_xattn_x_proj_w"].T
    w_x = np.concatenate([xp[:, :DR], zeros(DI, DR), xp[:, DR:]], axis=1)
    up = [a["L0_ffn_w1"][e] for e in range(NE)] + [a["L0_ffn_shared_w1"]]
    down = [a["L0_ffn_w2"][e] for e in range(NE)] + [a["L0_ffn_shared_w2"]]
    up, down = np.concatenate(up, axis=1), np.concatenate(down, axis=0)
    pick = zeros(GR, GR, P)
    for e in range(GR):
        pick[e, e] = 1.0
    return {
        "x": a["x"], "g_xattn": a["g_xattn"], "g_ffn": a["g_ffn"],
        "ctx_t": np.ascontiguousarray(a["ctx_1024"].transpose(0, 2, 1)),
        "ident": np.eye(P, dtype=np.float32),
        "w_in": tiles(a["L0_xattn_in_proj_w"].T),
        "conv_w": np.ascontiguousarray(a["L0_xattn_conv_w"].T),
        "w_x": tiles(w_x),
        "w_dt": np.ascontiguousarray(a["L0_xattn_dt_proj_w"].T),
        "scan_cols": np.stack([col(a["L0_xattn_conv_b"]), col(a["L0_xattn_dt_proj_b"]), col(a["L0_xattn_D"])], axis=1),
        "a_log": tiles(a["L0_xattn_A_log"]),
        "gate_w": tiles(a["L0_ffn_gate_w"]).reshape(P, DT * NE),
        "w_up": np.ascontiguousarray(up.reshape(DT, P, HT, P).transpose(1, 2, 0, 3)).reshape(P, HT, DT * P),
        "w_down": np.ascontiguousarray(down.reshape(HT, P, D).transpose(1, 0, 2)),
        "b_up": col(np.concatenate([a["L0_ffn_b1"].reshape(-1), a["L0_ffn_shared_b1"]])),
        "b_down": np.concatenate([a["L0_ffn_b2"], a["L0_ffn_shared_b2"][None], zeros(1, D)]),
        "expert_no": np.ascontiguousarray(np.broadcast_to(np.arange(NE, dtype=np.float32)[None, :, None], (P, NE, TT))),
        "thresholds": np.tile(np.arange(TT, dtype=np.float32) * P, (P, 1)),
        "tile_no": np.tile(np.arange(RT, dtype=np.float32), (P, 1)),
        "token_no": np.arange(B * L, dtype=np.float32).reshape(TT, P).T,
        "lower": -np.triu(np.ones((P, P), np.float32)).T,
        "pick": pick.reshape(GR, GR * P),
        "w_q": tiles(a["L1_xattn_Wq"].T), "w_k": tiles(a["L1_xattn_Wk"].T),
        "b_q": col(a["L1_xattn_bq"]), "b_k": col(a["L1_xattn_bk"]),
        "w_gate": np.ascontiguousarray(a["L1_ffn_W1"].T.reshape(DT, P, FT, P).transpose(1, 2, 0, 3)).reshape(P, FT, DT * P),
        "w_lin": np.ascontiguousarray(a["L1_ffn_W3"].T.reshape(DT, P, FT, P).transpose(1, 2, 0, 3)).reshape(P, FT, DT * P),
        "w_out": tiles(a["L1_ffn_W2"].T),
        "hadamard": hadamard,
    }


def program(nc, w, out):
    x1 = nc.dram_tensor("x1_scratch", [B, L, D], F32, kind="Internal").ap()
    x1s = nc.dram_tensor("x1s_scratch", [B, L, D], F32, kind="Internal").ap()
    xn_rows = nc.dram_tensor("xn_scratch", [B * L, D], F32, kind="Internal").ap()
    expert_out = nc.dram_tensor("expert_out_scratch", [RT, P, D], F32, kind="Internal").ap()
    token_table = nc.dram_tensor("token_table_scratch", [RT * P, 1], F32, kind="Internal").ap()
    routes = nc.dram_tensor("routes_scratch", [P, 2, TT], U32, kind="Internal").ap()
    scales = nc.dram_tensor("scales_scratch", [P, 2, TT], F32, kind="Internal").ap()
    b_rows = nc.dram_tensor("b_rows_scratch", [B, NS, L], F32, kind="Internal").ap()
    w_mix = nc.dram_tensor("w_mix_scratch", [P, FT, D], F32, kind="Internal").ap()
    scan_block(nc, w, w["x"], w["ctx_t"], x1, b_rows)
    moe_block(nc, w, x1, x1s, xn_rows, expert_out, token_table, routes, scales, w_mix)
    ffn_block(nc, w, w["ctx_t"], x1s, expert_out, routes, scales, w_mix, out)


def kernel(**inputs):
    import numpy as np
    import concourse.bacc as bacc
    from concourse.bass_utils import run_bass_kernel_spmd

    nc = bacc.Bacc("TRN2", target_bir_lowering=False, num_devices=1)
    arrays = {name: np.ascontiguousarray(a) for name, a in layout({k: np.asarray(v) for k, v in inputs.items()}).items()}
    w = {name: nc.dram_tensor(name, a.shape, mybir.dt.from_np(a.dtype), kind="ExternalInput").ap() for name, a in arrays.items()}
    out = nc.dram_tensor("out", [B, L, D], F32, kind="ExternalOutput").ap()
    program(nc, w, out)
    result = run_bass_kernel_spmd(nc, [arrays], core_ids=[0])
    return result.results[0]["out"]
```

```python
from contextlib import ExitStack

import concourse.bass as bass
from concourse import mybir

F32 = mybir.dt.float32
F16 = mybir.dt.float16
U32 = mybir.dt.uint32
ALU = mybir.AluOpType
ACT = mybir.ActivationFunctionType
AX_X = mybir.AxisListType.X

P = 128
B, L, D = 4, 512, 512
C = 256
DI, NS, DR, TAPS = 512, 16, 16, 4
NE, HE, SH = 8, 256, 512
H = 2048
ET, LT, DT, CT = DI // P, L // P, D // P, C // P
HT = (NE * HE + SH) // P
GR = HT // 2
FT = H // P
TT = B * LT
RT = 2 * TT + NE - 1
WS = 64.0
EPS = 1e-5
SLOTS = 8


def scan_block(nc, w, x, ctx_t, x1, b_rows):
    SCANS, ADDS = NS * ET, (NS + 1) * LT
    GAPS = (2, 10, 12, 14, NS)
    JOINT = 2
    CONV = 8
    with ExitStack() as stack:
        def sb(name, shape, dt=F32):
            return stack.enter_context(nc.sbuf_tensor("s_" + name, shape, dt))

        def sem(name):
            return stack.enter_context(nc.semaphore("scan_" + name))

        ident = sb("ident", [P, P])
        gates = sb("gates", [P, 4])
        tanh_g = sb("tanh_g", [P, 4])
        w_tap = sb("w_tap", [P, TAPS, CT, DI])
        w_x = sb("w_x", [P, ET, 64])
        w_dt = sb("w_dt", [DR, DI])
        cols = sb("cols", [P, 3 + TAPS, ET])
        a_log = sb("a_log", [P, ET, NS])
        a_exp = sb("a_exp", [P, ET, NS])
        a_neg = sb("a_neg", [P, ET, NS])
        half = sb("half", [P, LT])
        ctx_pad = sb("ctx_pad", [P, CT, TAPS - 1 + L])
        xs = sb("xs", [P, 2, LT, D])
        xn = sb("xn", [P, LT, D])
        stat = sb("stat", [P, LT, 6])
        mv = sb("mv", [P, LT, 2])
        var_eps = sb("var_eps", [P, LT])
        rstd = sb("rstd", [P, LT])
        neg_mean = sb("neg_mean", [P, LT])
        shift = sb("shift", [P, LT])
        sz = sb("sz", [P, LT, DI])
        u = sb("u", [P, ET, L])
        proj = sb("proj", [64, L])
        b_all = sb("b_all", [P, NS, L])
        c_col = sb("c_col", [P, 2, LT, 64])
        sp_y = sb("sp_y", [P, ET, L])
        sp_l = sb("sp_l", [P, ET, L])
        sp_r = sb("sp_r", [P, ET, L])
        delta = sb("delta", [P, ET, L])
        du = sb("du", [P, ET, L])
        decay = sb("decay", [P, 2, ET, L])
        drive = sb("drive", [P, 2, ET, L])
        state = sb("state", [P, 2, ET, L])
        acc = sb("acc", [P, LT, DI])
        work = [stack.enter_context(nc.psum_tensor(f"scan_work{i}", [P, 512], F32)) for i in range(4)]
        turned = [stack.enter_context(nc.psum_tensor(f"scan_turned{i}", [P, 512], F32)) for i in range(4)]
        w_in = sp_y[:, 0:CT, :]
        tap_rows = sp_l
        x_pad = drive[:].rearrange("p h e l -> p (h e l)")[:, 0:ET * (TAPS - 1 + L)].rearrange("p (e l) -> p e l", e=ET)
        x_conv = state[:, 0]

        consts = sem("consts")
        filled = sem("filled")
        taps_done = sem("taps_done")
        inproj_done = sem("inproj_done")
        x_pad_done = sem("x_pad_done")
        tap_added = sem("tap_added")
        a_done = sem("a_done")
        tanh_done = sem("tanh_done")
        ctx_in = sem("ctx_in")
        x_in = [sem("x_in_even"), sem("x_in_odd")]
        stat_done = sem("stat_done")
        mv_done = sem("mv_done")
        var_done = sem("var_done")
        rstd_done = sem("rstd_done")
        xn_done = sem("xn_done")
        conv_done = sem("conv_done")
        u_done = sem("u_done")
        xproj_done = sem("xproj_done")
        proj_done = sem("proj_done")
        rows_out = sem("rows_out")
        rows_in = [sem(f"rows_in{q}") for q in range(len(GAPS))]
        cT_done = sem("cT_done")
        c_done = sem("c_done")
        dt_done = sem("dt_done")
        relu_done = sem("relu_done")
        exp_done = sem("exp_done")
        ln_done = sem("ln_done")
        soft = sem("soft")
        sum_done = sem("sum_done")
        delta_done = sem("delta_done")
        du_done = sem("du_done")
        skip_done = sem("skip_done")
        zT_done = sem("zT_done")
        sz_done = sem("sz_done")
        decay_done = sem("decay_done")
        drive_done = sem("drive_done")
        scan_done = sem("scan_done")
        half_free = sem("half_free")
        turned_done = sem("turned_done")
        add_done = sem("add_done")
        mul_done = sem("mul_done")
        x1_done = sem("x1_done")
        x1_out = [sem("x1_out_even"), sem("x1_out_odd")]
        CONSTS = 8
        block = stack.enter_context(nc.Block())

        def segments(eng, b, step, gap):
            lo = 0
            for q, hi in enumerate(GAPS):
                if q == 0:
                    for n in range(lo, hi):
                        step(n, n % 2)
                else:
                    with eng.Fori(lo // 2, hi // 2) as pair:
                        for k in (0, 1):
                            step(pair * 2 + k, k)
                lo = hi
                gap(q)

        @block.sync
        def _(sp):
            def load(b):
                if b == 1:
                    sp.wait_ge(inproj_done, ET)
                if b >= 2:
                    sp.wait_ge(conv_done, ET * (b - 1))
                sp.dma_start(ctx_pad[:, :, TAPS - 1:], ctx_t[b].rearrange("(c p) l -> p c l", p=P)).then_inc(ctx_in, 16)
                if b >= 2:
                    sp.wait_ge(x1_out[b % 2], 16 * (b // 2))
                sp.dma_start(xs[:, b % 2], x[b].rearrange("(t p) d -> p t d", p=P)).then_inc(x_in[b % 2], 16)

            sp.dma_start(w_in, w["w_in"]).then_inc(ctx_in, 16)
            load(0)
            sp.dma_start(tap_rows[:], w["conv_w"].partition_broadcast(P)).then_inc(consts, 16)
            for dst, src in ((ident[:], "ident"), (w_x[:], "w_x"), (w_dt[:], "w_dt"), (cols[:], "scan_cols"),
                             (a_log[:], "a_log")):
                sp.dma_start(dst, w[src]).then_inc(consts, 16)
            sp.dma_start(gates[:, 0:2], w["g_xattn"].partition_broadcast(P)).then_inc(consts, 16)
            sp.dma_start(gates[:, 2:4], w["g_ffn"].partition_broadcast(P)).then_inc(consts, 16)

            def spread_b(b):
                sp.wait_ge(proj_done, b + 1)
                sp.dma_start(b_rows[b], proj[32:48, :]).then_inc(rows_out, 16)
                sp.wait_ge(rows_out, 16 * (b + 1))
                lo = 0
                for q, hi in enumerate(GAPS):
                    if b:
                        sp.wait_ge(drive_done, SCANS * (b - 1) + ET * hi)
                    sp.dma_start(b_all[:, lo:hi, :], b_rows[b, lo:hi, :].partition_broadcast(P)).then_inc(rows_in[q], 16)
                    lo = hi

            spread_b(0)
            for b in range(B):
                if b + 1 < B:
                    load(b + 1)
                    spread_b(b + 1)
                sp.wait_ge(x1_done, LT * (b + 1))
                sp.dma_start(x1[b].rearrange("(t p) d -> p t d", p=P), xs[:, b % 2]).then_inc(x1_out[b % 2], 16)
            sp.wait_ge(x1_out[0], 16 * (B // 2))
            sp.wait_ge(x1_out[1], 16 * (B // 2))

        @block.gpsimd
        def _(pool):
            nc.gpsimd.memset(ctx_pad[:, :, 0:TAPS - 1], 0.0).then_inc(filled, 1)
            nc.gpsimd.memset(x_pad[:, :, 0:TAPS - 1], 0.0).then_inc(filled, 1)
            nc.gpsimd.memset(half[:], -0.5).then_inc(filled, 1)
            nc.gpsimd.memset(decay[:, :, :, 0], 0.0).then_inc(filled, 1)
            pool.wait_ge(filled, 3)

            def rstd_of(b):
                pool.wait_ge(var_done, 2 * b + 2)
                nc.gpsimd.tensor_tensor(rstd[:], var_eps[:], half[:], ALU.pow).then_inc(rstd_done, 1)
                pool.wait_ge(rstd_done, 2 * b + 1)
                nc.gpsimd.tensor_tensor(shift[:], neg_mean[:], rstd[:], ALU.mult).then_inc(rstd_done, 1)

            def sum_of(b):
                for e in range(ET):
                    pool.wait_ge(ln_done, ET * b + e + 1)
                    nc.gpsimd.tensor_tensor(sp_r[:, e, :], sp_r[:, e, :], sp_l[:, e, :], ALU.add).then_inc(sum_done, 1)

            def du_of(b):
                for e in range(ET):
                    pool.wait_ge(delta_done, ET * b + e + 1)
                    nc.gpsimd.tensor_tensor(du[:, e, :], delta[:, e, :], u[:, e, :], ALU.mult).then_inc(du_done, 1)
                pool.wait_ge(du_done, ET * (b + 1))

            rstd_of(0)
            sum_of(0)
            for b in range(B):
                def step(n, half_of):
                    row = b_all[:, n, :] if isinstance(n, int) else \
                        b_all[:, bass.ds(n, 1), :].rearrange("p o l -> p (o l)")
                    for e in range(0, ET, JOINT):
                        if b == 0 and isinstance(n, int) and n == 0:
                            pool.wait_ge(du_done, e + JOINT)
                        if b or not isinstance(n, int) or n >= 2:
                            pool.wait_ge(scan_done, n * ET + (SCANS * b - 2 * ET + e + JOINT))
                            pool.sem_inc(half_free, 1)
                        nc.gpsimd.tensor_tensor(drive[:, half_of, e:e + JOINT, :], du[:, e:e + JOINT, :],
                                                row.unsqueeze(1).broadcast_to([P, JOINT, L]), ALU.mult)\
                            .then_inc(drive_done, JOINT)

                def gap(q):
                    if q + 1 < len(GAPS):
                        pool.wait_ge(rows_in[q + 1], 16 * (b + 1))
                    if b + 1 < B and q == 1:
                        rstd_of(b + 1)
                    if b + 1 < B and q == 4:
                        sum_of(b + 1)
                        du_of(b + 1)

                pool.wait_ge(rows_in[0], 16 * (b + 1))
                segments(pool, b, step, gap)

        @block.scalar
        def _(act):
            act.wait_ge(consts, 16 * CONSTS)
            nc.scalar.activation(tanh_g[:], gates[:], ACT.Tanh).then_inc(tanh_done, 1)
            nc.scalar.activation(a_exp[:], a_log[:], ACT.Exp).then_inc(a_done, 1)
            act.wait_ge(a_done, 1)
            nc.scalar.mul(a_neg[:], a_exp[:], -1.0).then_inc(a_done, 1)
            act.wait_ge(a_done, 2)

            def u_of(b):
                if b:
                    act.wait_ge(du_done, ET * b)
                    act.wait_ge(turned_done, ADDS * (b - 1) + LT)
                for e in range(ET):
                    if b:
                        act.wait_ge(conv_done, ET * (b - 1) + e + 1)
                    else:
                        act.wait_ge(tap_added, TAPS * (e + 1))
                    src = work[e][:] if b else x_conv[:, e, :]
                    nc.scalar.activation(u[:, e, :], src, ACT.Silu, bias=cols[:, 0, e:e + 1]).then_inc(u_done, 1)

            def proj_of(b):
                act.wait_ge(xproj_done, b + 1)
                if b:
                    act.wait_ge(rows_out, 16 * b)
                    act.wait_ge(dt_done, ET * b)
                    act.wait_ge(cT_done, b)
                nc.scalar.activation(proj[:], work[0][0:64, :], ACT.Copy).then_inc(proj_done, 1)

            def norm_of(b):
                act.wait_ge(rstd_done, 2 * b + 2)
                if b:
                    act.wait_ge(zT_done, LT * b)
                for i in range(LT):
                    nc.scalar.activation(xn[:, i, :], xs[:, b % 2, i, :], ACT.Identity, bias=shift[:, i:i + 1],
                                         scale=rstd[:, i:i + 1]).then_inc(xn_done, 1)

            def relu_of(b):
                act.wait_ge(cT_done, b + 1)
                nc.scalar.activation(c_col[:, b % 2], work[1][:, 0:LT * 64].rearrange("p (t c) -> p t c", t=LT), ACT.Copy)\
                    .then_inc(c_done, 1)
                if b:
                    act.wait_ge(turned_done, ADDS * (b - 1) + LT)
                    act.wait_ge(delta_done, ET * b)
                for e in range(ET):
                    act.wait_ge(dt_done, ET * b + e + 1)
                    bank = work[(e + 2) % 4]
                    nc.scalar.activation(sp_y[:, e, :], bank[:], ACT.Abs, bias=cols[:, 1, e:e + 1]).then_inc(relu_done, 1)
                    nc.scalar.activation(sp_r[:, e, :], bank[:], ACT.Relu, bias=cols[:, 1, e:e + 1]).then_inc(relu_done, 1)

            def exp_of(b):
                act.wait_ge(relu_done, 2 * ET * (b + 1))
                nc.scalar.activation(sp_y[:], sp_y[:], ACT.Exp, scale=-1.0).then_inc(exp_done, 1)

            def ln_of(b):
                act.wait_ge(exp_done, b + 1)
                for e in range(ET):
                    nc.scalar.activation(sp_l[:, e, :], sp_y[:, e, :], ACT.Ln, bias=1.0).then_inc(ln_done, 1)

            def skip_of(b):
                act.wait_ge(soft, 2 * ET * b + 2 * ET)
                act.wait_ge(ln_done, ET * (b + 1))
                act.wait_ge(u_done, ET * (b + 1))
                for e in range(ET):
                    nc.scalar.activation(sp_y[:, e, :], u[:, e, :], ACT.Copy, scale=cols[:, 2, e:e + 1])\
                        .then_inc(skip_done, 1)

            def sz_of(b):
                if b:
                    act.wait_ge(mul_done, LT * b)
                for j in range(LT):
                    act.wait_ge(zT_done, LT * b + j + 1)
                    nc.scalar.activation(sz[:, j, :], work[j][:], ACT.Silu).then_inc(sz_done, 1)

            for e in range(ET):
                act.wait_ge(inproj_done, e + 1)
                nc.scalar.activation(x_pad[:, e, TAPS - 1:], work[e][:], ACT.Copy).then_inc(x_pad_done, 1)
            u_of(0)
            proj_of(0)
            act.wait_ge(taps_done, TAPS * CT)
            relu_of(0)
            exp_of(0)
            ln_of(0)
            norm_of(0)
            skip_of(0)
            for b in range(B):
                def step(n, half_of):
                    for e in range(ET):
                        scale = a_neg[:, e, n:n + 1] if isinstance(n, int) else a_neg[:, e, bass.ds(n, 1)]
                        if isinstance(n, int) and n == 0:
                            act.wait_ge(delta_done, ET * b + e + 1)
                        if b or not isinstance(n, int) or n >= 2:
                            act.wait_ge(scan_done, n * ET + (SCANS * b - 2 * ET + e + 1))
                        nc.scalar.activation(decay[:, half_of, e, 1:], delta[:, e, 1:], ACT.Exp, scale=scale)\
                            .then_inc(decay_done, 1)
                    if isinstance(n, int) and n == 0:
                        for i in range(LT):
                            act.wait_ge(turned_done, ADDS * b + i + 1)
                            if b and i == 0:
                                act.wait_ge(mul_done, LT * b)
                                act.wait_ge(x1_done, LT * b)
                            nc.scalar.activation(acc[:, i, :], turned[i][:], ACT.Copy).then_inc(add_done, 1)

                def gap(q):
                    if q == 0:
                        sz_of(b)
                    if b + 1 < B:
                        if q == 1:
                            u_of(b + 1)
                        if q == 2:
                            proj_of(b + 1)
                            norm_of(b + 1)
                        if q == 3:
                            relu_of(b + 1)
                            exp_of(b + 1)
                        if q == 4:
                            ln_of(b + 1)
                            skip_of(b + 1)

                segments(act, b, step, gap)

        @block.vector
        def _(dve):

            def stats_of(b):
                dve.wait_ge(x_in[b % 2], 16 * (b // 2 + 1))
                if b:
                    dve.wait_ge(xn_done, LT * b)
                for i in range(LT):
                    nc.vector.bn_stats(stat[:, i, :], xs[:, b % 2, i, :]).then_inc(stat_done, 1)
                for i in range(LT):
                    dve.wait_ge(stat_done, LT * b + i + 1)
                    nc.vector.bn_aggr(mv[:, i, :], stat[:, i, :]).then_inc(mv_done, 1)
                dve.wait_ge(mv_done, LT * (b + 1))
                nc.vector.tensor_scalar_mul(neg_mean[:], mv[:, :, 0], -1.0).then_inc(var_done, 1)
                nc.vector.tensor_scalar_add(var_eps[:], mv[:, :, 1], EPS).then_inc(var_done, 1)

            def delta_of(b):
                dve.wait_ge(exp_done, b + 1)
                base = 2 * ET * b
                for e in range(ET):
                    nc.vector.tensor_scalar(delta[:, e, :], sp_y[:, e, :], 1.0, 1.0, ALU.add, ALU.subtract).then_inc(soft, 1)
                for e in range(ET):
                    dve.wait_ge(soft, base + e + 1)
                    nc.vector.tensor_tensor(delta[:, e, :], sp_y[:, e, :], delta[:, e, :], ALU.subtract).then_inc(soft, 1)
                for e in range(ET):
                    dve.wait_ge(soft, base + ET + e + 1)
                    dve.wait_ge(sum_done, ET * b + e + 1)
                    nc.vector.tensor_tensor(delta[:, e, :], sp_r[:, e, :], delta[:, e, :], ALU.add).then_inc(delta_done, 1)
                    if b == 0:
                        dve.wait_ge(delta_done, e + 1)
                        nc.vector.tensor_tensor(du[:, e, :], delta[:, e, :], u[:, e, :], ALU.mult).then_inc(du_done, 1)

            def x1_of(b):
                dve.wait_ge(sz_done, LT * (b + 1))
                for i in range(LT):
                    dve.wait_ge(add_done, ADDS * b + LT * NS + i + 1)
                    nc.vector.tensor_tensor(acc[:, i, :], acc[:, i, :], sz[:, i, :], ALU.mult).then_inc(mul_done, 1)
                for i in range(LT):
                    dve.wait_ge(mul_done, LT * b + i + 1)
                    nc.vector.scalar_tensor_tensor(xs[:, b % 2, i, :], acc[:, i, :], tanh_g[:, 0:1], xs[:, b % 2, i, :],
                                                   ALU.mult, ALU.add).then_inc(x1_done, 1)

            dve.wait_ge(consts, 16 * CONSTS)
            dve.wait_ge(filled, 4)
            for e in range(ET):
                dve.wait_ge(x_pad_done, e + 1)
                for k in range(TAPS):
                    seen, tap = x_pad[:, e, k:k + L], cols[:, 3 + k, e:e + 1]
                    if k:
                        dve.wait_ge(tap_added, TAPS * e + k)
                        nc.vector.scalar_tensor_tensor(x_conv[:, e, :], seen, tap, x_conv[:, e, :], ALU.mult, ALU.add)\
                            .then_inc(tap_added, 1)
                    else:
                        nc.vector.tensor_scalar_mul(x_conv[:, e, :], seen, tap).then_inc(tap_added, 1)
            for k in range(TAPS):
                for c in range(CT):
                    nc.vector.tensor_tensor(w_tap[:, k, c, :], w_in[:, c, :], tap_rows[:, k, :], ALU.mult).then_inc(taps_done, 1)
            dve.wait_ge(tanh_done, 1)
            stats_of(0)
            delta_of(0)
            for b in range(B):
                def adds(n):
                    for i in range(LT):
                        dve.wait_ge(turned_done, (n + 1) * LT + (ADDS * b + i + 1))
                        col = c_col[:, b % 2, i, 48 + n:49 + n] if isinstance(n, int) else \
                            c_col[:, b % 2, i, bass.ds(n + 48, 1)]
                        if isinstance(n, int) and n == 0:
                            dve.wait_ge(add_done, ADDS * b + LT)
                        else:
                            dve.wait_ge(add_done, n * LT + (ADDS * b + i + 1))
                        nc.vector.scalar_tensor_tensor(acc[:, i, :], turned[i][:], col, acc[:, i, :],
                                                       ALU.mult, ALU.add).then_inc(add_done, 1)

                def step(n, half_of):
                    if isinstance(n, int) and n < 2:
                        if b:
                            dve.wait_ge(turned_done, ADDS * b - LT + LT * n)
                    else:
                        dve.wait_ge(turned_done, n * LT + ADDS * b)
                    for e in range(0, ET, JOINT):
                        dve.wait_ge(decay_done, n * ET + (SCANS * b + e + JOINT))
                        dve.wait_ge(drive_done, n * ET + (SCANS * b + e + JOINT))
                        dst, by, add = (m[:, half_of, e:e + JOINT, :].rearrange("p e l -> p (e l)") for m in (state, decay, drive))
                        nc.vector.tensor_tensor_scan(dst, by, add, 0.0, ALU.mult, ALU.add).then_inc(scan_done, JOINT)
                    if not isinstance(n, int) or n:
                        adds(n - 1)

                def gap(q):
                    if q == 4:
                        if b + 1 < B:
                            delta_of(b + 1)
                        adds(NS - 1)
                        x1_of(b)
                    if b + 1 < B:
                        if q == 0:
                            stats_of(b + 1)

                if b == 0:
                    dve.wait_ge(c_done, 1)
                else:
                    dve.wait_ge(c_done, b + 1)
                segments(dve, b, step, gap)

        @block.tensor
        def _(pe):
            pe.wait_ge(filled, 1)

            def conv_of(b, part):
                if part == 0:
                    pe.wait_ge(taps_done, TAPS * CT)
                    pe.wait_ge(ctx_in, 16 * (b + 2))
                share = ET * TAPS // CONV
                for n in range(part * share, (part + 1) * share):
                    e, k = n // TAPS, n % TAPS
                    if b and k == 0:
                        pe.wait_ge(sz_done, LT * (b - 1) + e + 1)
                    for c in range(CT):
                        mm = nc.tensor.matmul(work[e][:], w_tap[:, k, c, e * P:(e + 1) * P], ctx_pad[:, c, k:k + L],
                                              start=(k == 0 and c == 0), stop=(k == TAPS - 1 and c == CT - 1))
                    if k == TAPS - 1:
                        mm.then_inc(conv_done, 1)

            def xproj_of(b):
                for e in range(ET):
                    pe.wait_ge(u_done, ET * b + e + 1)
                    mm = nc.tensor.matmul(work[0][0:64, :], w_x[:, e, :], u[:, e, :], start=(e == 0), stop=(e == ET - 1))
                mm.then_inc(xproj_done, 1)

            def turn_proj(b):
                pe.wait_ge(proj_done, b + 1)
                for i in range(LT):
                    mm = nc.tensor.transpose(work[1][:, i * 64:(i + 1) * 64], proj[:, i * P:(i + 1) * P], ident[0:64, 0:64])
                mm.then_inc(cT_done, 1)
                for e in range(ET):
                    if e == 3:
                        pe.wait_ge(c_done, b + 1)
                    mm = nc.tensor.matmul(work[(e + 2) % 4][:], w_dt[:, e * P:(e + 1) * P], proj[0:DR, :], start=True, stop=True)
                    mm.then_inc(dt_done, 1)

            def turn_z(b):
                for j in range(LT):
                    pe.wait_ge(relu_done, 2 * ET * (b + 1))
                    pe.wait_ge(xn_done, LT * (b + 1))
                    for i in range(LT):
                        mm = nc.tensor.transpose(work[j][:, i * P:(i + 1) * P], xn[:, i, j * P:(j + 1) * P], ident[:])
                    mm.then_inc(zT_done, 1)

            def turn(src, n, b):
                for i in range(LT):
                    if b or not (isinstance(n, int) and n < 0):
                        pe.wait_ge(add_done, n * LT + (ADDS * b + i + 1))
                    for e in range(ET):
                        mm = nc.tensor.transpose(turned[i][:, e * P:(e + 1) * P], src(e)[:, i * P:(i + 1) * P], ident[:])
                    mm.then_inc(turned_done, 1)

            pe.wait_ge(ctx_in, 32)
            for e in range(ET):
                for c in range(CT):
                    mm = nc.tensor.matmul(work[e][:], w_in[:, c, e * P:(e + 1) * P], ctx_pad[:, c, TAPS - 1:],
                                          start=(c == 0), stop=(c == CT - 1))
                mm.then_inc(inproj_done, 1)
            pe.wait_ge(consts, 16 * CONSTS)
            pe.wait_ge(x_pad_done, 1)
            xproj_of(0)
            pe.wait_ge(x_pad_done, ET)
            turn_proj(0)
            for b in range(B):
                pe.wait_ge(skip_done, ET * (b + 1))
                turn(lambda e: sp_y[:, e, :], -1, b)
                for n in range(NS):
                    pe.wait_ge(scan_done, SCANS * b + ET * (n + 1))
                    turn(lambda e: state[:, n % 2, e, :], n, b)
                    if n == 0:
                        turn_z(b)
                    if b + 1 < B:
                        if n < CONV:
                            conv_of(b + 1, n)
                        if n == 9:
                            xproj_of(b + 1)
                        if n == 11:
                            turn_proj(b + 1)


def moe_block(nc, w, x1, x1s, xn_rows, expert_out, token_table, routes, scales, w_mix):
    ORDER = [NE, NE + 1] + list(range(NE))
    SPLIT_AT = {6: 2, 8: 3, 9: 4, 10: 5, 11: 6, 12: 7, 13: 8, 14: 9}
    TURN_AFTER = {0: 1, 2: 2, 4: 3}
    LOGITS_AFTER = {1: 1, 3: 2, 5: 3}
    RANK_AFTER = 6
    ST = SH // P
    SHARED = B * ST
    USES = DT + 1
    RANK_USE, TABLE_USE, ROWS_USE = USES * B, USES * B + 1, USES * B + 2
    MIXC = D // 8
    with ExitStack() as stack:
        def sb(name, shape, dt=F32):
            return stack.enter_context(nc.sbuf_tensor("m_" + name, shape, dt))

        def sem(name):
            return stack.enter_context(nc.semaphore("moe_" + name))

        ident = sb("ident", [P, P])
        lower = sb("lower", [P, P])
        gates = sb("gates", [P, 2])
        tanh_g = sb("tanh_g", [P, 2])
        scale_out = sb("scale_out", [P, 1])
        expert_no = sb("expert_no", [P, NE, TT])
        thresholds = sb("thresholds", [P, TT])
        tile_no = sb("tile_no", [P, RT])
        token_no = sb("token_no", [P, TT])
        half = sb("half", [P, TT])
        b_up = sb("b_up", [P, HT])
        pick16 = sb("pick16", [GR, GR * P], F16)
        small = sb("small", [P, DT * NE])
        b_down = sb("b_down", [GR, D])
        gw = sb("gw", [P, 2, DT * NE], F16)
        bd = sb("bd", [GR, 2, D], F16)
        lower16 = sb("lower16", [P, P], F16)
        ones16 = sb("ones16", [P, P], F16)
        raw_up = sb("raw_up", [P, 2, 2, DT * P])
        raw_dn = sb("raw_dn", [P, 2, 2, D])
        up = sb("up", [P, 2, HT, DT, P], F16)
        dn = sb("dn", [P, 2, HT, D], F16)
        xs = sb("xs", [P, B, LT, D])
        xn = sb("xn", [P, 2, LT, D])
        pick = xn[0:GR, 1].rearrange("p t d -> p (t d)")[:, 0:GR * P]
        stat = sb("stat", [P, TT, 6])
        mv = sb("mv", [P, TT, 2])
        var_eps = sb("var_eps", [P, TT])
        rstd = sb("rstd", [P, TT])
        xt = sb("xt", [P, 3, 2, DT, L], F16)
        logit = sb("logit", [P, TT, NE])
        top = sb("top", [P, TT, 8])
        top_at = sb("top_at", [P, TT, 8], U32)
        at = sb("at", [P, TT, 2])
        diff = sb("diff", [P, TT])
        e1 = sb("e1", [P, TT])
        ge = sb("ge", [P, 3, TT])
        scaled = sb("scaled", [P, 2, TT])
        chosen = sb("chosen", [P, 2, NE, TT])
        member = sb("member", [P, NE, TT])
        member16 = sb("member16", [P, NE, TT], F16)
        restart = sb("restart", [P, NE, TT])
        upto = sb("upto", [P, NE, TT])
        upto16 = sb("upto16", [P, NE, TT], F16)
        rank = sb("rank", [P, NE, TT])
        count = sb("count", [P, NE])
        filled = sb("filled", [P, NE, TT])
        tiles = sb("tiles", [P, NE])
        ends = sb("ends", [P, NE])
        base = sb("base", [P, NE])
        place = sb("place", [P, 2, NE, TT])
        where = sb("where", [P, 2, TT])
        where_u = sb("where_u", [P, 2, TT], U32)
        passed = sb("passed", [P, RT, NE])
        owner = sb("owner", [P, RT])
        owner_u = sb("owner_u", [P, RT], U32)
        no_token = sb("no_token", [RT, P])
        table = sb("table", [RT, P])
        table_u = sb("table_u", [P, RT], U32)
        hid = sb("hid", [P, 2, L])
        h16 = sb("h16", [P, 2, 2, L], F16)
        mix = sb("mix", [P, 2, FT, MIXC])
        bias_rows = xs[:, 1:3].rearrange("p b t d -> p (b t) d")
        bias_and_more = xs[:, 1:4].rearrange("p b t d -> p (b t) d")
        bank_up = [stack.enter_context(nc.psum_tensor(f"moe_up{i}", [P, 512], F32)) for i in range(2)]
        prep = [stack.enter_context(nc.psum_tensor(f"moe_prep{i}", [P, 512], F32)) for i in range(2)]
        bank_out = [stack.enter_context(nc.psum_tensor(f"moe_out{i}", [P, 512], F32)) for i in range(LT)]

        consts = sem("consts")
        x_in = [sem(f"x_in{b}") for b in range(B)]
        raw_in = [sem("raw_in_even"), sem("raw_in_odd")]
        split_hi = sem("split_hi")
        split_lo = sem("split_lo")
        small_hi = sem("small_hi")
        small_lo = sem("small_lo")
        filled_in = sem("filled_in")
        zeroed = sem("zeroed")
        tanh_done = sem("tanh_done")
        var_done = sem("var_done")
        rstd_done = sem("rstd_done")
        xn_done = sem("xn_done")
        xn_sent = [sem("xn_sent_even"), sem("xn_sent_odd")]
        xT_done = sem("xT_done")
        xT_hi = sem("xT_hi")
        prep_read = sem("prep_read")
        logit_done = sem("logit_done")
        diff_done = sem("diff_done")
        e1_done = sem("e1_done")
        member_done = sem("member_done")
        rank_done = sem("rank_done")
        where_done = sem("where_done")
        tables_done = sem("tables_done")
        scaled_done = sem("scaled_done")
        routes_out = sem("routes_out")
        scattered = sem("scattered")
        table_in = sem("table_in")
        up_done = sem("up_done")
        gelu_done = sem("gelu_done")
        hi_done = sem("hi_done")
        h_done = sem("h_done")
        down_done = sem("down_done")
        x1s_done = sem("x1s_done")
        x1s_out = sem("x1s_out")
        bias_in = sem("bias_in")
        rows_in = [sem("rows_in_even"), sem("rows_in_odd")]
        rows_turned = sem("rows_turned")
        rows_hi = sem("rows_hi")
        e_up = sem("e_up")
        e_gelu = sem("e_gelu")
        e_hi = sem("e_hi")
        e_lo = sem("e_lo")
        e_down = sem("e_down")
        out_free = sem("out_free")
        y_free = [sem("y_free_even"), sem("y_free_odd")]
        chain = sem("chain")
        mix_in = sem("mix_in")
        mixed = sem("mixed")
        mix_out = sem("mix_out")
        CONSTS = 12
        block = stack.enter_context(nc.Block())

        def over(ap, axis, shape):
            return ap.unsqueeze(axis).broadcast_to(shape)

        def experts(engine, first, count):
            cells = owner_u[0:1, first:first + count] if isinstance(first, int) else owner_u[0:1, bass.ds(first, count)]
            return nc.values_load_multi_w_load_instructions(
                cells, engines=[engine], min_val=0, max_val=NE,
                skip_runtime_bounds_check_because="an expert's number is a sum of NE comparisons, each zero or one")[1]

        def tiles_of(eng, body, engine=None):
            e = experts(engine, 0, 2) if engine else (None, None)
            body(0, 0, 0, (None, e[0]))
            body(1, 1, 0, (None, e[1]))
            with eng.Fori(0, (RT - 3) // 4) as i:
                e = experts(engine, i * 4, 6) if engine else (None,) * 6
                for k in range(2, 6):
                    body(i * 4 + k, k % 4, i * 2 + k // 2, (e[k - 2], e[k]))
            e = experts(engine, RT - 3, 3) if engine else (None,) * 3
            body(RT - 1, (RT - 1) % 4, (RT - 1) // 2, (e[0], e[2]))
            return e[1:]

        @block.sync
        def _(sp):
            def raw(k):
                j = ORDER[k]
                if k >= 2:
                    sp.wait_ge(split_hi, 2 * (k - 1))
                    sp.wait_ge(split_lo, 2 * (k - 1))
                sp.dma_start(raw_up[:, k % 2], w["w_up"][:, 2 * j:2 * j + 2, :]).then_inc(raw_in[k % 2], 16)
                sp.dma_start(raw_dn[:, k % 2], w["w_down"][:, 2 * j:2 * j + 2, :]).then_inc(raw_in[k % 2], 16)

            def send_xn(b):
                sp.wait_ge(xn_done, LT * (b + 1))
                sp.dma_start(xn_rows[b * L:(b + 1) * L].rearrange("(t p) d -> p t d", p=P), xn[:, b % 2])\
                    .then_inc(xn_sent[b % 2], 16)

            def send_x1s(b):
                sp.wait_ge(x1s_done, LT * (b + 1))
                sp.dma_start(x1s[b].rearrange("(t p) d -> p t d", p=P), xs[:, b]).then_inc(x1s_out, 16)

            sp.dma_start(xs[:, 0], x1[0].rearrange("(t p) d -> p t d", p=P)).then_inc(x_in[0], 16)
            for dst, src in ((ident, "ident"), (small, "gate_w"), (b_up, "b_up"), (pick, "pick"), (b_down, "b_down"),
                             (lower, "lower"), (expert_no, "expert_no"), (thresholds, "thresholds"), (tile_no, "tile_no"),
                             (token_no, "token_no")):
                sp.dma_start(dst if src == "pick" else dst[:], w[src]).then_inc(consts, 16)
            sp.dma_start(gates[:, 0:1], w["g_ffn"][0:1].partition_broadcast(P)).then_inc(consts, 16)
            sp.dma_start(gates[:, 1:2], w["g_ffn"][1:2].partition_broadcast(P)).then_inc(consts, 16)
            raw(0)
            raw(1)
            for b in range(1, B):
                sp.dma_start(xs[:, b], x1[b].rearrange("(t p) d -> p t d", p=P)).then_inc(x_in[b], 16)
            sp.wait_ge(filled_in, 4)
            sp.dma_start(token_table.rearrange("(t p) o -> t (p o)", p=P), no_token[:]).then_inc(zeroed, 16)
            send_xn(0)
            send_xn(1)
            raw(2)
            raw(3)
            for g in range(SHARED):
                if g + 1 in TURN_AFTER and g:
                    send_xn(TURN_AFTER[g + 1])
                if g in SPLIT_AT and SPLIT_AT[g] + 2 < len(ORDER):
                    raw(SPLIT_AT[g] + 2)
                if g % ST == 0 and g:
                    send_x1s(g // ST - 1)
            sp.wait_ge(x1s_out, 16 * (B - 1))
            sp.dma_start(bias_rows, w["b_down"][0:NE].partition_broadcast(P)).then_inc(bias_in, 16)
            sp.wait_ge(where_done, 1)
            sp.dma_start(routes, where_u[:]).then_inc(routes_out, 16)
            sp.wait_ge(scaled_done, 1)
            sp.dma_start(scales, scaled[:]).then_inc(routes_out, 16)
            sp.wait_ge(scattered, 16 * 2 * TT)
            sp.dma_start(table[:], token_table.rearrange("(t p) o -> t (p o)", p=P)).then_inc(table_in, 16)
            send_x1s(B - 1)

            def send_y(t, ring, n, e):
                side = ring % 2
                sp.wait_ge(out_free, t + 3)
                at_tile = expert_out[t] if isinstance(t, int) else expert_out[bass.ds(t, 1)].rearrange("o p d -> (o p) d")
                sp.dma_start(at_tile, xs[:, 0, side, :]).then_inc(y_free[side], 16)

            sp.wait_ge(x1s_out, 16 * B)
            sp.sem_inc(y_free[0], 16)
            sp.sem_inc(y_free[1], 16)
            tiles_of(sp, send_y)
            sp.wait_ge(y_free[0], 16 * ((RT + 1) // 2) + 16)
            sp.wait_ge(y_free[1], 16 * (RT // 2) + 16)
            sp.wait_ge(routes_out, 32)

        @block.gpsimd
        def _(pool):
            STAGES = 4
            GROUPS = D // MIXC

            def load_mix(c):
                if c:
                    pool.wait_ge(mixed, 2 * STAGES * c)
                pool.dma_start(mix[:, c % 2], w["w_out"][:, :, c * MIXC:(c + 1) * MIXC]).then_inc(mix_in, 16)

            def mix_stage(c, stage):
                if stage == 0:
                    pool.wait_ge(mix_in, 16 * (c + 1))
                    if c:
                        pool.wait_ge(mix_out, 16 * c)
                else:
                    pool.wait_ge(mixed, 2 * (STAGES * c + stage))
                span, side = 1 << stage, (c + stage) % 2
                src = mix[:, side].rearrange("p (g two s) d -> p g two (s d)", two=2, s=span)
                dst = mix[:, 1 - side].rearrange("p (g two s) d -> p g two (s d)", two=2, s=span)
                for half_of, op in ((0, ALU.add), (1, ALU.subtract)):
                    nc.gpsimd.tensor_tensor(dst[:, :, half_of, :], src[:, :, 0, :], src[:, :, 1, :], op).then_inc(mixed, 1)

            def store_mix(c):
                pool.wait_ge(mixed, 2 * STAGES * (c + 1))
                pool.dma_start(w_mix[:, :, c * MIXC:(c + 1) * MIXC], mix[:, c % 2]).then_inc(mix_out, 16)

            nc.gpsimd.memset(half[:], -0.5).then_inc(filled_in, 1)
            nc.gpsimd.memset(restart[:], 1.0).then_inc(filled_in, 1)
            nc.gpsimd.memset(ones16[:], 1.0).then_inc(filled_in, 1)
            nc.gpsimd.memset(no_token[:], 0.0).then_inc(filled_in, 1)
            pool.wait_ge(filled_in, 4)
            nc.gpsimd.memset(restart[:, :, 0], 0.0).then_inc(filled_in, 1)
            load_mix(0)
            pool.wait_ge(var_done, 1)
            nc.gpsimd.tensor_tensor(rstd[:, 0:LT], var_eps[:, 0:LT], half[:, 0:LT], ALU.pow).then_inc(rstd_done, 1)
            pool.wait_ge(var_done, 2)
            nc.gpsimd.tensor_tensor(rstd[:, LT:2 * LT], var_eps[:, LT:2 * LT], half[:, LT:2 * LT], ALU.pow).then_inc(rstd_done, 1)
            BEFORE = 3
            BESIDE = (RT - 2) // (GROUPS - BEFORE)
            for c in range(BEFORE):
                for stage in range(STAGES):
                    mix_stage(c, stage)
                store_mix(c)
                load_mix(c + 1)
                if c == 0:
                    pool.wait_ge(var_done, 3)
                    nc.gpsimd.tensor_tensor(rstd[:, 2 * LT:TT], var_eps[:, 2 * LT:TT], half[:, 2 * LT:TT], ALU.pow).then_inc(rstd_done, 1)
            pool.wait_ge(where_done, 1)
            pool.wait_ge(zeroed, 16)
            for k in (0, 1):
                for t in range(TT):
                    pool.indirect_dma_start(token_table, bass.IndirectOffsetOnAxis(where_u[:, k, t:t + 1], 0),
                                            token_no[:, t:t + 1], None).then_inc(scattered, 16)
            pool.wait_ge(tables_done, 2)
            pool.wait_ge(xn_sent[0], 16 * (B // 2))
            pool.wait_ge(xn_sent[1], 16 * (B // 2))
            for t in range(RT):
                if t >= 2:
                    pool.wait_ge(rows_in[t % 2], 16 * (t // 2))
                if t >= 4:
                    pool.wait_ge(rows_turned, t - 3)
                pool.indirect_dma_start(xn[:, t % 2, t // 2 % 2, :], None, xn_rows,
                                        bass.IndirectOffsetOnAxis(table_u[:, t:t + 1], 0)).then_inc(rows_in[t % 2], 16)
                c, turn = BEFORE + (t - 2) // BESIDE, (t - 2) % BESIDE
                if t >= 2 and c < GROUPS:
                    if turn < STAGES:
                        mix_stage(c, turn)
                    if turn == STAGES:
                        store_mix(c)
                    if turn == STAGES + 1 and c + 1 < GROUPS:
                        load_mix(c + 1)
            pool.wait_ge(mix_out, 16 * GROUPS)

        @block.scalar
        def _(act):
            def split(k):
                j = ORDER[k]
                act.wait_ge(raw_in[k % 2], 32 * (k // 2 + 1))
                nc.scalar.activation(up[:, 0, 2 * j:2 * j + 2].rearrange("p t c q -> p t (c q)"), raw_up[:, k % 2], ACT.Copy, scale=WS)\
                    .then_inc(split_hi, 1)
                nc.scalar.activation(dn[:, 0, 2 * j:2 * j + 2], raw_dn[:, k % 2], ACT.Copy, scale=WS).then_inc(split_hi, 1)

            def turn_hi(b):
                for c in range(DT):
                    act.wait_ge(xT_done, DT * b + c + 1)
                    if b >= 3 and c == 0:
                        act.wait_ge(up_done, ST * (b - 2))
                    nc.scalar.activation(xt[:, b % 3, 0, c, :], prep[(USES * b + c) % 2][:], ACT.Copy).then_inc(xT_hi, 1)

            def shared(g):
                act.wait_ge(up_done, g + 1)
                if g >= 2:
                    act.wait_ge(h_done, g - 1)
                h = NE * 2 + g % ST
                nc.scalar.activation(hid[:, g % 2, :], bank_up[g % 2][:], ACT.Gelu, bias=b_up[:, h:h + 1], scale=1.0 / WS)\
                    .then_inc(gelu_done, 1)
                act.wait_ge(gelu_done, g + 1)
                if g >= 2:
                    act.wait_ge(down_done, g - 1)
                nc.scalar.activation(h16[:, g % 2, 0, :], hid[:, g % 2, :], ACT.Copy).then_inc(hi_done, 1)

            act.wait_ge(consts, 16 * CONSTS)
            nc.scalar.activation(tanh_g[:], gates[:], ACT.Tanh).then_inc(tanh_done, 1)
            nc.scalar.activation(gw[:, 0, :], small[:], ACT.Copy, scale=WS).then_inc(small_hi, 1)
            nc.scalar.activation(bd[:, 0, :], b_down[:], ACT.Copy, scale=WS).then_inc(small_hi, 1)
            nc.scalar.activation(pick16[:], pick, ACT.Copy).then_inc(small_hi, 1)
            nc.scalar.activation(lower16[:], lower[:], ACT.Copy).then_inc(small_hi, 1)
            turn_hi(0)
            split(0)
            split(1)
            for g in range(SHARED):
                shared(g)
                if g - 1 in TURN_AFTER:
                    turn_hi(TURN_AFTER[g - 1])
                if g in SPLIT_AT:
                    split(SPLIT_AT[g])
                if g == RANK_AFTER + 1:
                    act.wait_ge(diff_done, 1)
                    nc.scalar.activation(e1[:], diff[:], ACT.Exp, scale=1.0 / WS).then_inc(e1_done, 1)

            def rows_split(t, side):
                act.wait_ge(rows_turned, t + 1)
                if not isinstance(t, int) or t >= 2:
                    act.wait_ge(e_up, t - 1)
                nc.scalar.activation(xt[:, side, 0, :, 0:P], prep[side][:].rearrange("p (c q) -> p c q", q=P), ACT.Copy)\
                    .then_inc(rows_hi, 1)

            def routed(t, ring, n, e):
                side = ring % 2
                if not isinstance(t, int) or t + 1 < RT:
                    rows_split(t + 1, 1 - side)
                act.wait_ge(e_up, t + 1)
                if not isinstance(t, int) or t >= 2:
                    act.wait_ge(e_lo, t - 1)
                for m in (0, 1):
                    ins = nc.scalar.activation(hid[:, side, m * P:(m + 1) * P], bank_up[side][:, m * P:(m + 1) * P], ACT.Gelu,
                                               bias=b_up[:, bass.ds(e[1] * 2 + m, 1)], scale=1.0 / WS)
                ins.then_inc(e_gelu, 1)
                act.wait_ge(e_gelu, t + 1)
                if not isinstance(t, int) or t >= 2:
                    act.wait_ge(e_down, t - 1)
                nc.scalar.activation(h16[:, side, 0, 0:2 * P], hid[:, side, 0:2 * P], ACT.Copy).then_inc(e_hi, 1)

            act.wait_ge(tables_done, 1)
            act.wait_ge(h_done, SHARED)
            act.wait_ge(down_done, SHARED)
            rows_split(0, 0)
            tiles_of(act, routed, mybir.EngineType.Activation)

        @block.vector
        def _(dve):
            links = [0]

            def link(ins):
                links[0] += 1
                ins.then_inc(chain, 1)
                dve.wait_ge(chain, links[0])

            def split(k):
                j = ORDER[k]
                dve.wait_ge(split_hi, 2 * k + 2)
                nc.vector.scalar_tensor_tensor(up[:, 1, 2 * j:2 * j + 2].rearrange("p t c q -> p t (c q)"), raw_up[:, k % 2], WS,
                                               up[:, 0, 2 * j:2 * j + 2].rearrange("p t c q -> p t (c q)"),
                                               ALU.mult, ALU.subtract).then_inc(split_lo, 1)
                nc.vector.scalar_tensor_tensor(dn[:, 1, 2 * j:2 * j + 2], raw_dn[:, k % 2], WS, dn[:, 0, 2 * j:2 * j + 2],
                                               ALU.mult, ALU.subtract).then_inc(split_lo, 1)

            def stats_of(b):
                dve.wait_ge(x_in[b], 16)
                for i in range(LT):
                    ins = nc.vector.bn_stats(stat[:, LT * b + i, :], xs[:, b, i, :])
                link(ins)
                for i in range(LT):
                    ins = nc.vector.bn_aggr(mv[:, LT * b + i, :], stat[:, LT * b + i, :])
                link(ins)

            def norm_of(b):
                dve.wait_ge(rstd_done, min(b, 2) + 1)
                if b == 1:
                    dve.wait_ge(small_hi, 3)
                if b >= 2:
                    dve.wait_ge(xT_done, DT * (b - 1))
                    dve.wait_ge(xn_sent[b % 2], 16)
                for i in range(LT):
                    t = LT * b + i
                    nc.vector.tensor_scalar(xn[:, b % 2, i, :], xs[:, b, i, :], mv[:, t, 0:1], rstd[:, t:t + 1],
                                            ALU.subtract, ALU.mult).then_inc(xn_done, 1)

            def turn_lo(b):
                for c in range(DT):
                    dve.wait_ge(xT_hi, DT * b + c + 1)
                    nc.vector.tensor_tensor(xt[:, b % 3, 1, c, :], prep[(USES * b + c) % 2][:], xt[:, b % 3, 0, c, :], ALU.subtract)\
                        .then_inc(prep_read, 1)

            def route(b):
                dve.wait_ge(logit_done, b + 1)
                rows = slice(LT * b, LT * (b + 1))
                nc.vector.tensor_copy(logit[:, rows].rearrange("p t e -> p (t e)"), prep[(USES * b + DT) % 2][:, 0:LT * NE])\
                    .then_inc(prep_read, 1)
                dve.wait_ge(prep_read, USES * (b + 1))
                for t in range(LT * b, LT * (b + 1)):
                    ins = nc.vector.max(top[:, t, :], logit[:, t, :])
                link(ins)
                for t in range(LT * b, LT * (b + 1)):
                    ins = nc.vector.max_index(top_at[:, t, :], top[:, t, :], logit[:, t, :])
                link(ins)

            def members():
                nc.vector.tensor_tensor(diff[:], top[:, :, 1], top[:, :, 0], ALU.subtract).then_inc(diff_done, 1)
                link(nc.vector.tensor_copy(at[:], top_at[:, :, 0:2]))
                for k in (0, 1):
                    ins = nc.vector.tensor_tensor(chosen[:, k], expert_no[:], over(at[:, :, k], 1, [P, NE, TT]), ALU.is_equal)
                link(ins)
                link(nc.vector.tensor_tensor(member[:], chosen[:, 0], chosen[:, 1], ALU.add))
                nc.vector.tensor_copy(member16[:], member[:]).then_inc(member_done, 1)
                dve.wait_ge(filled_in, 5)
                link(nc.vector.tensor_tensor_scan(upto[:].rearrange("p e t -> p (e t)"), restart[:].rearrange("p e t -> p (e t)"),
                                                  member[:].rearrange("p e t -> p (e t)"), 0.0, ALU.mult, ALU.add))
                nc.vector.tensor_copy(upto16[:], upto[:]).then_inc(member_done, 1)

            def places():
                dve.wait_ge(rank_done, 1)
                nc.vector.tensor_copy(rank[:].rearrange("p e t -> p (e t)"), prep[RANK_USE % 2][:, 0:NE * TT])
                nc.vector.tensor_copy(count[:], prep[RANK_USE % 2][:, NE * TT:NE * TT + NE]).then_inc(prep_read, 1)
                dve.wait_ge(prep_read, RANK_USE + 1)
                link(nc.vector.tensor_tensor(filled[:], over(count[:], 2, [P, NE, TT]), over(thresholds[:], 1, [P, NE, TT]), ALU.is_gt))
                link(nc.vector.reduce_sum(tiles[:], filled[:], AX_X))
                link(nc.vector.tensor_tensor_scan(ends[:], restart[:, 0:NE, 1], tiles[:], 0.0, ALU.mult, ALU.add))
                link(nc.vector.tensor_tensor(base[:], ends[:], tiles[:], ALU.subtract))
                link(nc.vector.scalar_tensor_tensor(rank[:], over(base[:], 2, [P, NE, TT]), float(P), rank[:], ALU.mult, ALU.add))
                for k in (0, 1):
                    ins = nc.vector.tensor_tensor(place[:, k], chosen[:, k], rank[:], ALU.mult)
                link(ins)
                for k in (0, 1):
                    ins = nc.vector.reduce_sum(where[:, k, :], place[:, k].rearrange("p e t -> p t e"), AX_X)
                link(ins)
                nc.vector.tensor_copy(where_u[:], where[:]).then_inc(where_done, 1)
                link(nc.vector.tensor_tensor(passed[:], over(ends[:], 1, [P, RT, NE]), over(tile_no[:], 2, [P, RT, NE]), ALU.is_le))
                link(nc.vector.reduce_sum(owner[:], passed[:], AX_X))
                nc.vector.tensor_copy(owner_u[:], owner[:]).then_inc(tables_done, 1)

            def token_gates():
                dve.wait_ge(e1_done, 1)
                link(nc.vector.tensor_scalar_add(ge[:, 0, :], e1[:], 1.0))
                link(nc.vector.reciprocal(ge[:, 1, :], ge[:, 0, :]))
                link(nc.vector.tensor_tensor(ge[:, 2, :], e1[:], ge[:, 1, :], ALU.mult))
                nc.vector.tensor_scalar_mul(scaled[:], ge[:, 1:3, :], scale_out[:]).then_inc(scaled_done, 1)

            def shared_lo(g):
                dve.wait_ge(hi_done, g + 1)
                nc.vector.tensor_tensor(h16[:, g % 2, 1, :], hid[:, g % 2, :], h16[:, g % 2, 0, :], ALU.subtract).then_inc(h_done, 1)

            def x1s_of(b):
                dve.wait_ge(down_done, ST * (b + 1))
                for i in range(LT):
                    nc.vector.scalar_tensor_tensor(xs[:, b, i, :], bank_out[i][:], scale_out[:], xs[:, b, i, :],
                                                   ALU.mult, ALU.add).then_inc(x1s_done, 1)

            stats_of(0)
            nc.vector.tensor_scalar_add(var_eps[:, 0:LT], mv[:, 0:LT, 1], EPS).then_inc(var_done, 1)
            norm_of(0)
            dve.wait_ge(consts, 16 * CONSTS)
            dve.wait_ge(tanh_done, 1)
            link(nc.vector.tensor_scalar_mul(scale_out[:], tanh_g[:, 0:1], 1.0 / WS))
            dve.wait_ge(small_hi, 2)
            nc.vector.scalar_tensor_tensor(gw[:, 1, :], small[:], WS, gw[:, 0, :], ALU.mult, ALU.subtract).then_inc(small_lo, 1)
            nc.vector.scalar_tensor_tensor(bd[:, 1, :], b_down[:], WS, bd[:, 0, :], ALU.mult, ALU.subtract).then_inc(small_lo, 1)
            turn_lo(0)
            split(0)
            split(1)
            stats_of(1)
            nc.vector.tensor_scalar_add(var_eps[:, LT:2 * LT], mv[:, LT:2 * LT, 1], EPS).then_inc(var_done, 1)
            route(0)
            norm_of(1)
            for g in range(SHARED):
                shared_lo(g)
                if g < 2:
                    stats_of(2 + g)
                if g == 1:
                    nc.vector.tensor_scalar_add(var_eps[:, 2 * LT:TT], mv[:, 2 * LT:TT, 1], EPS).then_inc(var_done, 1)
                if g % ST == 0 and g:
                    x1s_of(g // ST - 1)
                if g - 1 in TURN_AFTER:
                    turn_lo(TURN_AFTER[g - 1])
                if g - 1 in LOGITS_AFTER:
                    route(LOGITS_AFTER[g - 1])
                    if g == RANK_AFTER:
                        members()
                if g + 1 in TURN_AFTER and g:
                    norm_of(TURN_AFTER[g + 1])
                if g == RANK_AFTER + 1:
                    places()
                    token_gates()
                if g in SPLIT_AT:
                    split(SPLIT_AT[g])
            dve.wait_ge(rank_done, 2)
            nc.vector.tensor_copy(table_u[:], prep[TABLE_USE % 2][:, 0:RT]).then_inc(prep_read, 1)
            dve.wait_ge(prep_read, TABLE_USE + 1)
            dve.sem_inc(tables_done, 1)
            x1s_of(B - 1)
            dve.wait_ge(x1s_done, LT * B)
            dve.sem_inc(out_free, 2)

            def rows_split(t, side):
                dve.wait_ge(rows_hi, t + 1)
                nc.vector.tensor_tensor(xt[:, side, 1, :, 0:P], prep[side][:].rearrange("p (c q) -> p c q", q=P),
                                        xt[:, side, 0, :, 0:P], ALU.subtract).then_inc(prep_read, 1)

            def y_of(t, side, n, e):
                dve.wait_ge(e_down, t + 1)
                dve.wait_ge(y_free[side], n * 16 + 16)
                bias = bias_and_more[:, bass.ds(e, 1), :].rearrange("p o d -> p (o d)")
                nc.vector.scalar_tensor_tensor(xs[:, 0, side, :], bias, WS, bank_out[side][:], ALU.mult, ALU.add).then_inc(out_free, 1)

            def routed(t, ring, n, e):
                side = ring % 2
                if not isinstance(t, int) or t + 1 < RT:
                    rows_split(t + 1, 1 - side)
                if not isinstance(t, int) or t >= 2:
                    y_of(t - 2, side, n - 1, e[0])
                dve.wait_ge(e_hi, t + 1)
                nc.vector.tensor_tensor(h16[:, side, 1, 0:2 * P], hid[:, side, 0:2 * P], h16[:, side, 0, 0:2 * P], ALU.subtract)\
                    .then_inc(e_lo, 1)

            rows_split(0, 0)
            dve.wait_ge(bias_in, 16)
            last = tiles_of(dve, routed, mybir.EngineType.DVE)
            for t in (RT - 2, RT - 1):
                y_of(t, t % 2, t // 2, last[t - RT + 2])

        @block.tensor
        def _(pe):
            def bank(use):
                if use >= 2:
                    pe.wait_ge(prep_read, use - 1)
                return prep[use % 2]

            def turn(b):
                pe.wait_ge(xn_done, LT * (b + 1))
                for c in range(DT):
                    dst = bank(USES * b + c)
                    for i in range(LT):
                        mm = nc.tensor.transpose(dst[:, i * P:(i + 1) * P], xn[:, b % 2, i, c * P:(c + 1) * P], ident[:])
                    mm.then_inc(xT_done, 1)

            def logits(b):
                dst = bank(USES * b + DT)
                pe.wait_ge(prep_read, USES * b + DT)
                pe.wait_ge(small_lo, 2)
                for i in range(LT):
                    n = 0
                    for c in range(DT):
                        for xh, wh in ((0, 0), (0, 1), (1, 0)):
                            mm = nc.tensor.matmul(dst[:, i * NE:(i + 1) * NE], xt[:, b % 3, xh, c, i * P:(i + 1) * P],
                                                  gw[:, wh, c * NE:(c + 1) * NE], start=(n == 0), stop=(n == 3 * DT - 1))
                            n += 1
                mm.then_inc(logit_done, 1)

            def ranks():
                pe.wait_ge(member_done, 2)
                pe.wait_ge(small_hi, 4)
                pe.wait_ge(filled_in, 5)
                dst = bank(RANK_USE)
                flat = "p e t -> p (e t)"
                nc.tensor.matmul(dst[:, 0:NE * TT], lower16[:], member16[:].rearrange(flat), start=True, stop=False)
                nc.tensor.matmul(dst[:, 0:NE * TT], ones16[:], upto16[:].rearrange(flat), start=False, stop=True)
                nc.tensor.matmul(dst[:, NE * TT:NE * TT + NE], ones16[:], upto16[:, :, TT - 1], start=True, stop=True).then_inc(rank_done, 1)

            def shared_up(g):
                b = g // ST
                if g < ST:
                    pe.wait_ge(split_lo, g // 2 * 2 + 1)
                pe.wait_ge(prep_read, USES * b + DT)
                if g >= 2:
                    pe.wait_ge(gelu_done, g - 1)
                n = 0
                for c in range(DT):
                    for wh, xh in ((0, 0), (0, 1), (1, 0)):
                        mm = nc.tensor.matmul(bank_up[g % 2][:], up[:, wh, NE * 2 + g % ST, c, :], xt[:, b % 3, xh, c, :],
                                              start=(n == 0), stop=(n == 3 * DT - 1))
                        n += 1
                mm.then_inc(up_done, 1)

            def shared_down(g):
                b = g // ST
                if g % ST == 0:
                    if g == 0:
                        pe.wait_ge(small_hi, 3)
                    else:
                        pe.wait_ge(x1s_done, LT * b)
                    for i in range(LT):
                        for hl in (0, 1):
                            nc.tensor.matmul(bank_out[i][:], pick16[:, NE * P:(NE + 1) * P], bd[:, hl, :], start=(hl == 0), stop=False)
                pe.wait_ge(h_done, g + 1)
                if g < ST:
                    pe.wait_ge(split_lo, g // 2 * 2 + 2)
                for i in range(LT):
                    for n, (hh, wh) in enumerate(((0, 0), (0, 1), (1, 0))):
                        mm = nc.tensor.matmul(bank_out[i][:], h16[:, g % 2, hh, i * P:(i + 1) * P], dn[:, wh, NE * 2 + g % ST, :],
                                              start=False, stop=(g % ST == ST - 1 and n == 2))
                mm.then_inc(down_done, 1)

            pe.wait_ge(consts, 16 * CONSTS)
            turn(0)
            logits(0)
            shared_up(0)
            for g in range(SHARED):
                if g + 1 < SHARED:
                    shared_up(g + 1)
                shared_down(g)
                if g in TURN_AFTER:
                    turn(TURN_AFTER[g])
                if g in LOGITS_AFTER:
                    logits(LOGITS_AFTER[g])
                if g == RANK_AFTER:
                    ranks()
            pe.wait_ge(table_in, 16)
            nc.tensor.transpose(bank(TABLE_USE)[:, 0:RT], table[:], ident[0:RT, 0:RT]).then_inc(rank_done, 1)

            def rows_turn(t, ring, n):
                side = ring % 2
                pe.wait_ge(rows_in[side], n * 16 + 16)
                pe.wait_ge(prep_read, t + (ROWS_USE - 1))
                for c in range(DT):
                    mm = nc.tensor.transpose(prep[side][:, c * P:(c + 1) * P], xn[:, side, ring // 2, c * P:(c + 1) * P], ident[:])
                mm.then_inc(rows_turned, 1)

            def up_products(side, e):
                for m in (0, 1):
                    n = 0
                    for c in range(DT):
                        for wh, xh in ((0, 0), (0, 1), (1, 0)):
                            wt = up[:, wh, bass.ds(e * 2 + m, 1), c, :].rearrange("p o q -> p (o q)")
                            yield bank_up[side][:, m * P:(m + 1) * P], wt, xt[:, side, xh, c, 0:P], n == 0, n == 3 * DT - 1
                            n += 1

            def down_products(side, e):
                for m in (0, 1):
                    for n, (hh, wh) in enumerate(((0, 0), (0, 1), (1, 0))):
                        wt = dn[:, wh, bass.ds(e * 2 + m, 1), :].rearrange("p o d -> p (o d)")
                        yield bank_out[side][:], h16[:, side, hh, m * P:(m + 1) * P], wt, m == 0 and n == 0, m == 1 and n == 2

            def product(dst, lhs, rhs, start, stop):
                return nc.tensor.matmul(dst, lhs, rhs, start=start, stop=stop)

            def routed(t, ring, n, e):
                side, early = ring % 2, isinstance(t, int) and t < 2
                if not isinstance(t, int) or t + 1 < RT:
                    rows_turn(t + 1, (ring + 1) % 4, n + side)
                pe.wait_ge(prep_read, t + (ROWS_USE + 1))
                if not early:
                    pe.wait_ge(e_gelu, t - 1)
                    pe.wait_ge(e_lo, t - 1)
                    pe.wait_ge(out_free, t - 1)
                ups = list(up_products(side, e[1]))
                downs = [] if early else list(down_products(side, e[0]))
                share = 5
                for k in range(0, len(ups), share):
                    if downs:
                        product(*downs[k // share])
                    for args in ups[k:k + share]:
                        mm = product(*args)
                mm.then_inc(e_up, 1)
                if downs:
                    product(*downs[-1]).then_inc(e_down, 1)

            def last_down(t, side, e):
                pe.wait_ge(e_lo, t + 1)
                pe.wait_ge(out_free, t + 1)
                for args in down_products(side, e):
                    mm = product(*args)
                mm.then_inc(e_down, 1)

            pe.wait_ge(tables_done, 1)
            pe.wait_ge(split_lo, 2 * len(ORDER))
            pe.wait_ge(gelu_done, SHARED)
            rows_turn(0, 0, 0)
            last = tiles_of(pe, routed, mybir.EngineType.PE)
            for t in (RT - 2, RT - 1):
                last_down(t, t % 2, last[t - RT + 2])




def ffn_block(nc, w, ctx_t, x1s, expert_out, routes, scales, w_mix, out):
    EXPERTS_AT, NORM2_AT, QK_AT, ENERGY_AT, EXP_AT, XQ_AT, PROBT_AT, PRODUCT_AT, NORM3_AT, XT_AT = 0, 1, 1, 2, 4, 5, 7, 9, 10, 12
    PROBS = 4096.0
    MIX = WS * float(H) ** -0.5
    USES = 11
    with ExitStack() as stack:
        def sb(name, shape, dt=F32):
            return stack.enter_context(nc.sbuf_tensor("f_" + name, shape, dt))

        def sem(name):
            return stack.enter_context(nc.semaphore("ffn_" + name))

        ident = sb("ident", [P, P])
        hada = sb("hada", [P, P])
        gates = sb("gates", [P, 2])
        tanh_g = sb("tanh_g", [P, 2])
        scale_x = sb("scale_x", [P, 1])
        scale_out = sb("scale_out", [P, 1])
        where = sb("where", [P, 2, TT], U32)
        gate = sb("gate", [P, 2, TT])
        half = sb("half", [P, LT])
        w_q = sb("w_q", [P, CT, P])
        w_k = sb("w_k", [P, CT, P])
        b_qk = sb("b_qk", [P, 2])
        raw = sb("raw", [P, 2, 2, DT * P])
        raw_mix = sb("raw_mix", [P, 4, D])
        wg = sb("wg", [P, 2, FT, DT, P], F16)
        wl = sb("wl", [P, 2, FT, DT, P], F16)
        wo = sb("wo", [P, 2, FT, D], F16)
        ctxs = sb("ctxs", [P, CT, L])
        qk = sb("qk", [P, 2, L])
        xs = sb("xs", [P, 2, LT, D])
        xn = sb("xn", [P, LT, D])
        stat = sb("stat", [P, LT, 6])
        mv = sb("mv", [P, LT, 2])
        var_eps = sb("var_eps", [P, LT])
        rstd = sb("rstd", [P, LT])
        neg_max = sb("neg_max", [P, LT])
        total = sb("total", [P, LT])
        inv = sb("inv", [P, LT])
        energy = sb("energy", [P, LT, L])
        prob = sb("prob", [P, LT, L])
        probT = sb("probT", [P, 2, LT, L], F16)
        second = sb("second", [P, LT, D])
        xq = second[:].rearrange("p i d -> p (i d)").bitcast(F16).rearrange("p (h c l) -> p h c l", h=2, c=DT)
        xt = sb("xt", [P, 2, 2, DT, L], F16)
        sg = sb("sg", [P, 2, L])
        hid = sb("hid", [P, 2, L])
        h16 = sb("h16", [P, 2, 2, L], F16)
        bank_g = stack.enter_context(nc.psum_tensor("ffn_g", [P, 512], F32))
        bank_u = stack.enter_context(nc.psum_tensor("ffn_u", [P, 512], F32))
        prep = [stack.enter_context(nc.psum_tensor(f"ffn_prep{i}", [P, 512], F32)) for i in range(2)]
        bank_out = [stack.enter_context(nc.psum_tensor(f"ffn_out{i}", [P, 512], F32)) for i in range(LT)]

        consts = sem("consts")
        x_in = [sem("x_in_even"), sem("x_in_odd")]
        ctx_in = sem("ctx_in")
        routes_in = sem("routes_in")
        y_in = [sem(f"y_in{i}") for i in range(LT)]
        x2_done = sem("x2_done")
        raw_in = [sem("raw_in_even"), sem("raw_in_odd")]
        mix_in = [sem(f"mix_in{i}") for i in range(4)]
        mix_done = sem("mix_done")
        mix_hi = sem("mix_hi")
        mix_lo = sem("mix_lo")
        split_hi = sem("split_hi")
        split_lo = sem("split_lo")
        half_set = sem("half_set")
        tanh_done = sem("tanh_done")
        var_done = sem("var_done")
        rstd_done = sem("rstd_done")
        xn_done = sem("xn_done")
        filled = [sem("filled0"), sem("filled1")]
        qk_done = sem("qk_done")
        max_done = sem("max_done")
        energy_done = sem("energy_done")
        exp_done = sem("exp_done")
        prob_done = sem("prob_done")
        xq_hi = sem("xq_hi")
        xq_done = sem("xq_done")
        probT_hi = sem("probT_hi")
        probT_done = sem("probT_done")
        x3_done = sem("x3_done")
        xT_hi = sem("xT_hi")
        xT_lo = sem("xT_lo")
        g_done = sem("g_done")
        u_done = sem("u_done")
        silu_done = sem("silu_done")
        hid_done = sem("hid_done")
        hi_done = sem("hi_done")
        h_done = sem("h_done")
        down_done = sem("down_done")
        out_done = sem("out_done")
        out_sent = [sem("out_sent_even"), sem("out_sent_odd")]
        chain = sem("chain")
        CONSTS = 8
        Q, K, ENERGY, XQ, PROBT, PRODUCT, XT = 0, 1, 2, 6, 10, 14, 18
        block = stack.enter_context(nc.Block())

        def bank(use):
            return prep[use % 2]

        def full(eng, use, b):
            eng.wait_ge(filled[use % 2], USES * b + use // 2 + 1)

        def read_last(eng, use, b):
            if use < ENERGY:
                eng.wait_ge(qk_done, 2 * b + use + 1)
            elif use < XQ:
                eng.wait_ge(energy_done, LT * b + use - ENERGY + 1)
            elif use < PROBT:
                eng.wait_ge(xq_done, DT * b + use - XQ + 1)
            elif use < PRODUCT:
                eng.wait_ge(probT_done, LT * b + use - PROBT + 1)
            elif use < XT:
                eng.wait_ge(x3_done, LT * b + use - PRODUCT + 1)
            else:
                eng.wait_ge(xT_lo, DT * b + use - XT + 1)

        def empty(eng, use, b):
            if use >= 2:
                read_last(eng, use - 2, b)
            elif b:
                read_last(eng, use - 2 + 2 * USES, b - 1)

        def two(t, first):
            return (2 * (t - first), 2 * (t - first) + 1) if first <= t <= first + 1 else ()

        @block.sync
        def _(sp):
            def load(b):
                if b:
                    sp.wait_ge(filled[1], USES * (b - 1) + K // 2 + 1)
                sp.dma_start(ctxs[:], ctx_t[b].rearrange("(c p) l -> p c l", p=P)).then_inc(ctx_in, 16)
                if b >= 2:
                    sp.wait_ge(out_sent[b % 2], 16 * (b // 2))
                sp.dma_start(xs[:, b % 2], x1s[b].rearrange("(t p) d -> p t d", p=P)).then_inc(x_in[b % 2], 16)

            def raw_of(t):
                if t >= 2:
                    sp.wait_ge(split_hi, 2 * (t - 1))
                    sp.wait_ge(split_lo, 2 * (t - 1))
                sp.dma_start(raw[:, t % 2, 0], w["w_gate"][:, t, :]).then_inc(raw_in[t % 2], 16)
                sp.dma_start(raw[:, t % 2, 1], w["w_lin"][:, t, :]).then_inc(raw_in[t % 2], 16)

            sp.dma_start(where[:], routes).then_inc(routes_in, 16)
            sp.dma_start(gate[:], scales).then_inc(routes_in, 16)
            load(0)
            for dst, src in ((w_q[:], "w_q"), (w_k[:], "w_k"), (b_qk[:, 0:1], "b_q"), (b_qk[:, 1:2], "b_k"),
                             (ident[:], "ident"), (hada[:], "hadamard")):
                sp.dma_start(dst, w[src]).then_inc(consts, 16)
            sp.dma_start(gates[:, 0:1], w["g_xattn"][1:2].partition_broadcast(P)).then_inc(consts, 16)
            sp.dma_start(gates[:, 1:2], w["g_ffn"][1:2].partition_broadcast(P)).then_inc(consts, 16)
            for t in range(FT):
                if t == FT // 2:
                    raw_of(0)
                    raw_of(1)
                if t >= 4:
                    sp.wait_ge(mix_done, t - 3)
                sp.dma_start(raw_mix[:, t % 4], w_mix[:, t, :]).then_inc(mix_in[t % 4], 16)
            load(1)
            for t in range(2, FT):
                raw_of(t)
            for b in range(B):
                if 2 <= b + 1 < B:
                    load(b + 1)
                if b + 1 < B:
                    sp.wait_ge(out_done, LT * (b + 1))
                    sp.dma_start(out[b].rearrange("(t p) d -> p t d", p=P), xs[:, b % 2]).then_inc(out_sent[b % 2], 16)
            for i in range(LT):
                sp.wait_ge(out_done, LT * (B - 1) + i + 1)
                sp.dma_start(out[B - 1, i * P:(i + 1) * P], xs[:, (B - 1) % 2, i, :]).then_inc(out_sent[(B - 1) % 2], 16)
            sp.wait_ge(out_sent[0], 16 * (B // 2))
            sp.wait_ge(out_sent[1], 16 * (B // 2 - 1 + LT))

        @block.gpsimd
        def _(pool):
            nc.gpsimd.memset(half[:], -0.5).then_inc(half_set, 1)
            pool.wait_ge(half_set, 1)
            pool.wait_ge(routes_in, 32)
            for n in range(2 * B):
                if n % 2 == 0:
                    b = n // 2
                    if b:
                        full(pool, XT + 3, b - 1)
                        pool.wait_ge(x3_done, LT * b)
                    for i in range(LT):
                        t = LT * b + i
                        for k, dst in enumerate((xn, second)):
                            pool.indirect_dma_start(dst[:, i, :], None, expert_out.rearrange("t p d -> (t p) d"),
                                                    bass.IndirectOffsetOnAxis(where[:, k, t:t + 1], 0)).then_inc(y_in[i], 16)
                pool.wait_ge(var_done, n + 1)
                nc.gpsimd.tensor_tensor(rstd[:], var_eps[:], half[:], ALU.pow).then_inc(rstd_done, 1)

        @block.scalar
        def _(act):
            def split(t):
                act.wait_ge(raw_in[t % 2], 32 * (t // 2 + 1))
                nc.scalar.activation(wg[:, 0, t].rearrange("p c q -> p (c q)"), raw[:, t % 2, 0], ACT.Copy, scale=WS).then_inc(split_hi, 1)
                nc.scalar.activation(wl[:, 0, t].rearrange("p c q -> p (c q)"), raw[:, t % 2, 1], ACT.Copy, scale=WS).then_inc(split_hi, 1)

            def mix(group):
                for t in range(4 * group, 4 * group + 4):
                    act.wait_ge(mix_done, t + 1)
                    nc.scalar.activation(wo[:, 0, t, :], bank_out[t % 4][:], ACT.Copy, scale=MIX).then_inc(mix_hi, 1)

            def qk_of(b):
                if b:
                    full(act, ENERGY + 3, b - 1)
                full(act, Q, b)
                nc.scalar.activation(qk[:, 0, :], bank(Q)[:], ACT.Identity, bias=b_qk[:, 0:1]).then_inc(qk_done, 1)
                full(act, K, b)
                nc.scalar.activation(qk[:, 1, :], bank(K)[:], ACT.Identity, bias=b_qk[:, 1:2]).then_inc(qk_done, 1)

            def copy_energy(b, tiles):
                for i in tiles:
                    full(act, ENERGY + i, b)
                    if b and i == 0:
                        act.wait_ge(exp_done, LT * b)
                    nc.scalar.activation(energy[:, i, :], bank(ENERGY + i)[:], ACT.Copy).then_inc(energy_done, 1)

            def exp_of(b):
                for i in range(LT):
                    act.wait_ge(max_done, LT * b + i + 1)
                    if b and i == 0:
                        full(act, PROBT + 3, b - 1)
                    nc.scalar.activation(prob[:, i, :], energy[:, i, :], ACT.Exp, bias=neg_max[:, i:i + 1],
                                         accum_out=total[:, i:i + 1]).then_inc(exp_done, 1)

            def copy_xq(b, tiles):
                for c in tiles:
                    full(act, XQ + c, b)
                    if b and c == 0:
                        act.wait_ge(x3_done, LT * b)
                    nc.scalar.activation(xq[:, 0, c, :], bank(XQ + c)[:], ACT.Copy).then_inc(xq_hi, 1)

            def copy_probT(b, tiles):
                for c in tiles:
                    full(act, PROBT + c, b)
                    if b and c == 0:
                        act.wait_ge(x3_done, LT * b)
                    nc.scalar.activation(probT[:, 0, c, :], bank(PROBT + c)[:], ACT.Copy, scale=PROBS).then_inc(probT_hi, 1)

            def turn_hi(b, tiles):
                for c in tiles:
                    full(act, XT + c, b)
                    if b >= 2 and c == 0:
                        act.wait_ge(down_done, FT * (b - 1))
                    nc.scalar.activation(xt[:, b % 2, 0, c, :], bank(XT + c)[:], ACT.Copy).then_inc(xT_hi, 1)

            def tile(t, side, b, first):
                act.wait_ge(g_done, t + (FT * b + 1))
                if not first:
                    act.wait_ge(hid_done, t + (FT * b - 1))
                nc.scalar.activation(sg[:, side, :], bank_g[:], ACT.Silu, scale=1.0 / WS).then_inc(silu_done, 1)

            act.wait_ge(consts, 16 * CONSTS)
            nc.scalar.activation(tanh_g[:], gates[:], ACT.Tanh).then_inc(tanh_done, 1)
            qk_of(0)
            copy_energy(0, range(LT))
            mix(0)
            copy_xq(0, range(DT))
            exp_of(0)
            copy_probT(0, range(LT))
            mix(1)
            split(0)
            mix(2)
            turn_hi(0, range(DT))
            for b in range(B):
                for t in range(FT):
                    if b == 0 and t + 1 < FT:
                        split(t + 1)
                    tile(t, t % 2, b, b == 0 and t < 2)
                    if b == 0 and t == 0:
                        mix(3)
                    if b + 1 < B:
                        if t == QK_AT:
                            qk_of(b + 1)
                        copy_energy(b + 1, two(t, ENERGY_AT))
                        if t == EXP_AT:
                            exp_of(b + 1)
                        copy_xq(b + 1, two(t, XQ_AT))
                        copy_probT(b + 1, two(t, PROBT_AT))
                        turn_hi(b + 1, two(t, XT_AT))

        @block.vector
        def _(dve):
            links = [0]

            def link(ins):
                links[0] += 1
                ins.then_inc(chain, 1)
                dve.wait_ge(chain, links[0])

            def split(t):
                dve.wait_ge(split_hi, 2 * t + 2)
                for n, dst in enumerate((wg, wl)):
                    nc.vector.scalar_tensor_tensor(dst[:, 1, t].rearrange("p c q -> p (c q)"), raw[:, t % 2, n], WS,
                                                   dst[:, 0, t].rearrange("p c q -> p (c q)"), ALU.mult, ALU.subtract).then_inc(split_lo, 1)

            def mix(group):
                for t in range(4 * group, 4 * group + 4):
                    dve.wait_ge(mix_hi, t + 1)
                    nc.vector.scalar_tensor_tensor(wo[:, 1, t, :], bank_out[t % 4][:], MIX, wo[:, 0, t, :], ALU.mult, ALU.subtract)\
                        .then_inc(mix_lo, 1)

            def add_experts(b):
                dve.wait_ge(x_in[b % 2], 16 * (b // 2 + 1))
                for i in range(LT):
                    t = LT * b + i
                    dve.wait_ge(y_in[i], 32 * (b + 1))
                    link(nc.vector.scalar_tensor_tensor(xs[:, b % 2, i, :], xn[:, i, :], gate[:, 0, t:t + 1], xs[:, b % 2, i, :],
                                                        ALU.mult, ALU.add))
                    nc.vector.scalar_tensor_tensor(xs[:, b % 2, i, :], second[:, i, :], gate[:, 1, t:t + 1], xs[:, b % 2, i, :],
                                                   ALU.mult, ALU.add).then_inc(x2_done, 1)

            def norm_of(n, b, ready, target):
                dve.wait_ge(ready, target)
                for i in range(LT):
                    ins = nc.vector.bn_stats(stat[:, i, :], xs[:, b % 2, i, :])
                link(ins)
                for i in range(LT):
                    ins = nc.vector.bn_aggr(mv[:, i, :], stat[:, i, :])
                link(ins)
                nc.vector.tensor_scalar_add(var_eps[:], mv[:, :, 1], EPS).then_inc(var_done, 1)
                dve.wait_ge(rstd_done, n + 1)
                if n:
                    use, of = (XQ + 3, b) if n % 2 else (XT + 3, b - 1)
                    dve.wait_ge(filled[use % 2], USES * of + use // 2 + 1)
                for i in range(LT):
                    nc.vector.tensor_scalar(xn[:, i, :], xs[:, b % 2, i, :], mv[:, i, 0:1], rstd[:, i:i + 1],
                                            ALU.subtract, ALU.mult).then_inc(xn_done, 1)

            def max_of(b, tiles):
                for i in tiles:
                    dve.wait_ge(energy_done, LT * b + i + 1)
                    link(nc.vector.reduce_max(neg_max[:, i:i + 1], energy[:, i, :], AX_X))
                    nc.vector.tensor_scalar_mul(neg_max[:, i:i + 1], neg_max[:, i:i + 1], -1.0).then_inc(max_done, 1)

            def normalise(b):
                for i in range(LT):
                    dve.wait_ge(exp_done, LT * b + i + 1)
                    link(nc.vector.reciprocal(inv[:, i:i + 1], total[:, i:i + 1]))
                    nc.vector.tensor_scalar_mul(prob[:, i, :], prob[:, i, :], inv[:, i:i + 1]).then_inc(prob_done, 1)

            def xq_lo(b, tiles):
                for c in tiles:
                    dve.wait_ge(xq_hi, DT * b + c + 1)
                    nc.vector.tensor_tensor(xq[:, 1, c, :], bank(XQ + c)[:], xq[:, 0, c, :], ALU.subtract).then_inc(xq_done, 1)

            def probT_lo(b, tiles):
                for c in tiles:
                    dve.wait_ge(probT_hi, LT * b + c + 1)
                    nc.vector.scalar_tensor_tensor(probT[:, 1, c, :], bank(PROBT + c)[:], PROBS, probT[:, 0, c, :],
                                                   ALU.mult, ALU.subtract).then_inc(probT_done, 1)

            def x3_of(b, tiles):
                for i in tiles:
                    full(dve, PRODUCT + i, b)
                    nc.vector.scalar_tensor_tensor(xs[:, b % 2, i, :], bank(PRODUCT + i)[:], scale_x[:], xs[:, b % 2, i, :],
                                                   ALU.mult, ALU.add).then_inc(x3_done, 1)

            def turn_lo(b, tiles):
                for c in tiles:
                    dve.wait_ge(xT_hi, DT * b + c + 1)
                    nc.vector.tensor_tensor(xt[:, b % 2, 1, c, :], bank(XT + c)[:], xt[:, b % 2, 0, c, :], ALU.subtract)\
                        .then_inc(xT_lo, 1)

            def tile(t, side, b, first):
                dve.wait_ge(silu_done, t + (FT * b + 1))
                dve.wait_ge(u_done, t + (FT * b + 1))
                nc.vector.scalar_tensor_tensor(hid[:, side, :], bank_u[:], 1.0 / WS, sg[:, side, :], ALU.mult, ALU.mult).then_inc(hid_done, 1)
                dve.wait_ge(hid_done, t + (FT * b + 1))
                if not first:
                    dve.wait_ge(down_done, t + (FT * b - 1))
                nc.vector.tensor_copy(h16[:, side, 0, :], hid[:, side, :]).then_inc(hi_done, 1)
                dve.wait_ge(hi_done, t + (FT * b + 1))
                nc.vector.tensor_tensor(h16[:, side, 1, :], hid[:, side, :], h16[:, side, 0, :], ALU.subtract).then_inc(h_done, 1)

            def out_of(b):
                dve.wait_ge(down_done, FT * (b + 1))
                for i in range(LT):
                    nc.vector.scalar_tensor_tensor(xs[:, b % 2, i, :], bank_out[i][:], scale_out[:], xs[:, b % 2, i, :],
                                                   ALU.mult, ALU.add).then_inc(out_done, 1)

            dve.wait_ge(tanh_done, 1)
            nc.vector.tensor_scalar_mul(scale_out[:], tanh_g[:, 1:2], 1.0 / WS)
            nc.vector.tensor_scalar_mul(scale_x[:], tanh_g[:, 0:1], 1.0 / PROBS)
            dve.wait_ge(routes_in, 32)
            add_experts(0)
            norm_of(0, 0, x2_done, LT)
            max_of(0, range(LT))
            xq_lo(0, range(DT))
            normalise(0)
            probT_lo(0, range(LT))
            mix(0)
            x3_of(0, (0, 1))
            mix(1)
            split(0)
            x3_of(0, (2, 3))
            norm_of(1, 0, x3_done, LT)
            turn_lo(0, range(DT))
            mix(2)
            for b in range(B):
                for t in range(FT):
                    if b == 0 and t + 1 < FT:
                        split(t + 1)
                    tile(t, t % 2, b, b == 0 and t < 2)
                    if b == 0 and t == 0:
                        mix(3)
                    if b + 1 < B:
                        if t == EXPERTS_AT:
                            add_experts(b + 1)
                        if t == NORM2_AT:
                            norm_of(2 * b + 2, b + 1, x2_done, LT * (b + 2))
                        max_of(b + 1, two(t, ENERGY_AT))
                        if t == EXP_AT:
                            normalise(b + 1)
                        xq_lo(b + 1, two(t, XQ_AT))
                        probT_lo(b + 1, two(t, PROBT_AT))
                        x3_of(b + 1, two(t, PRODUCT_AT))
                        if t == NORM3_AT:
                            norm_of(2 * b + 3, b + 1, x3_done, LT * (b + 2))
                        turn_lo(b + 1, two(t, XT_AT))
                out_of(b)

        @block.tensor
        def _(pe):
            def fill(mm, use):
                mm.then_inc(filled[use % 2], 1)

            def queries(b):
                pe.wait_ge(ctx_in, 16 * (b + 1))
                for use, weight in ((Q, w_q), (K, w_k)):
                    empty(pe, use, b)
                    for c in range(CT):
                        mm = nc.tensor.matmul(bank(use)[:], weight[:, c, :], ctxs[:, c, :], start=(c == 0), stop=(c == CT - 1))
                    fill(mm, use)

            def energies(b, tiles):
                for i in tiles:
                    pe.wait_ge(qk_done, 2 * (b + 1))
                    empty(pe, ENERGY + i, b)
                    fill(nc.tensor.matmul(bank(ENERGY + i)[:], qk[:, 0, i * P:(i + 1) * P], qk[:, 1, :], start=True, stop=True),
                         ENERGY + i)

            def turn_x(first, norm, b, tiles):
                for c in tiles:
                    pe.wait_ge(xn_done, LT * (norm + 1))
                    empty(pe, first + c, b)
                    for i in range(LT):
                        mm = nc.tensor.transpose(bank(first + c)[:, i * P:(i + 1) * P], xn[:, i, c * P:(c + 1) * P], ident[:])
                    fill(mm, first + c)

            def turn_prob(b, tiles):
                for c in tiles:
                    pe.wait_ge(prob_done, LT * (b + 1))
                    empty(pe, PROBT + c, b)
                    for i in range(LT):
                        mm = nc.tensor.transpose(bank(PROBT + c)[:, i * P:(i + 1) * P], prob[:, i, c * P:(c + 1) * P], ident[:])
                    fill(mm, PROBT + c)

            def product(b, tiles):
                for i in tiles:
                    pe.wait_ge(xq_done, DT * (b + 1))
                    pe.wait_ge(probT_done, LT * (b + 1))
                    empty(pe, PRODUCT + i, b)
                    n = 0
                    for c in range(DT):
                        for xh, ph in ((0, 0), (0, 1), (1, 0)):
                            mm = nc.tensor.matmul(bank(PRODUCT + i)[:], xq[:, xh, c, i * P:(i + 1) * P], probT[:, ph, c, :],
                                                  start=(n == 0), stop=(n == 3 * DT - 1))
                            n += 1
                    fill(mm, PRODUCT + i)

            def mix(group):
                for t in range(4 * group, 4 * group + 4):
                    pe.wait_ge(mix_in[t % 4], 16 * (t // 4 + 1))
                    if t >= 4:
                        pe.wait_ge(mix_lo, t - 3)
                    nc.tensor.matmul(bank_out[t % 4][:], hada[:], raw_mix[:, t % 4], start=True, stop=True).then_inc(mix_done, 1)

            def at(m, t):
                return m[:, t] if isinstance(t, int) else m[:, bass.ds(t, 1)].rearrange("p o n -> p (o n)")

            def tile_up(t, b, first=False):
                if b == 0:
                    pe.wait_ge(split_lo, 2 * (t + 1))
                if not first:
                    pe.wait_ge(hid_done, t + FT * b)
                for weight, dst, done in ((wg, bank_g, g_done), (wl, bank_u, u_done)):
                    n = 0
                    for c in range(DT):
                        for wh, xh in ((0, 0), (0, 1), (1, 0)):
                            mm = nc.tensor.matmul(dst[:], at(weight[:, wh, :, c, :], t), xt[:, b % 2, xh, c, :],
                                                  start=(n == 0), stop=(n == 3 * DT - 1))
                            n += 1
                    mm.then_inc(done, 1)

            def tile_down(t, side, b, first=False, last=False):
                pe.wait_ge(h_done, t + (FT * b + 1))
                for i in range(LT):
                    for n, (hh, wh) in enumerate(((0, 0), (0, 1), (1, 0))):
                        mm = nc.tensor.matmul(bank_out[i][:], h16[:, side, hh, i * P:(i + 1) * P], at(wo[:, wh], t),
                                              start=(first and n == 0), stop=(last and n == 2))
                mm.then_inc(down_done, 1)

            pe.wait_ge(consts, 16 * CONSTS)
            queries(0)
            energies(0, range(LT))
            mix(0)
            turn_x(XQ, 0, 0, range(DT))
            turn_prob(0, range(LT))
            product(0, (0, 1))
            mix(1)
            product(0, (2, 3))
            mix(2)
            turn_x(XT, 1, 0, range(DT))
            for b in range(B):
                pe.wait_ge(xT_lo, DT * (b + 1))
                for t in range(FT + 1):
                    if t < FT:
                        tile_up(t, b, first=b == 0 and t == 0)
                    if b == 0 and t == 1:
                        mix(3)
                    if t == 1:
                        if b:
                            pe.wait_ge(out_done, LT * b)
                        else:
                            pe.wait_ge(mix_lo, FT)
                    if t:
                        tile_down(t - 1, (t - 1) % 2, b, first=t == 1, last=t == FT)
                    if b + 1 < B:
                        if t == QK_AT:
                            queries(b + 1)
                        energies(b + 1, two(t, ENERGY_AT))
                        turn_x(XQ, 2 * b + 2, b + 1, two(t, XQ_AT))
                        turn_prob(b + 1, two(t, PROBT_AT))
                        product(b + 1, two(t, PRODUCT_AT))
                        turn_x(XT, 2 * b + 3, b + 1, two(t, XT_AT))


def layout(a):
    import numpy as np

    def tiles(m, p=P):
        return np.ascontiguousarray(m.reshape(m.shape[0] // p, p, m.shape[1]).transpose(1, 0, 2))

    def col(v):
        return np.ascontiguousarray(v.reshape(-1, P).T)

    def zeros(*shape):
        return np.zeros(shape, np.float32)

    hadamard = np.array([[1.0]], np.float32)
    while hadamard.shape[0] < P:
        hadamard = np.block([[hadamard, hadamard], [hadamard, -hadamard]])
    xp = a["L0_xattn_x_proj_w"].T
    w_x = np.concatenate([xp[:, :DR], zeros(DI, DR), xp[:, DR:]], axis=1)
    up = [a["L0_ffn_w1"][e] for e in range(NE)] + [a["L0_ffn_shared_w1"]]
    down = [a["L0_ffn_w2"][e] for e in range(NE)] + [a["L0_ffn_shared_w2"]]
    up, down = np.concatenate(up, axis=1), np.concatenate(down, axis=0)
    pick = zeros(GR, GR, P)
    for e in range(GR):
        pick[e, e] = 1.0
    return {
        "x": a["x"], "g_xattn": a["g_xattn"], "g_ffn": a["g_ffn"],
        "ctx_t": np.ascontiguousarray(a["ctx_1024"].transpose(0, 2, 1)),
        "ident": np.eye(P, dtype=np.float32),
        "w_in": tiles(a["L0_xattn_in_proj_w"].T),
        "conv_w": np.ascontiguousarray(a["L0_xattn_conv_w"].T),
        "w_x": tiles(w_x),
        "w_dt": np.ascontiguousarray(a["L0_xattn_dt_proj_w"].T),
        "scan_cols": np.stack([col(v) for v in (a["L0_xattn_conv_b"], a["L0_xattn_dt_proj_b"], a["L0_xattn_D"],
                                                *a["L0_xattn_conv_w"].T)], axis=1),
        "a_log": tiles(a["L0_xattn_A_log"]),
        "gate_w": tiles(a["L0_ffn_gate_w"]).reshape(P, DT * NE),
        "w_up": np.ascontiguousarray(up.reshape(DT, P, HT, P).transpose(1, 2, 0, 3)).reshape(P, HT, DT * P),
        "w_down": np.ascontiguousarray(down.reshape(HT, P, D).transpose(1, 0, 2)),
        "b_up": col(np.concatenate([a["L0_ffn_b1"].reshape(-1), a["L0_ffn_shared_b1"]])),
        "b_down": np.concatenate([a["L0_ffn_b2"], a["L0_ffn_shared_b2"][None], zeros(1, D)]),
        "expert_no": np.ascontiguousarray(np.broadcast_to(np.arange(NE, dtype=np.float32)[None, :, None], (P, NE, TT))),
        "thresholds": np.tile(np.arange(TT, dtype=np.float32) * P, (P, 1)),
        "tile_no": np.tile(np.arange(RT, dtype=np.float32), (P, 1)),
        "token_no": np.arange(B * L, dtype=np.float32).reshape(TT, P).T,
        "lower": -np.triu(np.ones((P, P), np.float32)).T,
        "pick": pick.reshape(GR, GR * P),
        "w_q": tiles(a["L1_xattn_Wq"].T), "w_k": tiles(a["L1_xattn_Wk"].T),
        "b_q": col(a["L1_xattn_bq"]), "b_k": col(a["L1_xattn_bk"]),
        "w_gate": np.ascontiguousarray(a["L1_ffn_W1"].T.reshape(DT, P, FT, P).transpose(1, 2, 0, 3)).reshape(P, FT, DT * P),
        "w_lin": np.ascontiguousarray(a["L1_ffn_W3"].T.reshape(DT, P, FT, P).transpose(1, 2, 0, 3)).reshape(P, FT, DT * P),
        "w_out": tiles(a["L1_ffn_W2"].T),
        "hadamard": hadamard,
    }


def program(nc, w, out):
    x1 = nc.dram_tensor("x1_scratch", [B, L, D], F32, kind="Internal").ap()
    x1s = nc.dram_tensor("x1s_scratch", [B, L, D], F32, kind="Internal").ap()
    xn_rows = nc.dram_tensor("xn_scratch", [B * L, D], F32, kind="Internal").ap()
    expert_out = nc.dram_tensor("expert_out_scratch", [RT, P, D], F32, kind="Internal").ap()
    token_table = nc.dram_tensor("token_table_scratch", [RT * P, 1], F32, kind="Internal").ap()
    routes = nc.dram_tensor("routes_scratch", [P, 2, TT], U32, kind="Internal").ap()
    scales = nc.dram_tensor("scales_scratch", [P, 2, TT], F32, kind="Internal").ap()
    b_rows = nc.dram_tensor("b_rows_scratch", [B, NS, L], F32, kind="Internal").ap()
    w_mix = nc.dram_tensor("w_mix_scratch", [P, FT, D], F32, kind="Internal").ap()
    scan_block(nc, w, w["x"], w["ctx_t"], x1, b_rows)
    moe_block(nc, w, x1, x1s, xn_rows, expert_out, token_table, routes, scales, w_mix)
    ffn_block(nc, w, w["ctx_t"], x1s, expert_out, routes, scales, w_mix, out)


def kernel(**inputs):
    import numpy as np
    import concourse.bacc as bacc
    from concourse.bass_utils import run_bass_kernel_spmd

    nc = bacc.Bacc("TRN2", target_bir_lowering=False, num_devices=1)
    arrays = {name: np.ascontiguousarray(a) for name, a in layout({k: np.asarray(v) for k, v in inputs.items()}).items()}
    w = {name: nc.dram_tensor(name, a.shape, mybir.dt.from_np(a.dtype), kind="ExternalInput").ap() for name, a in arrays.items()}
    out = nc.dram_tensor("out", [B, L, D], F32, kind="ExternalOutput").ap()
    program(nc, w, out)
    result = run_bass_kernel_spmd(nc, [arrays], core_ids=[0])
    return result.results[0]["out"]
```
